# Optimizing a Trainium2 kernel written in Bass

```python
import numpy as np
import jax
import jax.numpy as jnp

def _softmax(x, axis=-1):
    return jax.nn.softmax(x, axis=axis)

def _gelu(x):
    return jax.nn.gelu(x, approximate=True)

def _silu(x):
    return jax.nn.silu(x)

def _sigmoid(x):
    return jax.nn.sigmoid(x)

def _layernorm(x, axis=-1, eps=1e-05):
    m = jnp.mean(x, axis=axis, keepdims=True)
    v = jnp.var(x, axis=axis, keepdims=True)
    return (x - m) / jnp.sqrt(v + eps)

def _scatter_add(tgt, idx, src, axis=0):
    return tgt.at[idx].add(src)

def _segment_sum(src, seg, n):
    return jax.ops.segment_sum(src, seg, n)
kernel_name = 'mk_early_fusion_d1_tok_img1024_r4_b38cc3'

def setup_inputs(seed: int=0):
    np.random.seed(seed)
    _w = jnp.asarray

    def _rec_inputs():
        import jax
        import jax.numpy as jnp
        _rk = jax.random.key(seed)
        x = -0.00040386 + 0.999972 * jax.random.normal(jax.random.fold_in(_rk, 1), (64, 3, 64, 64), jnp.float32)
        txt = 0.305668 + 0.860336 * jax.random.normal(jax.random.fold_in(_rk, 2), (64, 128, 256), jnp.float32)
        return (x, txt)
    x, txt = _rec_inputs()

    def _L0_tok_setup():
        import math
        import jax, jax.numpy as jnp
        import numpy as np
        PATCH = 16
        HIDDEN = 256
        IMG = 64
        GRID = IMG // PATCH
        N_TOK = GRID * GRID
        PDIM = 3 * PATCH * PATCH

        def make_pos_emb(n: int, d: int) -> jnp.ndarray:
            pos = jnp.arange(n, dtype=jnp.float32)[:, None]
            div = jnp.exp(jnp.arange(0, d, 2, dtype=jnp.float32) * (-math.log(10000.0) / d))
            pe = jnp.zeros((n, d), dtype=jnp.float32)
            pe = pe.at[:, 0::2].set(jnp.sin(pos * div))
            pe = pe.at[:, 1::2].set(jnp.cos(pos * div[:d // 2]))
            return pe
        key = jax.random.key(seed)
        k_img, k_w, k_b = jax.random.split(key, 3)
        img = jax.random.normal(k_img, (64, 3, IMG, IMG), dtype=jnp.float32)
        bound = 1.0 / math.sqrt(PDIM)
        W = jax.random.uniform(k_w, (HIDDEN, PDIM), minval=-bound, maxval=bound, dtype=jnp.float32)
        b = jax.random.uniform(k_b, (HIDDEN,), minval=-bound, maxval=bound, dtype=jnp.float32)
        pos_emb = make_pos_emb(N_TOK, HIDDEN)
        return {'img': img, 'W': W, 'b': b, 'pos_emb': pos_emb}
    _L0_tok_all = _L0_tok_setup()
    _L0_tok_in = {k: v for k, v in _L0_tok_all.items() if k in ('W', 'b', 'pos_emb')}
    del _L0_tok_all

    def _L0_attn_setup():
        import jax, jax.numpy as jnp
        import numpy as np
        SEQ_LEN, BATCH, H, N = (1024, 8, 256, 16)

        def _to_c(t):
            return t[..., 0] + 1j * t[..., 1]

        def _s4_kernel(log_dt, inv_w_real, w_imaginary, B, P, C, L):
            dt = jnp.exp(log_dt)
            w = (-jnp.exp(inv_w_real) + 1j * w_imaginary) * dt
            Bc = _to_c(B)
            Cc = _to_c(C)
            Pc = _to_c(P)
            Qc = jnp.conj(Pc)
            Bcat = jnp.concatenate([Bc[None], Pc], axis=0)
            Ccat = jnp.concatenate([Cc[None], Qc], axis=0)
            v = Bcat[:, None] * Ccat[None]
            M = L // 2 + 1
            omega = jnp.exp(-2j * jnp.pi / L * jnp.arange(M)).astype(jnp.complex64)
            z = 2 * (1 - omega) / (1 + omega)
            cauchy = 1.0 / (z[None, None, :] - w[:, :, None])
            r = jnp.einsum('abhn,hnm->abhm', v, cauchy)
            r = r * dt[None, None]
            k_f = r[:1, :1] - r[:1, 1:] * r[1:, :1] / (1 + r[1:, 1:])
            k_f = k_f * 2 / (1 + omega)
            k = jnp.fft.irfft(k_f, n=L, axis=-1)[..., :L]
            return k[0, 0]
        key = jax.random.key(seed)
        ks = jax.random.split(key, 8)
        H_, N_ = (H, N)
        x = jax.random.normal(ks[0], (SEQ_LEN, BATCH, H_), dtype=jnp.float32)
        log_dt = jax.random.normal(ks[1], (H_, 1), dtype=jnp.float32) * 0.5 - 4.6
        inv_w_real = jax.random.normal(ks[2], (H_, N_), dtype=jnp.float32)
        w_imaginary = jax.random.normal(ks[3], (H_, N_), dtype=jnp.float32)
        B = jax.random.normal(ks[4], (H_, N_, 2), dtype=jnp.float32)
        P = jax.random.normal(ks[5], (1, H_, N_, 2), dtype=jnp.float32)
        C = jax.random.normal(ks[6], (H_, N_, 2), dtype=jnp.float32)
        D = jax.random.normal(ks[7], (H_,), dtype=jnp.float32)
        return {'x': x, 'log_dt': log_dt, 'inv_w_real': inv_w_real, 'w_imaginary': w_imaginary, 'B': B, 'P': P, 'C': C, 'D': D}
    _L0_attn_all = _L0_attn_setup()
    _L0_attn_in = {k: v for k, v in _L0_attn_all.items() if k in ('log_dt', 'inv_w_real', 'w_imaginary', 'B', 'P', 'C', 'D')}
    del _L0_attn_all

    def _L0_ffn_setup():
        import jax, jax.numpy as jnp
        import numpy as np
        B, S, D, H, F = (4, 1024, 256, 16, 1024)
        CAP = 0.125
        ROPE_BASE = 10000.0

        def rmsnorm(x, g):
            return x * jax.lax.rsqrt(jnp.mean(x * x, -1, keepdims=True) + 1e-06) * g

        def rope(t, pos):
            hd = t.shape[-1]
            inv = 1.0 / ROPE_BASE ** (jnp.arange(0, hd, 2, dtype=jnp.float32) / hd)
            f = pos[:, None, :, None].astype(jnp.float32) * inv
            emb = jnp.concatenate([f, f], axis=-1)
            cos, sin = (jnp.cos(emb), jnp.sin(emb))
            rot = jnp.concatenate([-t[..., hd // 2:], t[..., :hd // 2]], axis=-1)
            return t * cos + rot * sin
        key = jax.random.key(seed)
        ks = jax.random.split(key, 9)
        scale = 0.02
        x = jax.random.normal(ks[0], (B, S, D), jnp.float32)
        causal = jnp.where(jnp.tril(jnp.ones((S, S), bool)), 0.0, -1000000000.0).astype(jnp.float32)
        attention_mask = jnp.broadcast_to(causal[None, None], (B, 1, S, S))
        position_ids = jnp.broadcast_to(jnp.arange(S, dtype=jnp.int32), (B, S))
        return {'x': x, 'attention_mask': attention_mask, 'position_ids': position_ids, 'router_w': jax.random.normal(ks[1], (D, 1), jnp.float32) * scale, 'router_b': jnp.zeros((1,), jnp.float32), 'wq': jax.random.normal(ks[2], (D, D), jnp.float32) * scale, 'wk': jax.random.normal(ks[3], (D, D), jnp.float32) * scale, 'wv': jax.random.normal(ks[4], (D, D), jnp.float32) * scale, 'wo': jax.random.normal(ks[5], (D, D), jnp.float32) * scale, 'w1': jax.random.normal(ks[6], (D, F), jnp.float32) * scale, 'w2': jax.random.normal(ks[7], (F, D), jnp.float32) * scale, 'ln1': jnp.ones((D,), jnp.float32), 'ln2': jnp.ones((D,), jnp.float32)}
    _L0_ffn_all = _L0_ffn_setup()
    _L0_ffn_in = {k: v for k, v in _L0_ffn_all.items() if k in ('attention_mask', 'position_ids', 'router_w', 'router_b', 'wq', 'wk', 'wv', 'wo', 'w1', 'w2', 'ln1', 'ln2')}
    del _L0_ffn_all
    return {'x': x, 'txt': txt, 'L0_tok_W': _L0_tok_in['W'], 'L0_tok_b': _L0_tok_in['b'], 'L0_tok_pos_emb': _L0_tok_in['pos_emb'], 'L0_attn_log_dt': _L0_attn_in['log_dt'], 'L0_attn_inv_w_real': _L0_attn_in['inv_w_real'], 'L0_attn_w_imaginary': _L0_attn_in['w_imaginary'], 'L0_attn_B': _L0_attn_in['B'], 'L0_attn_P': _L0_attn_in['P'], 'L0_attn_C': _L0_attn_in['C'], 'L0_attn_D': _L0_attn_in['D'], 'L0_ffn_attention_mask': _L0_ffn_in['attention_mask'], 'L0_ffn_position_ids': _L0_ffn_in['position_ids'], 'L0_ffn_router_w': _L0_ffn_in['router_w'], 'L0_ffn_router_b': _L0_ffn_in['router_b'], 'L0_ffn_wq': _L0_ffn_in['wq'], 'L0_ffn_wk': _L0_ffn_in['wk'], 'L0_ffn_wv': _L0_ffn_in['wv'], 'L0_ffn_wo': _L0_ffn_in['wo'], 'L0_ffn_w1': _L0_ffn_in['w1'], 'L0_ffn_w2': _L0_ffn_in['w2'], 'L0_ffn_ln1': _L0_ffn_in['ln1'], 'L0_ffn_ln2': _L0_ffn_in['ln2']}

def reference(x, txt, L0_tok_W, L0_tok_b, L0_tok_pos_emb, L0_attn_log_dt, L0_attn_inv_w_real, L0_attn_w_imaginary, L0_attn_B, L0_attn_P, L0_attn_C, L0_attn_D, L0_ffn_attention_mask, L0_ffn_position_ids, L0_ffn_router_w, L0_ffn_router_b, L0_ffn_wq, L0_ffn_wk, L0_ffn_wv, L0_ffn_wo, L0_ffn_w1, L0_ffn_w2, L0_ffn_ln1, L0_ffn_ln2):
    import jax
    import jax.numpy as jnp

    def _L0_tok_ref(img, W, b, pos_emb):
        import math
        import jax, jax.numpy as jnp
        import numpy as np
        PATCH = 16
        HIDDEN = 256
        IMG = 64
        GRID = IMG // PATCH
        N_TOK = GRID * GRID
        PDIM = 3 * PATCH * PATCH

        def make_pos_emb(n: int, d: int) -> jnp.ndarray:
            pos = jnp.arange(n, dtype=jnp.float32)[:, None]
            div = jnp.exp(jnp.arange(0, d, 2, dtype=jnp.float32) * (-math.log(10000.0) / d))
            pe = jnp.zeros((n, d), dtype=jnp.float32)
            pe = pe.at[:, 0::2].set(jnp.sin(pos * div))
            pe = pe.at[:, 1::2].set(jnp.cos(pos * div[:d // 2]))
            return pe
        B, C, H, Wd = img.shape
        p = PATCH
        gh, gw = (H // p, Wd // p)
        x = img.reshape(B, C, gh, p, gw, p)
        x = jnp.transpose(x, (0, 2, 4, 1, 3, 5))
        x = x.reshape(B, gh * gw, C * p * p)
        z = jnp.einsum('bnd,hd->bnh', x, W) + b
        return z + pos_emb[None, :, :]

    def _L0_attn_ref(x, log_dt, inv_w_real, w_imaginary, B, P, C, D):
        import jax, jax.numpy as jnp
        import numpy as np
        SEQ_LEN, BATCH, H, N = (1024, 8, 256, 16)

        def _to_c(t):
            return t[..., 0] + 1j * t[..., 1]

        def _s4_kernel(log_dt, inv_w_real, w_imaginary, B, P, C, L):
            dt = jnp.exp(log_dt)
            w = (-jnp.exp(inv_w_real) + 1j * w_imaginary) * dt
            Bc = _to_c(B)
            Cc = _to_c(C)
            Pc = _to_c(P)
            Qc = jnp.conj(Pc)
            Bcat = jnp.concatenate([Bc[None], Pc], axis=0)
            Ccat = jnp.concatenate([Cc[None], Qc], axis=0)
            v = Bcat[:, None] * Ccat[None]
            M = L // 2 + 1
            omega = jnp.exp(-2j * jnp.pi / L * jnp.arange(M)).astype(jnp.complex64)
            z = 2 * (1 - omega) / (1 + omega)
            cauchy = 1.0 / (z[None, None, :] - w[:, :, None])
            r = jnp.einsum('abhn,hnm->abhm', v, cauchy)
            r = r * dt[None, None]
            k_f = r[:1, :1] - r[:1, 1:] * r[1:, :1] / (1 + r[1:, 1:])
            k_f = k_f * 2 / (1 + omega)
            k = jnp.fft.irfft(k_f, n=L, axis=-1)[..., :L]
            return k[0, 0]
        L = x.shape[0]
        residual = x * D
        xc = jnp.transpose(x, (1, 2, 0))
        k = _s4_kernel(log_dt, inv_w_real, w_imaginary, B, P, C, L)
        n = 2 * L
        k_f = jnp.fft.rfft(k, n=n, axis=-1)
        x_f = jnp.fft.rfft(xc, n=n, axis=-1)
        out = jnp.fft.irfft(x_f * k_f, n=n, axis=-1)[..., :L]
        out = jax.nn.silu(jnp.transpose(out, (2, 0, 1)) + residual)
        return out

    def _L0_ffn_ref(x, attention_mask, position_ids, router_w, router_b, wq, wk, wv, wo, w1, w2, ln1, ln2):
        import jax, jax.numpy as jnp
        import numpy as np
        B, S, D, H, F = (4, 1024, 256, 16, 1024)
        CAP = 0.125
        ROPE_BASE = 10000.0

        def rmsnorm(x, g):
            return x * jax.lax.rsqrt(jnp.mean(x * x, -1, keepdims=True) + 1e-06) * g

        def rope(t, pos):
            hd = t.shape[-1]
            inv = 1.0 / ROPE_BASE ** (jnp.arange(0, hd, 2, dtype=jnp.float32) / hd)
            f = pos[:, None, :, None].astype(jnp.float32) * inv
            emb = jnp.concatenate([f, f], axis=-1)
            cos, sin = (jnp.cos(emb), jnp.sin(emb))
            rot = jnp.concatenate([-t[..., hd // 2:], t[..., :hd // 2]], axis=-1)
            return t * cos + rot * sin
        b, s, d = x.shape
        hd = d // H
        weights = (x @ router_w)[..., 0] + router_b[0]
        k = int(CAP * s)
        topv, topi = jax.lax.top_k(weights, k)
        thr = topv[:, -1]
        sel_mask = (weights > thr[:, None]).astype(x.dtype)
        kc = k - 1
        sel_idx = jnp.sort(topi[:, :kc], axis=1)
        bidx = jnp.arange(b)[:, None]
        x_sel = x[bidx, sel_idx]
        pos_sel = position_ids[bidx, sel_idx]
        w_sel = weights[bidx, sel_idx]
        m = attention_mask[:, 0]
        m_sel = m[bidx[:, :, None], sel_idx[:, :, None], sel_idx[:, None, :]]
        hn = rmsnorm(x_sel, ln1)

        def heads(t):
            return t.reshape(b, kc, H, hd).transpose(0, 2, 1, 3)
        q = rope(heads(hn @ wq), pos_sel)
        kk = rope(heads(hn @ wk), pos_sel)
        v = heads(hn @ wv)
        sc = jnp.einsum('bhqd,bhkd->bhqk', q, kk) / np.sqrt(hd).astype(np.float32)
        sc = sc + m_sel[:, None]
        a = jax.nn.softmax(sc, axis=-1)
        o = jnp.einsum('bhqk,bhkd->bhqd', a, v).transpose(0, 2, 1, 3).reshape(b, kc, d) @ wo
        x1 = x_sel + o
        x2 = x1 + jax.nn.gelu(rmsnorm(x1, ln2) @ w1) @ w2
        proc = x2 * w_sel[..., None]
        out = jnp.zeros_like(x).at[bidx, sel_idx].set(proc)
        return out + x * (1.0 - sel_mask)[..., None]
    h = _L0_tok_ref(x, L0_tok_W, L0_tok_b, L0_tok_pos_emb)
    h = jnp.concatenate([h, txt], axis=1)
    h = h + _L0_attn_ref(_layernorm(h, axis=-1), L0_attn_log_dt, L0_attn_inv_w_real, L0_attn_w_imaginary, L0_attn_B, L0_attn_P, L0_attn_C, L0_attn_D)
    h = h + _L0_ffn_ref(_layernorm(h, axis=-1), L0_ffn_attention_mask, L0_ffn_position_ids, L0_ffn_router_w, L0_ffn_router_b, L0_ffn_wq, L0_ffn_wk, L0_ffn_wv, L0_ffn_wo, L0_ffn_w1, L0_ffn_w2, L0_ffn_ln1, L0_ffn_ln2)
    return h

_drawn_inputs = setup_inputs


def setup_inputs(seed=0):
    import zlib

    import numpy as np

    out = dict(_drawn_inputs(seed))
    spreads = {'L0_ffn_ln1': (1.0, 0.6), 'L0_ffn_ln2': (1.0, 0.6)}
    factors = {'L0_tok_b': 2.995,
     'L0_ffn_wq': 8.0,
     'L0_ffn_wk': 8.0,
     'L0_ffn_wv': 6.928,
     'L0_ffn_wo': 6.976,
     'L0_ffn_w1': 4.234,
     'L0_ffn_w2': 4.186}
    for name, (base, spread) in spreads.items():
        noise = np.random.default_rng([zlib.crc32(name.encode()), seed]).standard_normal(out[name].shape)
        drawn = base * np.exp(spread * noise) if base else spread * noise
        out[name] = jnp.asarray(drawn.astype(out[name].dtype))
    for name, factor in factors.items():
        out[name] = (out[name] * factor).astype(out[name].dtype)
    return out
```

```python
from contextlib import ExitStack

import numpy as np

import concourse.bass as bass
from concourse import mybir

F32 = mybir.dt.float32
F16 = mybir.dt.float16
BF16 = mybir.dt.bfloat16
I32 = mybir.dt.int32
U32 = mybir.dt.uint32
ALU = mybir.AluOpType
ACT = mybir.ActivationFunctionType
AX = mybir.AxisListType.X

P = 128
S = 64
TOK = 144
D = 256
POS = TOK // 2
CH = 8
NCH = POS // CH
KC = 768 // P
FR = S // 2 + 1
HG = 8
HF = D // HG
TCH = 16
NT = D // TCH
TRING = 3
UCH = 64
NU = D // UCH
QT = 4
NB = S // QT
GRP = 8
NGRP = D // GRP
CSLOT = 2
SIL = 3
KSEL = int(0.125 * TOK) - 1
SLOT = 32
HD = 16
FF = 1024
FC = FF // P
SG = 4
SQ = S // SG
NC = SQ * KSEL
NQ = S // 4
NBB = 4
LN_EPS = 1e-5
RMS_EPS = 1e-6
T_PEAK = 1024.0
X_GAIN = 64.0
NEG = -3.0e38
SKIP_ROW = 30000.0
RW_ACT = 4
PI_LOW = 3.1415925
TWO_PI = (6.28125, 0.0019350051879882812, float(2 * np.pi - 6.28125 - 0.0019350051879882812))

ORDER = [1, 2, 3, 0, 4, 5, 6, 7, 8]


def gemm_plan():
    plan = [("cs", s, i) for s in range(SG) for i in range(2)] + [("u", s, i) for s in range(SG) for i in range(2)]
    plan += [("mask", 0, 0)]

    def project(s):
        return ([("xt", s, i) for i in range(4)] + [(w, s, h) for h in range(2) for w in ("q", "qr", "k", "kr")]
                + [("v", s, i) for i in range(4)])

    def mlp(s):
        return ([("x2t", s, i) for i in range(4)] + [("h", s, i) for i in range(FC)] + [("y", s, i) for i in range(2)]
                + [("yt", s, i) for i in range(4)])

    plan += project(0)
    for s in range(SG):
        if s + 1 < SG:
            plan += project(s + 1)
        if s >= 1:
            plan += mlp(s - 1)
        plan += [("o", s, i) for i in range(4)]
    return plan + mlp(SG - 1)


BY_ACT = ("cs", "xt", "v", "x2t", "h")


def build(nc, a, out):
    with ExitStack() as ctx:
        def sb(name, shape, dt=F32):
            return ctx.enter_context(nc.sbuf_tensor(name, shape, dt))

        def sem(name):
            return ctx.enter_context(nc.semaphore(name))

        ctx.enter_context(nc.allow_non_contiguous_dma(reason="short rows of the kernel and of constants"))

        h1_rows = nc.dram_tensor("h1_rows", [S * TOK, D], F32, kind="Internal").ap()

        h0 = sb("h0", [P, POS, D])
        work = sb("work", [P, 24576])
        wbuf = sb("wbuf", [P, 20 * D])
        wsm = wbuf[:, 0:12 * D].rearrange("p (w c d) -> p w c d", w=6, c=2)
        w2 = wbuf[:, 12 * D:20 * D].rearrange("p (f d) -> p f d", f=FC)
        w1 = sb("w1", [P, 2, FF])
        ident = sb("ident", [P, P])
        st = sb("st", [P, POS, 6])
        vec = sb("vec", [P, 8, POS])
        small = sb("small", [P, 224])
        s4in = sb("s4in", [P, 9, HF])
        s4v = sb("s4v", [P, 14, HF])
        s4c = sb("s4c", [P, 2 * FR + HG])
        dft = sb("dft", [FR, 2 * S + 1])
        drow = sb("drow", [1, D + S + P])
        rwb = sb("rwb", [P, D])
        w1f = w1[:, :, :].rearrange("p a b -> p (a b)")
        V_S, V_D, V_Q, V_W, V_R, V_B, V_A, V_Z = range(8)

        wf = work[:, :]
        hn = wf[:, 0:18432].bitcast(F16).rearrange("p (c l j d) -> p c l j d", c=NCH, l=2, j=CH)
        hn32 = wf[:, 0:18432].rearrange("p (c j d) -> p c j d", c=NCH, j=CH)
        toep = wf[:, 18432:24576].bitcast(F16).rearrange("p (r t l c) -> p r t l c", r=TRING, t=P, l=2)
        stage = wbuf[:, 0:16 * D].bitcast(F16).rearrange("p (b x c) -> p b x c", b=UCH // TCH, c=TCH)
        img = wf[:, 18432:24576].rearrange("p (k n q) -> p k n q", k=KC, n=CH)
        junk4 = wf[:, 20448:22496].rearrange("p (j d) -> p j d", j=CH)
        wT = wsm[:, 0:3].rearrange("p a b d -> p (a b d)").rearrange("p (k d) -> p k d", k=KC)
        brow = wsm[:, 3, 0]
        posb = w2
        t32_even = w1f.rearrange("p (j d) -> p j d", j=CH)

        def sil(n):
            return w1f[:, (n % SIL) * GRP * POS:(n % SIL + 1) * GRP * POS]

        late = h0[:, 5 * CH:POS].rearrange("p j d -> p (j d)")
        rhsA = late[:, 0:2048].rearrange("p (f c e) -> p f c e", f=HF, c=8)
        rhsB = late[:, 2048:4096].rearrange("p (f c e) -> p f c e", f=HF, c=8)
        NE = HF * FR
        er, ei, iv = (late[:, 4096 + i * NE:4096 + (i + 1) * NE].rearrange("p (f m) -> p f m", m=FR) for i in range(3))
        t1 = w1f[:, 0:NE].rearrange("p (f m) -> p f m", m=FR)
        qs = late[0:FR, 0:2048].rearrange("p (f c e) -> p c f e", f=HF, c=8)
        gt = late[0:FR, 2048:4096].rearrange("p (c f e) -> p c f e", c=8, f=HF)
        ksb = late[0:S, 4096:4352]
        kneg = late[0:S, 4352:4608]
        kp = s4in[0:S].rearrange("p a b -> p (a b)")[:, 0:D].bitcast(F16).rearrange("p (l c) -> p l c", l=2)
        pick = vec[0:S, V_Z, 0:S].bitcast(F16)

        h1s = wf[:, 0:4096].rearrange("p (q d) -> p q d", q=NQ)
        gs = wf[:, 4096:8192].rearrange("p (q d) -> p q d", q=NQ)
        xT = wf[:, 8192:9216].rearrange("p (c n) -> p c n", c=2)
        hnr = wf[:, 9216:9728].rearrange("p (b d) -> p b d", b=2)
        hnr2 = wf[:, 9728:10240].rearrange("p (b d) -> p b d", b=2)
        tab = wf[:, 8192:10240].rearrange("p (k b f n) -> p k b f n", k=2, b=NBB, f=2)
        qT = wf[:, 10240:11264].rearrange("p (h t i) -> p h t i", h=2, t=SQ)
        kx = wf[:, 11264:12352].rearrange("p (h t e i) -> p h t e i", h=2, t=SQ, e=2)
        tmp = wf[:, 12352:12896].rearrange("p (b n) -> p b n", b=2)
        cs = wf[:, 12896:15072].rearrange("p (f n) -> p f n", f=2)
        su = wf[:, 15072:19424].rearrange("p (x n) -> p x n", x=4)
        pr = wf[:, 15072:17120].rearrange("p (q r c i) -> p q r c i", q=4, r=4, c=4)
        prT = wf[:, 17120:19168].rearrange("p (q r c i) -> p q r c i", q=4, r=4, c=4)
        vv = wf[:, 19424:21472].rearrange("p (b q d) -> p b q d", b=2, q=4)
        oT = wf[:, 21472:22496].rearrange("p (q h b i) -> p q h b i", q=4, h=2, b=4)
        x1 = wf[:, 22496:24544].rearrange("p (b q d) -> p b q d", b=2, q=4)
        am = wf[:, 22496:23648].rearrange("p (k b n) -> p k b n", k=2, b=NBB)
        tk = wf[0:S, 4096:8192].rearrange("p (x n) -> p x n", n=256)
        rp = wbuf[:, 16 * D:18 * D].rearrange("p (x n) -> p x n", n=P)
        dg = wf[0:S, 19424:19968].bitcast(BF16).rearrange("p (t i) -> p t i", t=S)
        ones_b = wf[0:S, 19968:20032].bitcast(BF16)
        hT = h0[:, 0:9].rearrange("p j d -> p (j d)")[:, 0:FC * NC].rearrange("p (f n) -> p f n", f=FC)
        yT = h0[:, 12:16].rearrange("p j d -> p (j d)").rearrange("p (h t i) -> p h t i", h=2, t=SQ)
        x2T = h0[:, 16:20].rearrange("p j d -> p (j d)").rearrange("p (c n) -> p c n", c=2)
        msk = s4in[:, :, :].rearrange("p a b -> p (a b)")[:, 0:NQ * KSEL].rearrange("p (q k) -> p q k", q=NQ)

        cols = {}

        def col(name, n=1):
            if name not in cols:
                cols[name] = sum(w for _, w in cols.values()), n
            o, w = cols[name]
            assert o + w <= 32
            return small[:, o:o + w]

        eps_ln, eps_rms, amax, kscale, yscale, am64, am1 = (
            col(x) for x in ("eps_ln", "eps_rms", "amax", "kscale", "yscale", "am64", "am1"))
        cst = col("cst", 5)
        rbias = col("rbias")
        lnw = col("lnw", 4)
        srw = col("srw")
        idxg = small[:, 32:48].bitcast(U32)
        idxs = small[:, 48:64].bitcast(U32)
        notm = small[:, 64:80]
        wsel = small[:, 80:96]
        r1 = small[:, 96:112]
        sm, sd, sq_, rr, nb = (small[:, 112 + 16 * i:128 + 16 * i] for i in range(5))
        rinv = s4v[:, 0:2, :].rearrange("p a b -> p (a b)")
        mx = s4v[:, 2:4, :].rearrange("p a b -> p (a b)")
        st2 = s4v[:, 4:7, :].rearrange("p a b -> p (a b)").rearrange("p (q x) -> p q x", x=6)
        ssq = s4v[:, 7, 0:16]
        ssq2 = s4v[:, 7, 16:32]
        rms1 = s4v[:, 9, 0:16]
        rms2 = s4v[:, 8, 0:16]
        rr2 = s4v[:, 8, 16:32]
        posi = small[:, 192:200].bitcast(I32)
        invf = small[:, 200:216]
        base = s4in[0:S].rearrange("p a b -> p (a b)")[:, 0:TOK]
        c_c, c_s, c_e = s4c[:, 0:FR], s4c[:, FR:2 * FR], s4c[:, 2 * FR:]

        psum = ctx.enter_context(nc.psum_tensor("psum", [P, 8, 512], F32))

        names = """const s4in rope img pos khl act_s4 dve x rhs q g k am amt amb emb embv var std nrm t32 hi lo
            tz rwprod rwdot conv built tba tbv sil addv addp wload w1load wready mload var3 std3 rows w72 wmov idx idxp idxr ind seldg oh
            tabf tabs tab tokload rvar rstd g1 ssq rms1 rms1r gemm evv eva qk sc pin pexp pt pv ot x1 ssq2 rms2 rms2r
            hrow h2row fin outc outd mbank h1out poolw""".split()
        s = {n: sem("s_" + n) for n in names}
        s_txt = [sem(f"s_txt{c}") for c in range(NCH)]
        s_scat = [sem(f"s_scat{g}") for g in range(SG)]
        s_gath = [sem(f"s_gath{q}") for q in range(NQ)]

        plan = gemm_plan()
        use_of = {u: n for n, u in enumerate(plan)}
        emptied = []
        for n, (what, _, _) in enumerate(plan):
            by = what in BY_ACT
            emptied.append((by, 1 + sum(1 for b, _ in emptied if b == by)))

        s_toep = [sem(f"s_toep{r}") for r in range(TRING)]
        toep_emptied = []
        for m in range(NU * NB):
            by = "tbv" if m >= 2 * NB and m % 2 else "tba"
            toep_emptied.append((by, 1 + sum(1 for b, _ in toep_emptied if b == by)))

        def later_builds(n):
            m = 2 * NB + 2 * (n - 4)
            return (m, m + 1) if 2 * NB <= m < NU * NB else ()

        def unit_kept(eng, u):
            for by in ("tba", "tbv"):
                count = max([c for b, c in toep_emptied[:(u + 1) * NB] if b == by] + [0])
                if count:
                    eng.wait_ge(s[by], count)

        def placed(eng, n):
            eng.wait_ge(s_toep[n % TRING], 32 * (n // TRING + 1))

        def keep_toep(eng, copy, m):
            u, k = divmod(m, NB)
            if u >= 2 and k < 2:
                for n in range(4 * (u - 2) + 1, 4 * (u - 2) + 4):
                    placed(eng, n)
            eng.wait_ge(s["built"], m + 1)
            h = slice(64 * (u % 2), 64 * (u % 2) + 64)
            copy(stage[h, :, k * 2 * QT:(k + 1) * 2 * QT, :].rearrange("p b x c -> p x b c"),
                 psum[h, 4 + m % 4, :].rearrange("p (x b c) -> p x b c", b=UCH // TCH, c=TCH)).then_inc(s[toep_emptied[m][0]], 1)

        def bank(u):
            return psum[:, 4 + use_of[u] % 4, :]

        def pos_of(c):
            return slice(c * CH, c * CH + CH)

        def t32(n):
            return t32_even if n % 2 == 0 else hn32[:, ORDER[-1]]

        def row1(x, n):
            return x.rearrange("p (o d) -> p o d", o=1).to_broadcast([x.shape[0], n, x.shape[1]])

        def col1(x, n):
            return x.rearrange("p (f o) -> p f o", o=1).to_broadcast([x.shape[0], x.shape[1], n])

        def add_group(eng, n):
            x = h0[:, :, n * GRP:(n + 1) * GRP]
            return eng.tensor_tensor(x, x, sil(n).rearrange("p (c j) -> p j c", c=GRP), ALU.add)

        block = ctx.enter_context(nc.Block())

        @block.sync
        def _(sp):
            sp.dma_start(s4in[:, :, :], a["s4in"]).then_inc(s["s4in"], 16)
            sp.dma_start(s4c[:, :], a["s4c"]).then_inc(s["s4in"], 16)
            for dst, name in ((dft[:, :], "dft"), (drow[:, :], "drow"), (ident[:, :], "ident"), (cst, "cst"), (lnw, "lnw"),
                              (pick, "pick")):
                sp.dma_start(dst, a[name]).then_inc(s["const"], 16)
            sp.dma_start(rwb[:, :], a["rw"].rearrange("d o -> o d").to_broadcast([P, D])).then_inc(s["const"], 16)

            sp.dma_start(rbias, a["rb"].rearrange("(o d) -> o d", o=1).to_broadcast([P, 1])).then_inc(s["const"], 16)
            sp.dma_start(posi, a["posT"]).then_inc(s["rope"], 16)
            sp.dma_start(invf, a["invf"]).then_inc(s["rope"], 16)

            def text(c):
                for g in range(2):
                    lo = (c - 1) * CH + 64 * g
                    sp.dma_start(h0[64 * g:64 * g + 64, pos_of(c), :], a["txt"][:, lo:lo + CH, :]).then_inc(s_txt[c], 16)

            text(1)
            sp.dma_start(wT, a["wT"]).then_inc(s["img"], 16)
            sp.dma_start(img, a["img"]).then_inc(s["img"], 16)
            for g in range(2):
                sp.dma_start(posb[64 * g:64 * g + 64, :, :],
                             a["pos_emb"][g * 8:g * 8 + 8, :].rearrange("(o n) d -> o n d", o=1).to_broadcast([64, 8, D])
                             ).then_inc(s["pos"], 16)
            sp.dma_start(brow, a["b"].rearrange("(o d) -> o d", o=1).to_broadcast([P, D])).then_inc(s["pos"], 16)
            for c in range(2, 5):
                text(c)
            sp.wait_ge(s["khl"], 1)
            for c in range(5, 9):
                text(c)
            sp.wait_ge(s["tz"], 2)
            for n in range(NT):
                u, k = divmod(n, UCH // TCH)
                if k == 0:
                    unit_kept(sp, u)
                if n >= TRING:
                    sp.wait_ge(s["conv"], TCH // GRP * (n - TRING + 1))
                for g in range(2):
                    h = slice(64 * (u % 2), 64 * (u % 2) + 64)
                    sp.dma_start(toep[64 * g:64 * g + 64, n % TRING, 64 * g:64 * g + 64],
                                 stage[h, k].rearrange("p (t l) c -> p t l c", l=2)).then_inc(s_toep[n % TRING], 16)
            for n in range(NT - TRING, NT):
                placed(sp, n)
            for i, w in ((0, "wq"), (1, "wk"), (4, "wv"), (5, "wo")):
                sp.dma_start(wsm[:, i], a[w].rearrange("(c p) d -> p c d", p=P)).then_inc(s["wload"], 16)
            sp.wait_ge(s["built"], NU * NB)
            sp.dma_start(base, a["base"]).then_inc(s["tokload"], 16)
            sp.wait_ge(s["addv"], NGRP // 2)
            sp.wait_ge(s["addp"], NGRP // 2)
            rows = h1_rows.rearrange("(s t) d -> s t d", t=TOK)
            for g in range(2):
                sp.dma_start(rows[:, 8 * g:8 * g + 8, :], h0[64 * g:64 * g + 64, 0:8, :]).then_inc(s["h1out"], 16)
                sp.dma_start(rows[:, 16 + 64 * g:80 + 64 * g, :], h0[64 * g:64 * g + 64, 8:POS, :]).then_inc(s["h1out"], 16)
            sp.wait_ge(s["tab"], 1)
            sp.dma_start(w2, a["w2"].rearrange("(c p) d -> p c d", p=P)).then_inc(s["w1load"], 16)
            sp.dma_start(w1[:, :, :], a["w1"].rearrange("(c p) f -> p c f", p=P)).then_inc(s["w1load"], 16)
            sp.dma_start(am[:, 0], a["mask"][:, 0:P, :].rearrange("b j n -> j b n")).then_inc(s["mload"], 16)
            sp.dma_start(am[0:TOK - P, 1], a["mask"][:, P:TOK, :].rearrange("b j n -> j b n")).then_inc(s["mload"], 16)
            for c in range(NCH):
                sp.wait_ge(s["outc"], c + 1)
                for g in range(2):
                    lo = 8 * g if c == 0 else 16 + 64 * g + (c - 1) * CH
                    sp.dma_start(out[:, lo:lo + CH, :], h0[64 * g:64 * g + 64, pos_of(c), :]).then_inc(s["outd"], 16)
            sp.wait_ge(s["outd"], 32 * NCH)

        @block.tensor
        def _(pe):
            mm = pe.matmul
            pe.wait_ge(s["x"], 1)
            pe.wait_ge(s["rhs"], 1)
            for f in range(HF):
                o = psum[0:FR, 4 + f // 8, (f % 8) * 64:(f % 8) * 64 + 64]
                mm(o, er[:, f, :], rhsA[:, f].rearrange("p c e -> p (c e)"), start=True, stop=False)
                ins = mm(o, ei[:, f, :], rhsB[:, f].rearrange("p c e -> p (c e)"), start=False, stop=True)
            ins.then_inc(s["q"], 1)

            def embed(j):
                if j >= 2:
                    pe.wait_ge(s["embv"], j - 1)
                for k in range(KC):
                    ins = mm(psum[:, j % 2, 0:D], img[:, k, j, :], wT[:, k, :], start=(k == 0), stop=(k == KC - 1))
                ins.then_inc(s["emb"], 1)

            pe.wait_ge(s["img"], 32)
            embed(0)
            embed(1)
            pe.wait_ge(s["const"], 128)
            pe.wait_ge(s["g"], 1)
            mm(psum[0:S, 2, 0:D], dft[:, 0:S], gt[:, 0].rearrange("p f e -> p (f e)"), start=True, stop=False)
            mm(psum[0:S, 2, 0:D], dft[:, S:2 * S], gt[:, 2].rearrange("p f e -> p (f e)"), start=False, stop=False)
            mm(psum[0:S, 2, 0:D], drow[:, D:D + S], drow[:, 0:D], start=False, stop=True).then_inc(s["k"], 1)
            pe.wait_ge(s["am"], 1)
            pe.transpose(psum[0:1, 3, 0:S], am64[0:S], ident[0:S, 0:S]).then_inc(s["amt"], 1)
            pe.wait_ge(s["am"], 2)
            mm(psum[:, 3, 128:129], drow[:, D + S:], am1[0:1], start=True, stop=True).then_inc(s["amt"], 1)
            for j in range(2, CH):
                embed(j)
            pe.wait_ge(s["khl"], 1)

            def build(m):
                if m >= 4:
                    by, count = toep_emptied[m - 4]
                    pe.wait_ge(s[by], count)
                u, k = divmod(m, NB)
                for i in range(QT):
                    t = k * QT + i
                    ins = mm(psum[64 * (u % 2):64 * (u % 2) + 64, 4 + m % 4, i * 2 * UCH:(i + 1) * 2 * UCH],
                             pick[:, S - 1 - t:2 * S - 1 - t], kp[:, :, u * UCH:(u + 1) * UCH], start=True, stop=True)
                ins.then_inc(s["built"], 1)

            for m in range(2 * NB):
                build(m)
            pe.wait_ge(s["hi"], NCH)
            pe.wait_ge(s["lo"], NCH)
            pe.wait_ge(s["amb"], 1)
            for n in range(NGRP):
                e, r = divmod(n, TCH // GRP)
                if r == 0:
                    placed(pe, e)
                if n >= CSLOT:
                    pe.wait_ge(s["sil"], n - CSLOT + 1)
                for i in range(GRP):
                    ch = n * GRP + i
                    o = psum[:, 2 * (n % CSLOT) + i // 4, (i % 4) * POS:(i % 4 + 1) * POS]
                    t_hi, t_lo = (toep[:, e % TRING, :, l, ch % TCH] for l in range(2))
                    x_hi, x_lo = (hn[:, :, l, :, ch] for l in range(2))
                    mm(o, t_hi, x_hi, start=True, stop=False)
                    mm(o, t_hi, x_lo, start=False, stop=False)
                    ins = mm(o, t_lo, x_hi, start=False, stop=True)
                ins.then_inc(s["conv"], 1)
                for m in later_builds(n):
                    build(m)
            pe.wait_ge(s["w72"], 1)
            pe.wait_ge(s["sil"], NGRP)
            for g in range(2):
                ins = mm(psum[0:S, 0, g * POS:(g + 1) * POS], ident[:, 64 * g:64 * g + 64], vec[:, V_W, :], start=True, stop=True)
            ins.then_inc(s["wmov"], 1)
            pe.wait_ge(s["idx"], 1)
            for x in range(3):
                for b in range(4):
                    ins = mm(psum[32 * b:32 * b + 32, 1, x * NQ:(x + 1) * NQ], tk[:, 10 + x, 0:SLOT], ident[0:S, b:S:4],
                             start=True, stop=True)
            ins.then_inc(s["idxp"], 1)
            pe.wait_ge(s["seldg"], 1)
            for b in range(4):
                ins = mm(psum[:, 2 + b, 0:NC], ones_b,
                         dg[:, SQ * b:SQ * b + SQ, :].rearrange("p t i -> p (t i)"), start=True, stop=True)
            ins.then_inc(s["ind"], 1)

            def begin(u):
                n = use_of[u]
                if n >= 4:
                    by, count = emptied[n - 4]
                    pe.wait_ge(s["eva"] if by else s["evv"], count)
                return bank(u)

            pe.wait_ge(s["oh"], 1)
            pe.wait_ge(s["tab"], 1)
            parts = [(bb * KSEL, (bb + 1) * KSEL, bb) for bb in range(NBB - 1)]
            for g in range(SG):
                for i in range(2):
                    o = begin(("cs", g, i))
                    for lo, hi, bb in (parts + [(3 * KSEL, NC, 3)] if g == 0 else [(0, NC, 3)]):
                        c = slice(g * NC + lo, g * NC + hi)
                        mm(o[:, lo:hi], tab[:, 0, bb, i, :], su[:, 0, c], start=True, stop=False)
                        ins = mm(o[:, lo:hi], tab[0:16, 1, bb, i, :], su[0:16, 1, c], start=False, stop=True)
                    ins.then_inc(s["gemm"], 1)
            pe.wait_ge(s["mload"], 32)
            for g in range(SG):
                for i in range(2):
                    o = begin(("u", g, i))
                    rows = P if i == 0 else TOK - P
                    for lo, hi, bb in (parts + [(3 * KSEL, NC, 3)] if g == 0 else [(0, NC, 3)]):
                        c = slice(g * NC + lo, g * NC + hi)
                        mm(o[0:rows, lo:hi], am[:, 0, bb, P * i:P * i + rows], su[:, 0, c], start=True, stop=False)
                        ins = mm(o[0:rows, lo:hi], am[0:16, 1, bb, P * i:P * i + rows], su[0:16, 1, c], start=False, stop=True)
                    ins.then_inc(s["gemm"], 1)
            o = begin(("mask", 0, 0))
            pe.wait_ge(s["mbank"], 1)
            pe.wait_ge(s["evv"], emptied[use_of[("u", SG - 1, 1)]][1])
            for t in range(S):
                c = slice(t * KSEL, (t + 1) * KSEL)
                b, q = t % 4, t // 4
                mm(o[32 * b:32 * b + KSEL, q * KSEL:(q + 1) * KSEL], su[:, 2, c], su[:, 0, c], start=True, stop=False)
                ins = mm(o[32 * b:32 * b + KSEL, q * KSEL:(q + 1) * KSEL], su[0:16, 3, c], su[0:16, 1, c], start=False, stop=True)
            ins.then_inc(s["gemm"], 1)

            def project(g):
                for i in range(4):
                    o = begin(("xt", g, i))
                    pe.wait_ge(s["hrow"], 4 * g + i + 1)
                    for c in range(2):
                        ins = pe.transpose(o[:, c * P:(c + 1) * P], hnr[:, i % 2, c * P:(c + 1) * P], ident[:, :])
                    ins.then_inc(s["gemm"], 1)
                pe.wait_ge(s["eva"], emptied[use_of[("xt", g, 3)]][1])
                if g == 0:
                    pe.wait_ge(s["wready"], 1)
                for h in range(2):
                    for w, name in ((0, "q"), (2, "qr"), (1, "k"), (3, "kr")):
                        o = begin((name, g, h))
                        for c in range(2):
                            x = xT[:, c, :].rearrange("p (t i) -> p t i", i=SLOT)[:, :, 0:KSEL]
                            ins = mm(o[:, 0:NC], wsm[:, w, c, h * P:(h + 1) * P], x, start=(c == 0), stop=(c == 1))
                        ins.then_inc(s["gemm"], 1)
                for i in range(4):
                    o = begin(("v", g, i))
                    for c in range(2):
                        ins = mm(o[:, 0:D], xT[:, c, i * P:(i + 1) * P], wsm[:, 4, c, :], start=(c == 0), stop=(c == 1))
                    ins.then_inc(s["gemm"], 1)

            def scores(g):
                pe.wait_ge(s["qk"], 4 * (g + 1))
                if g >= 1:
                    pe.wait_ge(s["ot"], g)
                for q in range(4):
                    for h in range(2):
                        for b in range(4):
                            for r in range(4):
                                t = 4 * q + b
                                ins = mm(psum[32 * b:32 * b + 32, r, (2 * q + h) * 34:(2 * q + h) * 34 + 34],
                                         qT[32 * r:32 * r + 32, h, t, :],
                                         kx[32 * r:32 * r + 32, h, t].rearrange("p e i -> p (e i)"), start=True, stop=True)
                ins.then_inc(s["sc"], 1)

            def attend(g):
                pe.wait_ge(s["pt"], g + 1)
                pe.wait_ge(s["eva"], emptied[use_of[("v", g, 3)]][1])
                for q in range(4):
                    for h in range(2):
                        for b in range(4):
                            for r in range(4):
                                ins = mm(psum[32 * r:32 * r + 32, b, (2 * q + h) * 34:(2 * q + h) * 34 + 34],
                                         vv[32 * b:32 * b + KSEL, g % 2, q, h * P + 32 * r:h * P + 32 * r + 32],
                                         prT[32 * b:32 * b + KSEL, q, r, 2 * h:2 * h + 2, 0:KSEL], start=True, stop=True)
                ins.then_inc(s["pv"], 1)

            def merge(g):
                pe.wait_ge(s["ot"], g + 1)
                for i in range(4):
                    o = begin(("o", g, i))
                    for h in range(2):
                        ins = mm(o[:, 0:D], oT[:, i, h].rearrange("p b i -> p (b i)"), wsm[:, 5, h, :],
                                 start=(h == 0), stop=(h == 1))
                    ins.then_inc(s["gemm"], 1)

            def mlp(g):
                for i in range(4):
                    o = begin(("x2t", g, i))
                    pe.wait_ge(s["h2row"], 4 * g + i + 1)
                    for c in range(2):
                        ins = pe.transpose(o[:, c * P:(c + 1) * P], hnr2[:, i % 2, c * P:(c + 1) * P], ident[:, :])
                    ins.then_inc(s["gemm"], 1)
                pe.wait_ge(s["eva"], emptied[use_of[("x2t", g, 3)]][1])
                if g == 0:
                    pe.wait_ge(s["wready"], 2)
                for f in range(FC):
                    o = begin(("h", g, f))
                    for c in range(2):
                        x = x2T[:, c, :].rearrange("p (t i) -> p t i", i=SLOT)[:, :, 0:KSEL]
                        ins = mm(o[:, 0:NC], w1[:, c, f * P:(f + 1) * P], x, start=(c == 0), stop=(c == 1))
                    ins.then_inc(s["gemm"], 1)
                for h in range(2):
                    o = begin(("y", g, h))
                    for f in range(FC):
                        if h == 0:
                            pe.wait_ge(s["eva"], emptied[use_of[("h", g, f)]][1])
                        ins = mm(o[:, 0:NC], w2[:, f, h * P:(h + 1) * P], hT[:, f, :], start=(f == 0), stop=(f == FC - 1))
                    ins.then_inc(s["gemm"], 1)
                pe.wait_ge(s["evv"], emptied[use_of[("y", g, 1)]][1])
                for i in range(4):
                    o = begin(("yt", g, i))
                    for h in range(2):
                        ins = pe.transpose(o[:, h * P:(h + 1) * P], yT[:, h, 4 * i:4 * i + 4, :].rearrange("p t i -> p (t i)"),
                                           ident[:, :])
                    ins.then_inc(s["gemm"], 1)

            project(0)
            for g in range(SG):
                scores(g)
                if g + 1 < SG:
                    project(g + 1)
                attend(g)
                if g >= 1:
                    mlp(g - 1)
                merge(g)
            mlp(SG - 1)

        @block.scalar
        def _(act):
            fn = act.activation
            act.wait_ge(s["s4in"], 32)
            fn(s4v[:, 0, :], s4in[:, 0, :], ACT.Exp).then_inc(s["act_s4"], 1)
            fn(s4v[:, 1, :], s4in[:, 1, :], ACT.Exp).then_inc(s["act_s4"], 1)
            for n, c in enumerate(ORDER):
                act.wait_ge(s["var"], n + 1)
                fn(vec[:, V_D, pos_of(c)], vec[:, V_Q, pos_of(c)], ACT.Sqrt, bias=eps_ln, scale=1.0 / D).then_inc(s["std"], 1)
                act.wait_ge(s["nrm"], n + 1)
                if n == NCH - 1:
                    act.wait_ge(s["lo"], n)
                for j in range(CH):
                    q = c * CH + j
                    ins = fn(hn[:, c, 0, j, :], h0[:, q, :], ACT.Identity, bias=vec[:, V_B, q:q + 1], scale=vec[:, V_R, q:q + 1])
                ins.then_inc(s["hi"], 1)
                for m in range(6 * (n - 3), min(6 * (n - 2), 2 * NB)) if n >= 3 else ():
                    keep_toep(act, act.copy, m)
            act.wait_ge(s["tabf"], 1)
            fn(rp[:, 2:4], rp[:, 2:4], ACT.Sin).then_inc(s["tabs"], 1)
            act.wait_ge(s["lo"], NCH)
            for n in range(NGRP):
                act.wait_ge(s["conv"], n + 1)
                if n >= SIL:
                    act.wait_ge(s["addv"] if (n - SIL) % 2 == 0 else s["addp"], (n - SIL) // 2 + 1)
                k = 2 * (n % CSLOT)
                fn(sil(n).rearrange("p (b x) -> p b x", b=2), psum[:, k:k + 2, 0:4 * POS], ACT.Silu, scale=yscale
                   ).then_inc(s["sil"], 1)
                for m in later_builds(n)[0:1]:
                    keep_toep(act, act.copy, m)
            for c in range(RW_ACT):
                act.wait_ge(s["rwprod"], c + 1)
                for q in range(c * CH, (c + 1) * CH):
                    ins = fn(hn32[:, c, q % CH, :], hn32[:, c, q % CH, :], ACT.Identity, accum_out=vec[:, V_W, q:q + 1])
            ins.then_inc(s["rwdot"], 1)
            act.wait_ge(s["var3"], 1)
            fn(vec[:, V_D, :], vec[:, V_Q, :], ACT.Sqrt, bias=eps_ln, scale=1.0 / D).then_inc(s["std3"], 1)
            for g in range(SG):
                q4 = slice(4 * g, 4 * g + 4)
                act.wait_ge(s["rvar"], g + 1)
                fn(sd[:, q4], sq_[:, q4], ACT.Sqrt, bias=eps_ln, scale=1.0 / D).then_inc(s["rstd"], 1)
                act.wait_ge(s["rows"], g + 1)
                for q in range(4 * g, 4 * g + 4):
                    fn(gs[:, q], h1s[:, q], ACT.Identity, bias=nb[:, q:q + 1], scale=rr[:, q:q + 1]).then_inc(s["g1"], 1)
                    act.wait_ge(s["g1"], q + 1)
                    if q >= 2:
                        act.wait_ge(s["ssq"], q - 1)
                    fn(tmp[:, q % 2, 0:D], gs[:, q], ACT.Square, accum_out=ssq[:, q:q + 1]).then_inc(s["ssq"], 1)
                act.wait_ge(s["ssq"], 4 * g + 4)
                fn(rms1[:, q4], ssq[:, q4], ACT.Sqrt, bias=eps_rms, scale=1.0 / D).then_inc(s["rms1"], 1)

            def empty(u, dst, src, func=ACT.Copy):
                act.wait_ge(s["gemm"], use_of[u] + 1)
                fn(dst, src, func).then_inc(s["eva"], 1)

            for g in range(SG):
                for i in range(2):
                    empty(("cs", g, i), cs[:, i, g * NC:(g + 1) * NC], bank(("cs", g, i))[:, 0:NC])

            def project(g):
                act.wait_ge(s["rms1r"], g + 1)
                for i in range(4):
                    q = 4 * g + i
                    if q < 2:
                        act.wait_ge(s["ssq"], NQ)
                        act.wait_ge(s["eva"], emptied[use_of[("cs", SG - 1, 1)]][1])
                    else:
                        act.wait_ge(s["gemm"], use_of[("xt", (q - 2) // 4, (q - 2) % 4)] + 1)
                    fn(hnr[:, i % 2], gs[:, q], ACT.Identity, scale=r1[:, q:q + 1]).then_inc(s["hrow"], 1)
                    if i >= 1:
                        turn(g, i - 1)
                turn(g, 3)
                for i in range(4):
                    if g >= 2:
                        act.wait_ge(s["pv"], g - 1)
                    empty(("v", g, i), vv[:, g % 2, i], bank(("v", g, i))[:, 0:D])

            def turn(g, i):
                if g >= 1:
                    act.wait_ge(s["gemm"], use_of[("v", g - 1, 3)] + 1)
                empty(("xt", g, i), xT[:, :, i * P:(i + 1) * P], bank(("xt", g, i))[:, 0:2 * P].rearrange("p (c n) -> p c n", c=2))

            def mlp(g):
                for i in range(4):
                    act.wait_ge(s["ssq2"], 4 * g + i + 1)
                    fn(rms2[:, 4 * g + i:4 * g + i + 1], ssq2[:, 4 * g + i:4 * g + i + 1], ACT.Sqrt, bias=eps_rms,
                       scale=1.0 / D).then_inc(s["rms2"], 1)
                    act.wait_ge(s["rms2r"], 4 * g + i + 1)
                    fn(hnr2[:, i % 2], x1[:, g % 2, i], ACT.Identity, scale=rr2[:, 4 * g + i:4 * g + i + 1]).then_inc(s["h2row"], 1)
                    if g >= 1:
                        act.wait_ge(s["gemm"], use_of[("h", g - 1, FC - 1)] + 1)
                    else:
                        act.wait_ge(s["outd"], 32 * NCH)
                    empty(("x2t", g, i), x2T[:, :, i * P:(i + 1) * P],
                          bank(("x2t", g, i))[:, 0:2 * P].rearrange("p (c n) -> p c n", c=2))
                for f in range(FC):
                    if g >= 1:
                        act.wait_ge(s["gemm"], use_of[("y", g - 1, 1)] + 1)
                    empty(("h", g, f), hT[:, f, :], bank(("h", g, f))[:, 0:NC], ACT.Gelu_apprx_tanh)

            def exps(g):
                act.wait_ge(s["pin"], g + 1)
                p3 = pr.rearrange("p q r c i -> p (q r c) i")[:, :, 0:KSEL]
                fn(p3, p3, ACT.Exp).then_inc(s["pexp"], 1)

            project(0)
            for g in range(SG):
                exps(g)
                if g + 1 < SG:
                    project(g + 1)
                if g >= 1:
                    mlp(g - 1)
            mlp(SG - 1)

        @block.vector
        def _(v):
            done = [0]
            TT = v.tensor_tensor

            def link(ins):
                done[0] += 1
                ins.then_inc(s["dve"], 1)
                v.wait_ge(s["dve"], done[0])

            def moments(dst_s, dst_d, dst_q, x):
                TT(dst_s, x[:, :, 1], x[:, :, 4], ALU.add)
                TT(dst_q, x[:, :, 2], x[:, :, 5], ALU.add)
                link(TT(dst_d, x[:, :, 1], x[:, :, 4], ALU.subtract))
                link(v.scalar_tensor_tensor(dst_d, dst_d, D / 4.0, dst_d, ALU.mult, ALU.mult))
                return TT(dst_q, dst_q, dst_d, ALU.add)

            v.memset(eps_ln, LN_EPS)
            v.memset(eps_rms, RMS_EPS)
            v.wait_ge(s["s4in"], 32)
            v.wait_ge(s["act_s4"], 2)
            dt, ew, aw, bw = (s4v[:, i, :] for i in range(4))
            TT(aw, ew, dt, ALU.mult)
            link(TT(bw, s4in[:, 2, :], dt, ALU.mult))
            cb, sb_ = row1(c_c, HF), row1(c_s, HF)
            TT(er, col1(aw, FR), cb, ALU.mult)
            link(TT(t1, col1(bw, FR), cb, ALU.mult))
            link(TT(ei, sb_, t1, ALU.subtract))
            TT(iv, ei, ei, ALU.mult)
            link(TT(t1, er, er, ALU.mult))
            link(TT(iv, iv, t1, ALU.add))
            link(v.reciprocal(iv, iv))
            TT(er, er, iv, ALU.mult)
            TT(ei, ei, iv, ALU.mult).then_inc(s["x"], 1)
            Br, Bi, Pr, Pi, Cr, Ci = (s4in[:, 3 + i, :] for i in range(6))
            ta, tb = s4v[:, 12, :], s4v[:, 13, :]
            for ab, (xr, xi, yr, yi, sg) in enumerate([(Br, Bi, Cr, Ci, 1), (Br, Bi, Pr, Pi, -1),
                                                       (Pr, Pi, Cr, Ci, 1), (Pr, Pi, Pr, Pi, -1)]):
                re, im = s4v[:, 4 + ab, :], s4v[:, 8 + ab, :]
                TT(ta, xr, yr, ALU.mult)
                link(TT(tb, xi, yi, ALU.mult))
                link(TT(re, ta, tb, ALU.subtract if sg > 0 else ALU.add))
                TT(ta, xi, yr, ALU.mult)
                link(TT(tb, xr, yi, ALU.mult))
                link(TT(im, ta, tb, ALU.add if sg > 0 else ALU.subtract))
            link(TT(s4v[:, 4:12, :], s4v[:, 4:12, :], row1(dt, 8), ALU.mult))
            eb = row1(c_e, HF)
            for i in range(4):
                re, im = col1(s4v[:, 4 + i, :], HG), col1(s4v[:, 8 + i, :], HG)
                TT(rhsA[:, :, i, :], re, eb, ALU.mult)
                TT(rhsA[:, :, 4 + i, :], im, eb, ALU.mult)
                TT(rhsB[:, :, i, :], im, eb, ALU.mult)
                ins = v.scalar_tensor_tensor(rhsB[:, :, 4 + i, :], re, -1.0, eb, ALU.mult, ALU.mult)
            ins.then_inc(s["rhs"], 1)
            v.wait_ge(s["pos"], 48)
            link(TT(posb[:, :, :], posb[:, :, :], row1(brow, 8), ALU.add))

            def kernel_spectrum():
                v.wait_ge(s["q"], 1)
                link(v.tensor_copy(late[0:FR, 0:2048], psum[0:FR, 4:8, :].rearrange("p b x -> p (b x)")))
                v.wait_ge(s["const"], 128)
                q = [qs[:, i] for i in range(8)]
                g = [gt[:, i] for i in range(8)]
                c = dft[:, 2 * S:2 * S + 1]
                TT(g[0], q[1], q[2], ALU.mult)
                TT(g[1], q[5], q[6], ALU.mult)
                TT(g[2], q[1], q[6], ALU.mult)
                link(TT(g[3], q[5], q[2], ALU.mult))
                TT(g[0], g[0], g[1], ALU.subtract)
                link(TT(g[2], g[2], g[3], ALU.add))
                v.tensor_scalar(g[0], g[0], c, None, ALU.mult)
                v.tensor_scalar(g[2], g[2], c, None, ALU.mult)
                v.tensor_scalar(g[4], q[3], c, 1.0, ALU.mult, ALU.add)
                link(v.tensor_scalar(g[5], q[7], c, None, ALU.mult))
                TT(g[6], g[4], g[4], ALU.mult)
                link(TT(g[7], g[5], g[5], ALU.mult))
                link(TT(g[6], g[6], g[7], ALU.add))
                link(v.reciprocal(g[6], g[6]))
                TT(g[1], g[0], g[4], ALU.mult)
                TT(g[3], g[2], g[5], ALU.mult)
                TT(g[7], g[2], g[4], ALU.mult)
                link(TT(g[0], g[0], g[5], ALU.mult))
                TT(g[1], g[1], g[3], ALU.add)
                link(TT(g[7], g[7], g[0], ALU.subtract))
                TT(g[1], g[1], g[6], ALU.mult)
                link(TT(g[7], g[7], g[6], ALU.mult))
                TT(g[0], q[0], g[1], ALU.subtract)
                link(TT(g[2], q[4], g[7], ALU.subtract))
                v.sem_inc(s["g"], 1)

            def kernel_parts():
                v.wait_ge(s["k"], 1)
                link(v.tensor_copy(ksb, psum[0:S, 2, 0:D]))
                link(v.tensor_scalar(kneg, ksb, -1.0, None, ALU.mult))
                link(TT(kneg, kneg, ksb, ALU.max))
                v.reduce_max(am64[0:S], kneg, AX).then_inc(s["am"], 1)
                v.wait_ge(s["amt"], 1)
                link(v.reduce_max(am1[0:1], psum[0:1, 3, 0:S], AX))
                v.tensor_scalar(am1[0:1], am1[0:1], 1e-30, None, ALU.max).then_inc(s["am"], 1)
                v.wait_ge(s["amt"], 2)
                link(v.tensor_copy(amax, psum[:, 3, 128:129]))
                v.tensor_scalar(yscale, amax, 1.0 / (T_PEAK * X_GAIN), None, ALU.mult).then_inc(s["amb"], 1)
                link(v.reciprocal(kscale, amax))
                link(v.tensor_scalar(kscale, kscale, T_PEAK, None, ALU.mult))
                link(v.tensor_scalar(ksb, ksb, kscale[0:S], None, ALU.mult))
                link(v.tensor_copy(kp[:, 0], ksb))
                link(TT(kp[:, 1], ksb, kp[:, 0], ALU.subtract))
                v.sem_inc(s["khl"], 1)

            def rope_angles():
                v.wait_ge(s["rope"], 32)
                v.wait_ge(s["embv"], CH)
                for k in range(2):
                    ins = v.tensor_copy(rp[:, 0, k * 64:k * 64 + 64].rearrange("p (b d) -> p b d", b=NBB),
                                        col1(posi[:, k * NBB:(k + 1) * NBB], HD))
                link(ins)
                x = rp[:, 0].rearrange("p (x d) -> p x d", d=HD)
                link(TT(x, x, row1(invf, 8), ALU.mult))
                link(v.tensor_scalar(rp[:, 1], rp[:, 0], float(1 / (2 * np.pi)), 12582912.0, ALU.mult, ALU.add))
                link(v.tensor_scalar(rp[:, 1], rp[:, 1], -12582912.0, None, ALU.add))
                for part in TWO_PI:
                    link(v.scalar_tensor_tensor(rp[:, 0], rp[:, 1], -part, rp[:, 0], ALU.mult, ALU.add))
                link(v.tensor_scalar(rp[:, 2], rp[:, 0], float(np.pi / 2), None, ALU.add))
                link(v.tensor_scalar(rp[:, 1], rp[:, 2], float(np.pi), float(-2 * np.pi), ALU.is_gt, ALU.mult))
                link(TT(rp[:, 2], rp[:, 2], rp[:, 1], ALU.add))
                v.tensor_scalar(rp[:, 2], rp[:, 2], PI_LOW, -PI_LOW, ALU.min, ALU.max)
                link(v.tensor_scalar(rp[:, 3], rp[:, 0], PI_LOW, -PI_LOW, ALU.min, ALU.max))
                v.sem_inc(s["tabf"], 1)

            def normaliser(n):
                p = pos_of(ORDER[n])
                v.wait_ge(s["std"], n + 1)
                link(v.reciprocal(vec[:, V_R, p], vec[:, V_D, p]))
                link(v.tensor_scalar(vec[:, V_R, p], vec[:, V_R, p], X_GAIN, None, ALU.mult))
                v.scalar_tensor_tensor(vec[:, V_B, p], vec[:, V_S, p], -0.5, vec[:, V_R, p], ALU.mult, ALU.mult
                                       ).then_inc(s["nrm"], 1)

            def low_part(n):
                v.wait_ge(s["hi"], n + 1)
                v.wait_ge(s["t32"], n + 1)
                TT(hn[:, ORDER[n], 1], t32(n), hn[:, ORDER[n], 0], ALU.subtract).then_inc(s["lo"], 1)

            for n, c in enumerate(ORDER):
                if c == 0:
                    for j in range(CH):
                        v.wait_ge(s["emb"], j + 1)
                        TT(h0[:, j, :], psum[:, j % 2, 0:D], posb[:, j, :], ALU.add).then_inc(s["embv"], 1)
                    v.wait_ge(s["embv"], CH)
                else:
                    v.wait_ge(s_txt[c], 32)
                for j in range(CH):
                    ins = v.bn_stats(st[:, c * CH + j, :], h0[:, c * CH + j, :])
                link(ins)
                p = pos_of(c)
                moments(vec[:, V_S, p], vec[:, V_D, p], vec[:, V_Q, p], st[:, p, :]).then_inc(s["var"], 1)
                if n >= 1:
                    normaliser(n - 1)
                if n >= 2:
                    low_part(n - 2)
                if n == 0:
                    kernel_spectrum()
                if n == 1:
                    kernel_parts()
                if n == 4:
                    rope_angles()
            normaliser(NCH - 1)
            low_part(NCH - 2)
            low_part(NCH - 1)
            for n in range(0, NGRP, 2):
                v.wait_ge(s["sil"], n + 1)
                add_group(v, n).then_inc(s["addv"], 1)
                for m in later_builds(n)[1:] + later_builds(n + 1)[1:]:
                    keep_toep(v, v.tensor_copy, m)
            v.wait_ge(s["addv"], NGRP // 2)
            v.wait_ge(s["addp"], NGRP // 2)
            for q in range(POS):
                ins = v.bn_stats(st[:, q, :], h0[:, q, :])
            link(ins)
            moments(vec[:, V_S, :], vec[:, V_D, :], vec[:, V_Q, :], st[:, :, :]).then_inc(s["var3"], 1)
            v.wait_ge(s["conv"], NGRP)
            v.memset(ones_b, 1.0)
            def junk_of(q):
                return (hn32[:, q // CH] if q // CH != RW_ACT else junk4)[:, q % CH, :]

            for q in range(RW_ACT * CH, POS):
                v.tensor_tensor_reduce(junk_of(q), h0[:, q, :], rwb[:, :], 1.0, 0.0, ALU.mult, ALU.add,
                                       vec[:, V_W, q:q + 1])
            link(v.reduce_sum(srw, rwb[:, :], AX))
            v.wait_ge(s["rwdot"], 1)
            v.wait_ge(s["std3"], 1)
            link(v.reciprocal(vec[:, V_R, :], vec[:, V_D, :]))
            link(v.scalar_tensor_tensor(vec[:, V_B, :], vec[:, V_S, :], -0.5, vec[:, V_R, :], ALU.mult, ALU.mult))
            TT(vec[:, V_W, :], vec[:, V_W, :], vec[:, V_R, :], ALU.mult)
            link(v.tensor_scalar(vec[:, V_A, :], vec[:, V_R, :], 1.0, None, ALU.add))
            link(v.scalar_tensor_tensor(vec[:, V_W, :], vec[:, V_B, :], srw, vec[:, V_W, :], ALU.mult, ALU.add))
            link(v.tensor_scalar(vec[:, V_W, :], vec[:, V_W, :], rbias, None, ALU.add))
            v.sem_inc(s["w72"], 1)
            W, W2, W3, gtm, eqm, pre, sel, key, _, m8 = (tk[:, i, 0:TOK] for i in range(10))
            v.wait_ge(s["wmov"], 1)
            for g in range(2):
                v.tensor_copy(W[:, 8 * g:8 * g + 8], psum[0:S, 0, g * POS:g * POS + 8])
                ins = v.tensor_copy(W[:, 16 + 64 * g:80 + 64 * g], psum[0:S, 0, g * POS + 8:(g + 1) * POS])
            link(ins)

            def top24(x, y, z):
                link(v.max(m8[:, 0:8], x))
                link(v.match_replace(y, m8[:, 0:8], x, NEG))
                link(v.max(m8[:, 8:16], y))
                link(v.match_replace(z, m8[:, 8:16], y, NEG))
                link(v.max(m8[:, 16:24], z))

            top24(W, W2, W3)
            last, thr = m8[:, KSEL - 1:KSEL], m8[:, KSEL:KSEL + 1]
            v.tensor_scalar(gtm, W, last, None, ALU.is_gt)
            v.tensor_scalar(key, W, thr, None, ALU.is_gt)
            link(v.memset(W2, 1.0))
            link(v.tensor_scalar(eqm, W, last, None, ALU.is_equal))
            v.reduce_sum(m8[:, 24:25], gtm, AX)
            link(v.tensor_tensor_scan(pre, W2, eqm, 0.0, ALU.mult, ALU.add))
            link(v.tensor_scalar(m8[:, 25:26], m8[:, 24:25], -1.0, float(KSEL), ALU.mult, ALU.add))
            link(v.scalar_tensor_tensor(eqm, pre, m8[:, 25:26], eqm, ALU.is_le, ALU.mult))
            TT(sel, gtm, eqm, ALU.add)
            v.wait_ge(s["tokload"], 16)
            link(TT(key, key, base, ALU.add))
            link(TT(key, key, sel, ALU.mult))
            top24(key, W2, W3)
            ki = tk[:, 13, 0:KSEL].bitcast(I32)
            kb = tk[:, 13, 32:32 + KSEL].bitcast(I32)
            bit, tok = tk[:, 14, 0:KSEL], tk[:, 14, 32:64]
            link(v.tensor_copy(ki, m8[:, 0:KSEL]))
            link(v.tensor_scalar(kb, ki, 1, None, ALU.bitwise_and))
            v.memset(tok, 0.0)
            v.memset(tk[:, 11, 0:SLOT], SKIP_ROW)
            v.memset(tk[:, 12, 0:SLOT], 0.0)
            link(v.tensor_copy(bit, kb))
            link(TT(tok[:, 0:KSEL], m8[:, 0:KSEL], bit, ALU.subtract))
            v.tensor_scalar(tk[:, 12, 0:KSEL], bit, -1.0, 1.0, ALU.mult, ALU.add)
            link(v.tensor_scalar(tok[:, 0:KSEL], tok[:, 0:KSEL], -0.5, 256.0, ALU.mult, ALU.add))
            v.tensor_scalar(tk[:, 11, 0:KSEL], tok[:, 0:KSEL], cst[0:S, 2:3], None, ALU.add)
            link(v.tensor_scalar(tk[:, 10, 0:SLOT], tok, cst[0:S, 2:3], None, ALU.add))
            v.sem_inc(s["idx"], 1)
            link(TT(dg, tok[:, 0:KSEL].rearrange("p (o i) -> p o i", o=1).to_broadcast([S, S, KSEL]),
                    col1(ident[0:S, 0:S], KSEL), ALU.mult))
            v.sem_inc(s["seldg"], 1)
            v.wait_ge(s["idxp"], 1)
            v.tensor_copy(idxg, psum[:, 1, 0:NQ])
            v.tensor_copy(idxs, psum[:, 1, NQ:2 * NQ])
            link(v.tensor_copy(notm, psum[:, 1, 2 * NQ:3 * NQ]))
            v.sem_inc(s["idxr"], 1)
            v.wait_ge(s["ind"], 1)
            sv = [su[:, x, :].rearrange("p (b n) -> p b n", b=4) for x in range(2)]
            v.tensor_scalar(sv[0], psum[:, 2:6, 0:NC], cst[:, 0:1], None, ALU.is_equal)
            link(v.tensor_scalar(sv[1], psum[:, 2:6, 0:NC], cst[:, 1:2], None, ALU.is_equal))
            v.sem_inc(s["oh"], 1)

            def begin(u):
                v.wait_ge(s["gemm"], use_of[u] + 1)
                return bank(u)

            v.memset(oT.rearrange("p q h b i -> p (q h b i)"), 0.0)
            link(v.memset(qT.rearrange("p h t i -> p (h t i)"), 0.0))

            def routed(g):
                q4 = slice(4 * g, 4 * g + 4)
                for q in range(4 * g, 4 * g + 4):
                    v.wait_ge(s_gath[q], 16)
                    ins = v.bn_stats(st2[:, q, :], h1s[:, q, :])
                link(ins)
                moments(sm[:, q4], sd[:, q4], sq_[:, q4], st2[:, q4, :]).then_inc(s["rvar"], 1)
                v.wait_ge(s["rstd"], g + 1)
                link(v.reciprocal(rr[:, q4], sd[:, q4]))
                v.scalar_tensor_tensor(nb[:, q4], sm[:, q4], -0.5, rr[:, q4], ALU.mult, ALU.mult).then_inc(s["rows"], 1)
                for q in range(4 * g, 4 * g + 4):
                    v.wait_ge(s["g1"], q + 1)
                    ins = v.tensor_tensor_reduce(junk(q), gs[:, q], rwb[:, :], 1.0, 0.0, ALU.mult, ALU.add, wsel[:, q:q + 1])
                    v.scalar_tensor_tensor(h1s[:, q], gs[:, q], notm[:, q:q + 1], h1s[:, q], ALU.mult, ALU.add)
                link(ins)
                v.tensor_scalar(wsel[:, q4], wsel[:, q4], rbias, None, ALU.add)
                v.wait_ge(s["rms1"], g + 1)
                v.reciprocal(r1[:, q4], rms1[:, q4]).then_inc(s["rms1r"], 1)

            def junk(q):
                return vv.rearrange("p b q d -> p (b q) d")[:, q % 8]

            for g in range(SG):
                routed(g)
            for g in range(SG):
                for i in range(2):
                    o = begin(("u", g, i))
                    rows = P if i == 0 else TOK - P
                    v.tensor_copy(su[0:rows, 2 + i, g * NC:(g + 1) * NC], o[0:rows, 0:NC]).then_inc(s["evv"], 1)
            v.wait_ge(s["evv"], emptied[use_of[("mask", 0, 0)] - 4][1])
            v.memset(bank(("mask", 0, 0))[:, 0:NC], 0.0).then_inc(s["mbank"], 1)
            o = begin(("mask", 0, 0))
            v.tensor_copy(msk, o[:, 0:NC].rearrange("p (q k) -> p q k", q=NQ)).then_inc(s["evv"], 1)
            v.wait_ge(s["evv"], emptied[use_of[("mask", 0, 0)]][1])

            def project(g):
                c0 = slice(g * NC, (g + 1) * NC)
                if g >= 1:
                    v.wait_ge(s["sc"], g)
                for h in range(2):
                    for w in ("q", "k"):
                        o = begin((w, g, h))
                        if g == 0 and h == 0 and w == "q":
                            v.wait_ge(s["eva"], emptied[use_of[("cs", SG - 1, 1)]][1])
                        TT(tmp[:, 0], o[:, 0:NC], cs[:, 0, c0], ALU.mult).then_inc(s["evv"], 1)
                        o = begin((w + "r", g, h))
                        TT(tmp[:, 1], o[:, 0:NC], cs[:, 1, c0], ALU.mult).then_inc(s["evv"], 1)
                        v.wait_ge(s["evv"], emptied[use_of[(w + "r", g, h)]][1])
                        t3 = [tmp[:, x].rearrange("p (t i) -> p t i", t=SQ) for x in range(2)]
                        if w == "q":
                            link(TT(qT[:, h, :, 0:KSEL], t3[0], t3[1], ALU.add))
                            v.sem_inc(s["qk"], 1)
                        else:
                            link(TT(tmp[:, 0], tmp[:, 0], tmp[:, 1], ALU.add))
                            v.tensor_scalar(kx[:, h, :, 0, :], t3[0], cst[:, 3:4], None, ALU.mult)
                            link(v.tensor_scalar(kx[:, h, :, 1, :], t3[0], cst[:, 4:5], None, ALU.mult))
                            v.sem_inc(s["qk"], 1)

            def softmax(g):
                v.wait_ge(s["sc"], g + 1)
                if g >= 1:
                    v.wait_ge(s["pv"], g)
                p4 = pr.rearrange("p q r c i -> p (q r c) i")[:, :, 0:KSEL]
                for r in range(4):
                    ins = TT(pr[:, :, r, :, 0:KSEL], psum[:, r, 0:4 * 4 * KSEL].rearrange("p (q c k) -> p q c k", q=4, c=4),
                             msk[:, 4 * g:4 * g + 4, :].rearrange("p q (o k) -> p q o k", o=1).to_broadcast([P, 4, 4, KSEL]),
                             ALU.add)
                link(ins)
                link(v.reduce_max(mx, p4, AX))
                TT(p4, p4, col1(mx, KSEL), ALU.subtract).then_inc(s["pin"], 1)

            def weights(g):
                p4 = pr.rearrange("p q r c i -> p (q r c) i")[:, :, 0:KSEL]
                v.wait_ge(s["pexp"], g + 1)
                link(v.reduce_sum(rinv, p4, AX))
                link(v.reciprocal(rinv, rinv))
                link(TT(p4, p4, col1(rinv, KSEL), ALU.mult))
                v.transpose(prT.rearrange("p q r c i -> p (q r c i)"), pr.rearrange("p q r c i -> p (q r c i)")
                            ).then_inc(s["pt"], 1)

            def heads_out(g):
                v.wait_ge(s["pv"], g + 1)
                if g >= 1:
                    v.wait_ge(s["gemm"], use_of[("o", g - 1, 3)] + 1)
                o8 = oT.rearrange("p q h b i -> p (q h) b i")
                pp = psum[:, 0:4, 0:8 * 34].rearrange("p b (x e i) -> p b x e i", x=8, e=2)
                for b in range(4):
                    ins = v.tensor_scalar(o8[:, :, b, 0:KSEL], pp[:, b, :, 0, :], cst[:, 3:4], None, ALU.mult)
                link(ins)
                for b in range(4):
                    ins = v.scalar_tensor_tensor(o8[:, :, b, 0:KSEL], pp[:, b, :, 1, :], cst[:, 4:5], o8[:, :, b, 0:KSEL],
                                                 ALU.mult, ALU.add)
                ins.then_inc(s["ot"], 1)

            def merge(g):
                for i in range(4):
                    o = begin(("o", g, i))
                    if g >= 2:
                        v.wait_ge(s_scat[g - 2], 64)
                    q = 4 * g + i
                    TT(x1[:, g % 2, i], o[:, 0:D], gs[:, q], ALU.add).then_inc(s["evv"], 1)
                    v.wait_ge(s["evv"], emptied[use_of[("o", g, i)]][1])
                    v.tensor_tensor_reduce(gs[:, q], x1[:, g % 2, i], x1[:, g % 2, i], 1.0, 0.0, ALU.mult, ALU.add,
                                           ssq2[:, q:q + 1]).then_inc(s["ssq2"], 1)

            def rms2_of(g):
                for i in range(4):
                    q = 4 * g + i
                    v.wait_ge(s["rms2"], q + 1)
                    v.reciprocal(rr2[:, q:q + 1], rms2[:, q:q + 1]).then_inc(s["rms2r"], 1)

            def mlp(g):
                rms2_of(g)
                if g == 0:
                    v.wait_ge(s["outd"], 32 * NCH)
                    link(v.memset(yT.rearrange("p h t i -> p (h t i)"), 0.0))
                for h in range(2):
                    o = begin(("y", g, h))
                    if g >= 1:
                        v.wait_ge(s["gemm"], use_of[("yt", g - 1, 3)] + 1)
                    v.tensor_copy(yT[:, h, :, 0:KSEL], o[:, 0:NC].rearrange("p (t i) -> p t i", t=SQ)).then_inc(s["evv"], 1)
                for i in range(4):
                    q = 4 * g + i
                    o = begin(("yt", g, i))
                    x = x1[:, g % 2, i]
                    TT(x, x, o[:, 0:D], ALU.add).then_inc(s["evv"], 1)
                    v.wait_ge(s["evv"], emptied[use_of[("yt", g, i)]][1])
                    v.scalar_tensor_tensor(x, x, wsel[:, q:q + 1], h1s[:, q], ALU.mult, ALU.add).then_inc(s["fin"], 1)

            project(0)
            for g in range(SG):
                softmax(g)
                weights(g)
                if g + 1 < SG:
                    project(g + 1)
                heads_out(g)
                if g >= 1:
                    mlp(g - 1)
                merge(g)
            mlp(SG - 1)

        @block.gpsimd
        def _(pool):
            pool.wait_ge(s["x"], 1)
            for n, c in enumerate(ORDER):
                pool.wait_ge(s["nrm"], n + 1)
                if n >= 2:
                    pool.wait_ge(s["lo"], n - 1)
                for j in range(CH):
                    q = c * CH + j
                    ins = pool.tensor_scalar(t32(n)[:, j, :], h0[:, q, :], vec[:, V_R, q:q + 1], vec[:, V_B, q:q + 1],
                                             ALU.mult, ALU.add)
                ins.then_inc(s["t32"], 1)
                if ORDER[n] == 0:
                    for g in range(2):
                        z = toep[64 * g:64 * g + 64, :, 64 - 64 * g:128 - 64 * g].rearrange("p r t l c -> p r (t l c)")
                        if g == 0:
                            pool.wait_ge(s["t32"], n + 1)
                        else:
                            pool.wait_ge(s["tz"], 1)
                        pool.memset(z, 0.0).then_inc(s["tz"], 1)
                    pool.wait_ge(s["tz"], 2)
            for n in range(1, NGRP, 2):
                pool.wait_ge(s["sil"], n + 1)
                add_group(pool, n).then_inc(s["addp"], 1)
            pool.wait_ge(s["addv"], NGRP // 2)
            pool.wait_ge(s["addp"], NGRP // 2)
            pool.wait_ge(s["conv"], NGRP)
            for c in range(RW_ACT):
                pool.tensor_tensor(hn32[:, c], h0[:, pos_of(c), :], row1(rwb[:, :], CH), ALU.mult).then_inc(s["rwprod"], 1)
            pool.wait_ge(s["tabs"], 1)
            for k in range(2):
                for f in range(2):
                    ins = pool.tensor_copy(tab[:, k, :, f, :].rearrange("p b (h d) -> p b h d", d=HD),
                                           rp[:, 2 + f, k * 64:k * 64 + 64].rearrange("p (b o d) -> p b o d", b=NBB, o=1)
                                           .to_broadcast([P, NBB, 8, HD]))
            ins.then_inc(s["tab"], 1)
            pool.wait_ge(s["wload"], 64)
            k = [0]

            def link(ins):
                k[0] += 1
                ins.then_inc(s["poolw"], 1)
                pool.wait_ge(s["poolw"], k[0])

            for c in range(2):
                pool.tensor_scalar(wsm[:, 0, c], wsm[:, 0, c], lnw[:, c:c + 1], HD ** -0.5, ALU.mult, ALU.mult)
                pool.tensor_scalar(wsm[:, 1, c], wsm[:, 1, c], lnw[:, c:c + 1], None, ALU.mult)
                ins = pool.tensor_scalar(wsm[:, 4, c], wsm[:, 4, c], lnw[:, c:c + 1], None, ALU.mult)
            link(ins)
            for w in range(2):
                src = wsm[:, w].rearrange("p c (h e d) -> p (c h) e d", e=2, d=HD // 2)
                dst = wsm[:, 2 + w].rearrange("p c (h e d) -> p (c h) e d", e=2, d=HD // 2)
                pool.tensor_scalar(dst[:, :, 0, :], src[:, :, 1, :], -1.0, None, ALU.mult)
                ins = pool.tensor_copy(dst[:, :, 1, :], src[:, :, 0, :])
            link(ins)
            pool.sem_inc(s["wready"], 1)
            pool.wait_ge(s["h1out"], 64)
            pool.wait_ge(s["idxr"], 1)
            for q in range(NQ):
                pool.indirect_dma_start(h1s[:, q, :], None, h1_rows, bass.IndirectOffsetOnAxis(ap=idxg[:, q:q + 1], axis=0),
                                        bounds_check=S * TOK - 1, oob_is_err=False).then_inc(s_gath[q], 16)
            for c in range(NCH):
                for j in range(CH):
                    q = c * CH + j
                    ins = pool.tensor_scalar(h0[:, q, :], h0[:, q, :], vec[:, V_A, q:q + 1], vec[:, V_B, q:q + 1],
                                             ALU.mult, ALU.add)
                ins.then_inc(s["outc"], 1)
            pool.wait_ge(s["w1load"], 32)
            for c in range(2):
                ins = pool.tensor_scalar(w1[:, c], w1[:, c], lnw[:, 2 + c:3 + c], None, ALU.mult)
            link(ins)
            pool.sem_inc(s["wready"], 1)
            pool.wait_ge(s["outd"], 32 * NCH)
            for q in range(NQ):
                pool.wait_ge(s["fin"], q + 1)
                pool.indirect_dma_start(out.rearrange("s t d -> (s t) d"), bass.IndirectOffsetOnAxis(ap=idxs[:, q:q + 1], axis=0),
                                        x1[:, q // 4 % 2, q % 4, :], None, bounds_check=S * TOK - 1, oob_is_err=False
                                        ).then_inc(s_scat[q // 4], 16)
            for g in range(SG):
                pool.wait_ge(s_scat[g], 64)


def _constants():
    m = np.arange(FR)
    half = np.pi * m / S
    out = {}
    own = np.zeros((P, HG), np.float32)
    own[np.arange(P), np.arange(P) % HG] = 1
    wave = np.concatenate([np.cos(half), 2 * np.sin(half)]).astype(np.float32)
    wave[FR - 1] = 0.0
    out["s4c"] = np.concatenate([np.broadcast_to(wave, (P, 2 * FR)), own], axis=1)
    phase = 2 * np.pi * m[:, None] * (np.arange(S) + 0.5) / S
    wgt = (np.where((m == 0) | (m == FR - 1), 1, 2) / S)[:, None]
    out["dft"] = np.concatenate([wgt * np.cos(phase), -wgt * np.sin(phase), wave[:FR, None]], axis=1)
    out["ident"] = np.eye(P)
    cst = np.zeros((P, 5))
    cst[:, 0] = np.arange(P)
    cst[:, 1] = np.arange(P) + P
    cst[:S, 2] = TOK * np.arange(S)
    cst[:, 3] = np.arange(P) % 32 < HD
    cst[:, 4] = np.arange(P) % 32 >= HD
    out["cst"] = cst
    pick = np.zeros((S, 2 * S), np.float32)
    pick[S - 1 - np.arange(S), np.arange(S)] = 1
    out["base"] = np.broadcast_to(2.0 * (256 - np.arange(TOK)), (S, TOK))
    inv = 1.0 / np.float32(10000.0) ** (np.arange(0, HD, 2, dtype=np.float32) / np.float32(HD))
    out["invf"] = np.broadcast_to(np.concatenate([inv, inv]), (P, HD))
    return {"pick": pick.astype(np.float16)} | {k: np.ascontiguousarray(x, dtype=np.float32) for k, x in out.items()}


def _lay_out(i):
    i = {k: np.asarray(v) for k, v in i.items()}
    h = {}

    def states(x):
        return x.reshape(HF, HG, 16).transpose(2, 1, 0).reshape(P, HF)

    h["s4in"] = np.stack([states(np.broadcast_to(i["L0_attn_log_dt"], (D, 16))), states(i["L0_attn_inv_w_real"]),
                          states(i["L0_attn_w_imaginary"])]
                         + [states(i["L0_attn_" + n].reshape(D, 16, 2)[..., x]) for n in "BPC" for x in range(2)], axis=1)
    x = i["x"].reshape(S, 3, 4, 16, 4, 16).transpose(1, 3, 5, 2, 4, 0)
    h["img"] = x.reshape(KC, P, 2, CH, S).transpose(1, 0, 3, 2, 4).reshape(P, KC, CH, P)
    h["wT"] = i["L0_tok_W"].T.reshape(KC, P, D).transpose(1, 0, 2)
    lag0 = np.zeros((1, S), np.float32)
    lag0[0, 0] = 1
    h["drow"] = np.concatenate([i["L0_attn_D"].reshape(1, D), lag0, np.ones((1, P), np.float32)], axis=1)
    h["lnw"] = np.concatenate([i["L0_ffn_ln1"].reshape(2, P).T, i["L0_ffn_ln2"].reshape(2, P).T], axis=1)
    pos = np.zeros((2 * P, NBB), i["L0_ffn_position_ids"].dtype)
    pos[:TOK] = i["L0_ffn_position_ids"][:, :TOK].T
    h["posT"] = pos.reshape(2, P, NBB).transpose(1, 0, 2).reshape(P, 2 * NBB)
    h["mask"] = i["L0_ffn_attention_mask"][:, 0, :TOK, :TOK]
    for name, src in (("txt", "txt"), ("b", "L0_tok_b"), ("pos_emb", "L0_tok_pos_emb"), ("rw", "L0_ffn_router_w"),
                      ("rb", "L0_ffn_router_b"), ("wq", "L0_ffn_wq"), ("wk", "L0_ffn_wk"), ("wv", "L0_ffn_wv"),
                      ("wo", "L0_ffn_wo"), ("w1", "L0_ffn_w1"), ("w2", "L0_ffn_w2")):
        h[name] = i[src]
    return {k: np.ascontiguousarray(x) for k, x in h.items()}


def program(nc, arrays):
    args = {n: nc.dram_tensor("in_" + n, x.shape, mybir.dt.from_np(x.dtype), kind="ExternalInput").ap()
            for n, x in arrays.items()}
    out = nc.dram_tensor("out_rows", (S, TOK, D), F32, kind="ExternalOutput").ap()
    build(nc, args, out)


def kernel(**inputs):
    import concourse.bacc as bacc
    from concourse.bass_utils import run_bass_kernel_spmd as run

    arrays = {**_lay_out(inputs), **_constants()}
    nc = bacc.Bacc("TRN2", target_bir_lowering=False, num_devices=1)
    program(nc, arrays)
    r = run(nc, [{"in_" + n: x for n, x in arrays.items()}], core_ids=[0])
    return r.results[0]["out_rows"]
```

```python
from contextlib import ExitStack

import numpy as np

import concourse.bass as bass
from concourse import mybir

F32 = mybir.dt.float32
F16 = mybir.dt.float16
BF16 = mybir.dt.bfloat16
I32 = mybir.dt.int32
U32 = mybir.dt.uint32
ALU = mybir.AluOpType
ACT = mybir.ActivationFunctionType
AX = mybir.AxisListType.X

P = 128
S = 64
TOK = 144
D = 256
POS = TOK // 2
CH = 8
NCH = POS // CH
KC = 768 // P
FR = S // 2 + 1
HG = 8
HF = D // HG
TCH = 16
NT = D // TCH
TRING = 3
UCH = 64
NU = D // UCH
QT = 4
NB = S // QT
GRP = 8
NGRP = D // GRP
CSLOT = 2
SIL = 3
KSEL = int(0.125 * TOK) - 1
SLOT = 32
HD = 16
HALF_TURN = [16 * (j // 16) + (j + 8) % 16 for j in range(32)]
HP = P // HD
FF = 1024
FC = FF // P
SG = 4
SQ = S // SG
NC = SQ * KSEL
NQ = S // 4
NBB = 4
LN_EPS = 1e-5
RMS_EPS = 1e-6
T_PEAK = 1024.0
X_GAIN = 64.0
NEG = -3.0e38
SKIP_ROW = 30000.0
RW_ACT = 5
PI_LOW = 3.1415925
TWO_PI = (6.28125, 0.0019350051879882812, float(2 * np.pi - 6.28125 - 0.0019350051879882812))

ORDER = [1, 2, 3, 0, 4, 5, 6, 7, 8]


def gemm_plan():
    plan = [("cs", s, i) for s in range(SG) for i in range(2)]

    def project(s):
        return ([("xt", s, i) for i in range(4)] + [(w, s, h) for h in range(2) for w in ("q", "k")]
                + [("v", s, i) for i in range(4)])

    def hidden(s):
        return [("x2t", s, i) for i in range(4)] + [("h", s, i) for i in range(FC)]

    def outer(s):
        return [("y", s, i) for i in range(2)] + [("yt", s, i) for i in range(4)]

    plan += project(0) + [("u", s, i) for s in range(SG) for i in range(2)] + [("mask", 0, 0)]
    for s in range(SG):
        if s + 1 < SG:
            plan += project(s + 1)
        if s >= 1:
            plan += hidden(s - 1) + outer(s - 1)
        plan += [("o", s, i) for i in range(4)]
    return plan + hidden(SG - 1) + outer(SG - 1)


BY_ACT = ("cs", "xt", "v", "x2t", "h")


def build(nc, a, out):
    with ExitStack() as ctx:
        def sb(name, shape, dt=F32):
            return ctx.enter_context(nc.sbuf_tensor(name, shape, dt))

        def sem(name):
            return ctx.enter_context(nc.semaphore(name))

        ctx.enter_context(nc.allow_non_contiguous_dma(reason="short rows of the kernel and of constants"))

        h1_rows = nc.dram_tensor("h1_rows", [S * TOK, D], F32, kind="Internal").ap()

        h0 = sb("h0", [P, POS, D])
        work = sb("work", [P, 24576])
        wbuf = sb("wbuf", [P, 20 * D])
        wsm = wbuf[:, 0:12 * D].rearrange("p (w c d) -> p w c d", w=6, c=2)
        w2 = wbuf[:, 12 * D:20 * D].rearrange("p (f d) -> p f d", f=FC)
        w1 = sb("w1", [P, 2, FF])
        ident = sb("ident", [P, P])
        st = sb("st", [P, POS, 6])
        vec = sb("vec", [P, 8, POS])
        small = sb("small", [P, 224])
        s4in = sb("s4in", [P, 9, HF])
        s4v = sb("s4v", [P, 14, HF])
        s4c = sb("s4c", [P, 2 * FR + HG])
        dft = sb("dft", [FR, 2 * S + 1])
        drow_full = sb("drow", [P, D + S + P])
        drow = drow_full[0:1]
        rwb = sb("rwb", [P, D])
        w1f = w1[:, :, :].rearrange("p a b -> p (a b)")
        V_S, V_D, V_Q, V_W, V_R, V_B, V_A, V_Z = range(8)

        wf = work[:, :]
        hn = wf[:, 0:18432].bitcast(F16).rearrange("p (c l j d) -> p c l j d", c=NCH, l=2, j=CH)
        hn32 = wf[:, 0:18432].rearrange("p (c j d) -> p c j d", c=NCH, j=CH)
        toep = wf[:, 18432:24576].bitcast(F16).rearrange("p (r t l c) -> p r t l c", r=TRING, t=P, l=2)
        stage = wbuf[:, 0:16 * D].bitcast(F16).rearrange("p (b x c) -> p b x c", b=UCH // TCH, c=TCH)
        img = wf[:, 18432:24576].rearrange("p (k n q) -> p k n q", k=KC, n=CH)
        wT = wsm[:, 0:3].rearrange("p a b d -> p (a b d)").rearrange("p (k d) -> p k d", k=KC)
        brow = wsm[:, 3, 0]
        posb = w2
        t32_even = w1f.rearrange("p (j d) -> p j d", j=CH)

        def sil(n):
            return w1f[:, (n % SIL) * GRP * POS:(n % SIL + 1) * GRP * POS]

        late = h0[:, 5 * CH:POS].rearrange("p j d -> p (j d)")
        rhsA = late[:, 0:2048].rearrange("p (f c e) -> p f c e", f=HF, c=8)
        rhsB = late[:, 2048:4096].rearrange("p (f c e) -> p f c e", f=HF, c=8)
        NE = HF * FR
        er, ei, iv = (late[:, 4096 + i * NE:4096 + (i + 1) * NE].rearrange("p (f m) -> p f m", m=FR) for i in range(3))
        t1 = w1f[:, 0:NE].rearrange("p (f m) -> p f m", m=FR)
        qs = late[0:FR, 0:2048].rearrange("p (f c e) -> p c f e", f=HF, c=8)
        gt = late[0:FR, 2048:4096].rearrange("p (c f e) -> p c f e", c=8, f=HF)
        ksb = late[0:S, 4096:4352]
        kneg = late[0:S, 4352:4608]
        kp = s4in[0:S].rearrange("p a b -> p (a b)")[:, 0:D].bitcast(F16).rearrange("p (l c) -> p l c", l=2)
        pick = vec[0:S, V_Z, 0:S].bitcast(F16)

        h1s = wf[:, 0:4096].rearrange("p (q d) -> p q d", q=NQ)
        gs = wf[:, 4096:8192].rearrange("p (q d) -> p q d", q=NQ)
        xT = wf[:, 8192:9216].rearrange("p (c n) -> p c n", c=2)
        diag1 = wf[:, 9216:9728].rearrange("p (b d) -> p b d", b=4)
        diag2 = wf[:, 9728:10240].rearrange("p (b d) -> p b d", b=4)
        tab = wf[:, 8192:10240].rearrange("p (k b f n) -> p k b f n", k=2, b=NBB, f=2)
        qT = wf[:, 10240:11264].rearrange("p (h t i) -> p h t i", h=2, t=SQ)
        kT = wf[:, 11264:11808].rearrange("p (h t i) -> p h t i", h=2, t=SQ)
        tmp = wf[:, 12352:12896].rearrange("p (b n) -> p b n", b=2)
        cs = wf[:, 12896:15072].rearrange("p (f n) -> p f n", f=2)
        su = wf[:, 15072:19424].rearrange("p (x n) -> p x n", x=4)
        pr = wf[:, 15072:17120].rearrange("p (q c i) -> p q c i", q=4, c=2 * HP)
        prT = wf[:, 17120:19168].rearrange("p (q c i) -> p q c i", q=4, c=2 * HP)
        vv = wf[:, 19424:21472].rearrange("p (b q d) -> p b q d", b=2, q=4)
        oT = wf[:, 21472:22496].rearrange("p (q h b i) -> p q h b i", q=4, h=2, b=4)
        x1 = wf[:, 22496:24544].rearrange("p (b q d) -> p b q d", b=2, q=4)
        am = wf[:, 22496:23648].rearrange("p (k b n) -> p k b n", k=2, b=NBB)
        tk = wf[0:S, 4096:8192].rearrange("p (x n) -> p x n", n=256)
        rp = wbuf[:, 16 * D:18 * D].rearrange("p (x n) -> p x n", n=P)
        dg = wf[0:S, 19424:19968].bitcast(BF16).rearrange("p (t i) -> p t i", t=S)
        ones_b = wf[0:S, 19968:20032].bitcast(BF16)
        hT = h0[:, 0:9].rearrange("p j d -> p (j d)")[:, 0:FC * NC].rearrange("p (f n) -> p f n", f=FC)
        yT = h0[:, 12:16].rearrange("p j d -> p (j d)").rearrange("p (h t i) -> p h t i", h=2, t=SQ)
        x2T = h0[:, 16:20].rearrange("p j d -> p (j d)").rearrange("p (c n) -> p c n", c=2)
        kx_first = wf[:, 15072:19424].rearrange("p (h t e i) -> p h t e i", h=2, t=SQ, e=HP)
        kx_later = h0[:, 24:41].rearrange("p j d -> p (j d)").rearrange("p (h t e i) -> p h t e i", h=2, t=SQ, e=HP)
        msk = s4in[:, :, :].rearrange("p a b -> p (a b)")[:, 0:NQ * KSEL].rearrange("p (q k) -> p q k", q=NQ)

        cols = {}

        def col(name, n=1):
            if name not in cols:
                cols[name] = sum(w for _, w in cols.values()), n
            o, w = cols[name]
            assert o + w <= 32
            return small[:, o:o + w]

        eps_ln, eps_rms, amax, kscale, yscale, am64, am1 = (
            col(x) for x in ("eps_ln", "eps_rms", "amax", "kscale", "yscale", "am64", "am1"))
        cst = col("cst", 5)
        own_head = col("own_head", HP)
        rbias = col("rbias")
        lnw = col("lnw", 4)
        srw = col("srw")
        idxg = small[:, 32:48].bitcast(U32)
        idxs = small[:, 48:64].bitcast(U32)
        notm = small[:, 64:80]
        wsel = small[:, 80:96]
        r1 = small[:, 96:112]
        sm, sd, sq_, rr, nb = (small[:, 112 + 16 * i:128 + 16 * i] for i in range(5))
        st_first = s4v[:, :, :].rearrange("p a b -> p (a b)")[:, 0:POS * 6].rearrange("p (q x) -> p q x", x=6)
        rinv = s4v[:, 0:2, :].rearrange("p a b -> p (a b)")
        mx = s4v[:, 2:4, :].rearrange("p a b -> p (a b)")
        st2 = s4v[:, 4:7, :].rearrange("p a b -> p (a b)").rearrange("p (q x) -> p q x", x=6)
        ssq = s4v[:, 7, 0:16]
        ssq2 = s4v[:, 7, 16:32]
        rms1 = s4v[:, 9, 0:16]
        rms2 = s4v[:, 8, 0:16]
        rr2 = s4v[:, 8, 16:32]
        posi = small[:, 192:200].bitcast(I32)
        invf = small[:, 200:216]
        base = s4in[0:S].rearrange("p a b -> p (a b)")[:, 0:TOK]
        c_c, c_s, c_e = s4c[:, 0:FR], s4c[:, FR:2 * FR], s4c[:, 2 * FR:]

        psum = ctx.enter_context(nc.psum_tensor("psum", [P, 8, 512], F32))

        names = """const s4in rope img pos khl act_s4 dve x rhs q g k am amt amb emb embv var std nrm t32 hi lo
            tz rwprod rwdot conv built tba tbv sil addv addp wload w1load wready mload var3 std3 rows w72 wmov idx idxp idxr ind seldg oh
            tabf tabs tab tokload rvar rstd g1 ssq rms1 rms1r gemm evv eva qk keys kx ownf own sc pin pexp pt pv ot x1 ssq2 rms2 rms2r
            hrow h2row fin outc outd mbank h1out poolw""".split()
        s = {n: sem("s_" + n) for n in names}
        s_txt = [sem(f"s_txt{c}") for c in range(NCH)]
        s_scat = [sem(f"s_scat{g}") for g in range(SG)]
        s_gath = [sem(f"s_gath{q}") for q in range(NQ)]

        plan = gemm_plan()
        use_of = {u: n for n, u in enumerate(plan)}
        emptied = []
        for n, (what, _, _) in enumerate(plan):
            by = what in BY_ACT
            emptied.append((by, 1 + sum(1 for b, _ in emptied if b == by)))

        s_toep = [sem(f"s_toep{r}") for r in range(TRING)]
        toep_emptied = []
        for m in range(NU * NB):
            by = "tbv" if (m % 6 == 5 if m < 2 * NB else m % 2) else "tba"
            toep_emptied.append((by, 1 + sum(1 for b, _ in toep_emptied if b == by)))

        def later_builds(n):
            m = 2 * NB + 2 * (n - 4)
            return (m, m + 1) if 2 * NB <= m < NU * NB else ()

        def early_builds(n, by):
            return [m for m in range(max(0, 6 * (n - 3)), min(6 * (n - 2), 2 * NB)) if toep_emptied[m][0] == by]

        def unit_kept(eng, u):
            for by in ("tba", "tbv"):
                count = max([c for b, c in toep_emptied[:(u + 1) * NB] if b == by] + [0])
                if count:
                    eng.wait_ge(s[by], count)

        def placed(eng, n):
            eng.wait_ge(s_toep[n % TRING], 32 * (n // TRING + 1))

        def keep_toep(eng, copy, m):
            u, k = divmod(m, NB)
            if u >= 2 and k < 2:
                for n in range(4 * (u - 2) + 1, 4 * (u - 2) + 4):
                    placed(eng, n)
            eng.wait_ge(s["built"], m + 1)
            h = slice(64 * (u % 2), 64 * (u % 2) + 64)
            copy(stage[h, :, k * 2 * QT:(k + 1) * 2 * QT, :].rearrange("p b x c -> p x b c"),
                 psum[h, 4 + m % 4, :].rearrange("p (x b c) -> p x b c", b=UCH // TCH, c=TCH)).then_inc(s[toep_emptied[m][0]], 1)

        def bank(u):
            return psum[:, 4 + use_of[u] % 4, :]

        def embedded(j):
            b = j // 2 if j < 4 else 2 + j // 2
            return psum[:, b, j % 2 * D:j % 2 * D + D]

        def pos_of(c):
            return slice(c * CH, c * CH + CH)

        def t32(n):
            return t32_even if n % 2 == 0 else hn32[:, ORDER[-1]]

        junk_a = drow_full[:, 0:D]
        junk_v = st[:, :, :].rearrange("p a b -> p (a b)")[:, 0:D]

        def spread(eng, scaled, g, h):
            kx = kx_later if g else kx_first
            for e in range(HP):
                ins = scaled(kx[:, h, :, e, :], kT[:, h], own_head[:, e:e + 1])
            return ins

        def row1(x, n):
            return x.rearrange("p (o d) -> p o d", o=1).to_broadcast([x.shape[0], n, x.shape[1]])

        def col1(x, n):
            return x.rearrange("p (f o) -> p f o", o=1).to_broadcast([x.shape[0], x.shape[1], n])

        def add_group(eng, n):
            x = h0[:, :, n * GRP:(n + 1) * GRP]
            return eng.tensor_tensor(x, x, sil(n).rearrange("p (c j) -> p j c", c=GRP), ALU.add)

        block = ctx.enter_context(nc.Block())

        @block.sync
        def _(sp):
            sp.dma_start(s4in[:, :, :], a["s4in"]).then_inc(s["s4in"], 16)
            sp.dma_start(s4c[:, :], a["s4c"]).then_inc(s["s4in"], 16)
            for dst, name in ((dft[:, :], "dft"), (drow[:, :], "drow"), (ident[:, :], "ident"), (cst, "cst"), (lnw, "lnw"), (own_head, "own_head"),
                              (pick, "pick")):
                sp.dma_start(dst, a[name]).then_inc(s["const"], 16)
            sp.dma_start(rwb[:, :], a["rw"].rearrange("d o -> o d").to_broadcast([P, D])).then_inc(s["const"], 16)

            sp.dma_start(rbias, a["rb"].rearrange("(o d) -> o d", o=1).to_broadcast([P, 1])).then_inc(s["const"], 16)
            sp.dma_start(posi, a["posT"]).then_inc(s["rope"], 16)
            sp.dma_start(invf, a["invf"]).then_inc(s["rope"], 16)

            def text(c):
                for g in range(2):
                    lo = (c - 1) * CH + 64 * g
                    sp.dma_start(h0[64 * g:64 * g + 64, pos_of(c), :], a["txt"][:, lo:lo + CH, :]).then_inc(s_txt[c], 16)

            text(1)
            sp.dma_start(wT, a["wT"]).then_inc(s["img"], 16)
            sp.dma_start(img, a["img"]).then_inc(s["img"], 16)
            for g in range(2):
                sp.dma_start(posb[64 * g:64 * g + 64, :, :],
                             a["pos_emb"][g * 8:g * 8 + 8, :].rearrange("(o n) d -> o n d", o=1).to_broadcast([64, 8, D])
                             ).then_inc(s["pos"], 16)
            sp.dma_start(brow, a["b"].rearrange("(o d) -> o d", o=1).to_broadcast([P, D])).then_inc(s["pos"], 16)
            for c in range(2, 5):
                text(c)
            sp.wait_ge(s["khl"], 1)
            for c in range(5, 9):
                text(c)
            sp.wait_ge(s["tz"], 2)
            for n in range(NT):
                u, k = divmod(n, UCH // TCH)
                if k == 0:
                    unit_kept(sp, u)
                if n >= TRING:
                    sp.wait_ge(s["conv"], TCH // GRP * (n - TRING + 1))
                for g in range(2):
                    h = slice(64 * (u % 2), 64 * (u % 2) + 64)
                    sp.dma_start(toep[64 * g:64 * g + 64, n % TRING, 64 * g:64 * g + 64],
                                 stage[h, k].rearrange("p (t l) c -> p t l c", l=2)).then_inc(s_toep[n % TRING], 16)
            rows = h1_rows.rearrange("(s t) d -> s t d", t=TOK)
            for half in range(2):
                d = slice(half * D // 2, (half + 1) * D // 2)
                sp.wait_ge(s["addv"], NGRP // 4 * (half + 1))
                sp.wait_ge(s["addp"], NGRP // 4 * (half + 1))
                for g in range(2):
                    h = slice(64 * g, 64 * g + 64)
                    sp.dma_start(rows[:, 8 * g:8 * g + 8, d], h0[h, 0:8, d]).then_inc(s["h1out"], 16)
                    sp.dma_start(rows[:, 16 + 64 * g:80 + 64 * g, d], h0[h, 8:POS, d]).then_inc(s["h1out"], 16)
                if half == 0:
                    for n in range(NT - TRING, NT):
                        placed(sp, n)
                    for i, w in ((0, "wq"), (1, "wk"), (4, "wv"), (5, "wo")):
                        sp.dma_start(wsm[:, i], a[w].rearrange("(c p) d -> p c d", p=P)).then_inc(s["wload"], 16)
                    sp.wait_ge(s["built"], NU * NB)
                    sp.dma_start(base, a["base"]).then_inc(s["tokload"], 16)
            sp.wait_ge(s["tab"], 1)
            sp.dma_start(w2, a["w2"].rearrange("(c p) d -> p c d", p=P)).then_inc(s["w1load"], 16)
            sp.dma_start(w1[:, :, :], a["w1"].rearrange("(c p) f -> p c f", p=P)).then_inc(s["w1load"], 16)
            sp.dma_start(am[:, 0], a["mask"][:, 0:P, :].rearrange("b j n -> j b n")).then_inc(s["mload"], 16)
            sp.dma_start(am[0:TOK - P, 1], a["mask"][:, P:TOK, :].rearrange("b j n -> j b n")).then_inc(s["mload"], 16)
            for c in range(NCH):
                sp.wait_ge(s["outc"], c + 1)
                for g in range(2):
                    lo = 8 * g if c == 0 else 16 + 64 * g + (c - 1) * CH
                    sp.dma_start(out[:, lo:lo + CH, :], h0[64 * g:64 * g + 64, pos_of(c), :]).then_inc(s["outd"], 16)
            sp.wait_ge(s["outd"], 32 * NCH)

        @block.tensor
        def _(pe):
            mm = pe.matmul
            pe.wait_ge(s["x"], 1)
            pe.wait_ge(s["rhs"], 1)
            for f in range(HF):
                o = psum[0:FR, 4 + f // 8, (f % 8) * 64:(f % 8) * 64 + 64]
                mm(o, er[:, f, :], rhsA[:, f].rearrange("p c e -> p (c e)"), start=True, stop=False)
                ins = mm(o, ei[:, f, :], rhsB[:, f].rearrange("p c e -> p (c e)"), start=False, stop=True)
            ins.then_inc(s["q"], 1)

            def embed(j):
                for k in range(KC):
                    ins = mm(embedded(j), img[:, k, j, :], wT[:, k, :], start=(k == 0), stop=(k == KC - 1))
                if j % 2:
                    ins.then_inc(s["emb"], 1)

            pe.wait_ge(s["img"], 32)
            for j in range(4):
                embed(j)
            pe.wait_ge(s["const"], 144)
            pe.wait_ge(s["g"], 1)
            mm(psum[0:S, 2, 0:D], dft[:, 0:S], gt[:, 0].rearrange("p f e -> p (f e)"), start=True, stop=False)
            mm(psum[0:S, 2, 0:D], dft[:, S:2 * S], gt[:, 2].rearrange("p f e -> p (f e)"), start=False, stop=False)
            mm(psum[0:S, 2, 0:D], drow[:, D:D + S], drow[:, 0:D], start=False, stop=True).then_inc(s["k"], 1)
            pe.wait_ge(s["am"], 1)
            pe.transpose(psum[0:1, 3, 0:S], am64[0:S], ident[0:S, 0:S]).then_inc(s["amt"], 1)
            pe.wait_ge(s["am"], 2)
            mm(psum[:, 3, 128:129], drow[:, D + S:], am1[0:1], start=True, stop=True).then_inc(s["amt"], 1)
            for j in range(4, CH):
                embed(j)
            pe.wait_ge(s["khl"], 1)

            def build(m):
                if m >= 4:
                    by, count = toep_emptied[m - 4]
                    pe.wait_ge(s[by], count)
                elif m == 0:
                    pe.wait_ge(s["embv"], CH // 2)
                u, k = divmod(m, NB)
                for i in range(QT):
                    t = k * QT + i
                    ins = mm(psum[64 * (u % 2):64 * (u % 2) + 64, 4 + m % 4, i * 2 * UCH:(i + 1) * 2 * UCH],
                             pick[:, S - 1 - t:2 * S - 1 - t], kp[:, :, u * UCH:(u + 1) * UCH], start=True, stop=True)
                ins.then_inc(s["built"], 1)

            for m in range(2 * NB):
                build(m)
            pe.wait_ge(s["hi"], NCH)
            pe.wait_ge(s["lo"], NCH)
            pe.wait_ge(s["amb"], 1)
            for n in range(NGRP):
                e, r = divmod(n, TCH // GRP)
                if r == 0:
                    placed(pe, e)
                if n >= CSLOT:
                    pe.wait_ge(s["sil"], n - CSLOT + 1)
                for i in range(GRP):
                    ch = n * GRP + i
                    o = psum[:, 2 * (n % CSLOT) + i // 4, (i % 4) * POS:(i % 4 + 1) * POS]
                    t_hi, t_lo = (toep[:, e % TRING, :, l, ch % TCH] for l in range(2))
                    x_hi, x_lo = (hn[:, :, l, :, ch] for l in range(2))
                    mm(o, t_hi, x_hi, start=True, stop=False)
                    mm(o, t_hi, x_lo, start=False, stop=False)
                    ins = mm(o, t_lo, x_hi, start=False, stop=True)
                ins.then_inc(s["conv"], 1)
                for m in later_builds(n):
                    build(m)
            pe.wait_ge(s["w72"], 1)
            pe.wait_ge(s["sil"], NGRP)
            for g in range(2):
                ins = mm(psum[0:S, 0, g * POS:(g + 1) * POS], ident[:, 64 * g:64 * g + 64], vec[:, V_W, :], start=True, stop=True)
            ins.then_inc(s["wmov"], 1)
            pe.wait_ge(s["idx"], 1)
            for x in range(3):
                for b in range(4):
                    ins = mm(psum[32 * b:32 * b + 32, 1, x * NQ:(x + 1) * NQ], tk[:, 10 + x, 0:SLOT], ident[0:S, b:S:4],
                             start=True, stop=True)
            ins.then_inc(s["idxp"], 1)
            pe.wait_ge(s["seldg"], 1)
            for b in range(4):
                ins = mm(psum[:, 2 + b, 0:NC], ones_b,
                         dg[:, SQ * b:SQ * b + SQ, :].rearrange("p t i -> p (t i)"), start=True, stop=True)
            ins.then_inc(s["ind"], 1)

            def begin(u):
                n = use_of[u]
                if n >= 4:
                    by, count = emptied[n - 4]
                    pe.wait_ge(s["eva"] if by else s["evv"], count)
                return bank(u)

            pe.wait_ge(s["oh"], 1)
            pe.wait_ge(s["tab"], 1)
            parts = [(bb * KSEL, (bb + 1) * KSEL, bb) for bb in range(NBB - 1)]
            for g in range(SG):
                for i in range(2):
                    o = begin(("cs", g, i))
                    for lo, hi, bb in (parts + [(3 * KSEL, NC, 3)] if g == 0 else [(0, NC, 3)]):
                        c = slice(g * NC + lo, g * NC + hi)
                        mm(o[:, lo:hi], tab[:, 0, bb, i, :], su[:, 0, c], start=True, stop=False)
                        ins = mm(o[:, lo:hi], tab[0:16, 1, bb, i, :], su[0:16, 1, c], start=False, stop=True)
                    ins.then_inc(s["gemm"], 1)

            def masks():
                pe.wait_ge(s["mload"], 32)
                for g in range(SG):
                    for i in range(2):
                        o = begin(("u", g, i))
                        rows = P if i == 0 else TOK - P
                        for lo, hi, bb in (parts + [(3 * KSEL, NC, 3)] if g == 0 else [(0, NC, 3)]):
                            c = slice(g * NC + lo, g * NC + hi)
                            mm(o[0:rows, lo:hi], am[:, 0, bb, P * i:P * i + rows], su[:, 0, c], start=True, stop=False)
                            ins = mm(o[0:rows, lo:hi], am[0:16, 1, bb, P * i:P * i + rows], su[0:16, 1, c], start=False, stop=True)
                        ins.then_inc(s["gemm"], 1)
                o = begin(("mask", 0, 0))
                pe.wait_ge(s["mbank"], 1)
                pe.wait_ge(s["evv"], emptied[use_of[("u", SG - 1, 1)]][1])
                for t in range(S):
                    c = slice(t * KSEL, (t + 1) * KSEL)
                    b, q = t % 4, t // 4
                    mm(o[32 * b:32 * b + KSEL, q * KSEL:(q + 1) * KSEL], su[:, 2, c], su[:, 0, c], start=True, stop=False)
                    ins = mm(o[32 * b:32 * b + KSEL, q * KSEL:(q + 1) * KSEL], su[0:16, 3, c], su[0:16, 1, c], start=False, stop=True)
                ins.then_inc(s["gemm"], 1)

            def project(g):
                for i in range(4):
                    o = begin(("xt", g, i))
                    pe.wait_ge(s["hrow"], 4 * g + i + 1)
                    for c in range(2):
                        ins = mm(o[:, c * P:(c + 1) * P], gs[:, 4 * g + i, c * P:(c + 1) * P], diag1[:, i], start=True, stop=True)
                    ins.then_inc(s["gemm"], 1)
                pe.wait_ge(s["eva"], emptied[use_of[("xt", g, 3)]][1])
                if g == 0:
                    pe.wait_ge(s["wready"], 1)
                for h in range(2):
                    for w, name in ((0, "q"), (1, "k")):
                        o = begin((name, g, h))
                        for c in range(2):
                            x = xT[:, c, :].rearrange("p (t i) -> p t i", i=SLOT)[:, :, 0:KSEL]
                            ins = mm(o[:, 0:NC], wsm[:, w, c, h * P:(h + 1) * P], x, start=(c == 0), stop=(c == 1))
                        ins.then_inc(s["gemm"], 1)
                for i in range(4):
                    o = begin(("v", g, i))
                    for c in range(2):
                        ins = mm(o[:, 0:D], xT[:, c, i * P:(i + 1) * P], wsm[:, 4, c, :], start=(c == 0), stop=(c == 1))
                    ins.then_inc(s["gemm"], 1)

            def scores(g):
                pe.wait_ge(s["qk"], 2 * (g + 1))
                pe.wait_ge(s["kx"], 2 * (g + 1))
                kx = kx_later if g else kx_first
                if g >= 1:
                    pe.wait_ge(s["ot"], g)
                for q in range(4):
                    for h in range(2):
                        for b in range(4):
                            t = 4 * q + b
                            ins = mm(psum[32 * b:32 * b + 32, q, h * HP * KSEL:(h + 1) * HP * KSEL], qT[:, h, t, :],
                                     kx[:, h, t].rearrange("p e i -> p (e i)"), start=True, stop=True)
                ins.then_inc(s["sc"], 1)

            def attend(g):
                pe.wait_ge(s["pt"], g + 1)
                pe.wait_ge(s["eva"], emptied[use_of[("v", g, 3)]][1])
                for q in range(4):
                    for h in range(2):
                        for b in range(4):
                            for r in range(4):
                                ins = mm(psum[32 * r:32 * r + 32, b, (2 * q + h) * 34:(2 * q + h) * 34 + 34],
                                         vv[32 * b:32 * b + KSEL, g % 2, q, h * P + 32 * r:h * P + 32 * r + 32],
                                         prT[32 * b:32 * b + KSEL, q, HP * h + 2 * r:HP * h + 2 * r + 2, 0:KSEL], start=True, stop=True)
                ins.then_inc(s["pv"], 1)

            def merge(g):
                pe.wait_ge(s["ot"], g + 1)
                for i in range(4):
                    o = begin(("o", g, i))
                    for h in range(2):
                        ins = mm(o[:, 0:D], oT[:, i, h].rearrange("p b i -> p (b i)"), wsm[:, 5, h, :],
                                 start=(h == 0), stop=(h == 1))
                    ins.then_inc(s["gemm"], 1)

            def hidden(g):
                for i in range(4):
                    o = begin(("x2t", g, i))
                    pe.wait_ge(s["h2row"], 4 * g + i + 1)
                    for c in range(2):
                        ins = mm(o[:, c * P:(c + 1) * P], x1[:, g % 2, i, c * P:(c + 1) * P], diag2[:, i], start=True, stop=True)
                    ins.then_inc(s["gemm"], 1)
                pe.wait_ge(s["eva"], emptied[use_of[("x2t", g, 3)]][1])
                if g == 0:
                    pe.wait_ge(s["wready"], 2)
                for f in range(FC):
                    o = begin(("h", g, f))
                    for c in range(2):
                        x = x2T[:, c, :].rearrange("p (t i) -> p t i", i=SLOT)[:, :, 0:KSEL]
                        ins = mm(o[:, 0:NC], w1[:, c, f * P:(f + 1) * P], x, start=(c == 0), stop=(c == 1))
                    ins.then_inc(s["gemm"], 1)

            def outer(g):
                for h in range(2):
                    o = begin(("y", g, h))
                    for f in range(FC):
                        if h == 0:
                            pe.wait_ge(s["eva"], emptied[use_of[("h", g, f)]][1])
                        ins = mm(o[:, 0:NC], w2[:, f, h * P:(h + 1) * P], hT[:, f, :], start=(f == 0), stop=(f == FC - 1))
                    ins.then_inc(s["gemm"], 1)
                pe.wait_ge(s["evv"], emptied[use_of[("y", g, 1)]][1])
                for i in range(4):
                    o = begin(("yt", g, i))
                    for h in range(2):
                        ins = pe.transpose(o[:, h * P:(h + 1) * P], yT[:, h, 4 * i:4 * i + 4, :].rearrange("p t i -> p (t i)"),
                                           ident[:, :])
                    ins.then_inc(s["gemm"], 1)

            project(0)
            masks()
            for g in range(SG):
                scores(g)
                if g + 1 < SG:
                    project(g + 1)
                if g >= 1:
                    hidden(g - 1)
                attend(g)
                if g >= 1:
                    outer(g - 1)
                merge(g)
            hidden(SG - 1)
            outer(SG - 1)

        @block.scalar
        def _(act):
            fn = act.activation
            act.wait_ge(s["s4in"], 32)
            fn(s4v[:, 0, :], s4in[:, 0, :], ACT.Exp).then_inc(s["act_s4"], 1)
            fn(s4v[:, 1, :], s4in[:, 1, :], ACT.Exp).then_inc(s["act_s4"], 1)
            for n, c in enumerate(ORDER):
                act.wait_ge(s["var"], n + 1)
                fn(vec[:, V_D, pos_of(c)], vec[:, V_Q, pos_of(c)], ACT.Sqrt, bias=eps_ln, scale=1.0 / D).then_inc(s["std"], 1)
                act.wait_ge(s["nrm"], n + 1)
                if n == NCH - 1:
                    act.wait_ge(s["lo"], n)
                for j in range(CH):
                    q = c * CH + j
                    ins = fn(hn[:, c, 0, j, :], h0[:, q, :], ACT.Identity, bias=vec[:, V_B, q:q + 1], scale=vec[:, V_R, q:q + 1])
                ins.then_inc(s["hi"], 1)
                for m in early_builds(n, "tba"):
                    keep_toep(act, act.copy, m)
            act.wait_ge(s["tabf"], 1)
            fn(rp[:, 2], rp[:, 2], ACT.Sin)
            for k, sign in enumerate((-1.0, 1.0)):
                x = rp[:, 3].rearrange("p (x d) -> p x d", d=HD)[:, :, k * 8:k * 8 + 8]
                ins = fn(x, x, ACT.Sin, scale=sign)
            ins.then_inc(s["tabs"], 1)
            act.wait_ge(s["lo"], NCH)
            for n in range(NGRP):
                act.wait_ge(s["conv"], n + 1)
                if n >= SIL:
                    act.wait_ge(s["addv"] if (n - SIL) % 2 == 0 else s["addp"], (n - SIL) // 2 + 1)
                k = 2 * (n % CSLOT)
                fn(sil(n).rearrange("p (b x) -> p b x", b=2), psum[:, k:k + 2, 0:4 * POS], ACT.Silu, scale=yscale
                   ).then_inc(s["sil"], 1)
                for m in later_builds(n)[0:1]:
                    keep_toep(act, act.copy, m)
            for c in range(RW_ACT):
                act.wait_ge(s["rwprod"], c + 1)
                for q in range(c * CH, (c + 1) * CH):
                    ins = fn(hn32[:, c, q % CH, :], hn32[:, c, q % CH, :], ACT.Identity, accum_out=vec[:, V_W, q:q + 1])
            ins.then_inc(s["rwdot"], 1)
            act.wait_ge(s["var3"], 1)
            fn(vec[:, V_D, :], vec[:, V_Q, :], ACT.Sqrt, bias=eps_ln, scale=1.0 / D).then_inc(s["std3"], 1)
            def routed(g):
                q4 = slice(4 * g, 4 * g + 4)
                act.wait_ge(s["rvar"], g + 1)
                fn(sd[:, q4], sq_[:, q4], ACT.Sqrt, bias=eps_ln, scale=1.0 / D).then_inc(s["rstd"], 1)
                act.wait_ge(s["rows"], g + 1)
                for q in range(4 * g, 4 * g + 4):
                    fn(gs[:, q], h1s[:, q], ACT.Identity, bias=nb[:, q:q + 1], scale=rr[:, q:q + 1]).then_inc(s["g1"], 1)
                    act.wait_ge(s["g1"], q + 1)
                    if q >= 1:
                        act.wait_ge(s["ssq"], q)
                    fn(junk_a, gs[:, q], ACT.Square, accum_out=ssq[:, q:q + 1]).then_inc(s["ssq"], 1)
                act.wait_ge(s["ssq"], 4 * g + 4)
                fn(rms1[:, q4], ssq[:, q4], ACT.Sqrt, bias=eps_rms, scale=1.0 / D).then_inc(s["rms1"], 1)

            def empty(u, dst, src, func=ACT.Copy):
                act.wait_ge(s["gemm"], use_of[u] + 1)
                fn(dst, src, func).then_inc(s["eva"], 1)

            routed(0)
            for g in range(SG):
                for i in range(2):
                    empty(("cs", g, i), cs[:, i, g * NC:(g + 1) * NC], bank(("cs", g, i))[:, 0:NC])

            def project(g):
                act.wait_ge(s["rms1r"], g + 1)
                if g == 0:
                    act.wait_ge(s["eva"], emptied[use_of[("cs", SG - 1, 1)]][1])
                else:
                    act.wait_ge(s["gemm"], use_of[("xt", g - 1, 3)] + 1)
                for i in range(4):
                    fn(diag1[:, i], ident[:, :], ACT.Copy, scale=r1[:, 4 * g + i:4 * g + i + 1]).then_inc(s["hrow"], 1)
                for i in range(4):
                    turn(g, i)

            def values(g):
                for i in range(4):
                    if g >= 2:
                        act.wait_ge(s["pv"], g - 1)
                    empty(("v", g, i), vv[:, g % 2, i], bank(("v", g, i))[:, 0:D])


            def spread_keys(g):
                if g >= 1:
                    act.wait_ge(s["sc"], g)
                    if g == 1:
                        act.wait_ge(s["outd"], 32 * NCH)
                else:
                    act.wait_ge(s["gemm"], use_of[("mask", 0, 0)] + 1)
                act.wait_ge(s["keys"], 2 * (g + 1))
                spread(act, lambda o, x, f: fn(o, x, ACT.Copy, scale=f), g, 1).then_inc(s["kx"], 1)

            def turn(g, i):
                if g >= 1:
                    act.wait_ge(s["gemm"], use_of[("v", g - 1, 3)] + 1)
                empty(("xt", g, i), xT[:, :, i * P:(i + 1) * P], bank(("xt", g, i))[:, 0:2 * P].rearrange("p (c n) -> p c n", c=2))

            def second_rms(g):
                q4 = slice(4 * g, 4 * g + 4)
                act.wait_ge(s["ssq2"], 4 * g + 4)
                fn(rms2[:, q4], ssq2[:, q4], ACT.Sqrt, bias=eps_rms, scale=1.0 / D).then_inc(s["rms2"], 1)

            def feed(g):
                act.wait_ge(s["rms2r"], g + 1)
                if g >= 1:
                    act.wait_ge(s["gemm"], use_of[("x2t", g - 1, 3)] + 1)
                for i in range(4):
                    fn(diag2[:, i], ident[:, :], ACT.Copy, scale=rr2[:, 4 * g + i:4 * g + i + 1]).then_inc(s["h2row"], 1)
                for i in range(4):
                    if g >= 1:
                        act.wait_ge(s["gemm"], use_of[("h", g - 1, FC - 1)] + 1)
                    else:
                        act.wait_ge(s["outd"], 32 * NCH)
                    empty(("x2t", g, i), x2T[:, :, i * P:(i + 1) * P],
                          bank(("x2t", g, i))[:, 0:2 * P].rearrange("p (c n) -> p c n", c=2))

            def hidden(g):
                for f in range(FC):
                    if g >= 1:
                        act.wait_ge(s["gemm"], use_of[("y", g - 1, 1)] + 1)
                    empty(("h", g, f), hT[:, f, :], bank(("h", g, f))[:, 0:NC], ACT.Gelu_apprx_tanh)

            def exps(g):
                act.wait_ge(s["pin"], g + 1)
                p3 = pr.rearrange("p q c i -> p (q c) i")[:, :, 0:KSEL]
                fn(p3, p3, ACT.Exp).then_inc(s["pexp"], 1)

            project(0)
            values(0)
            routed(1)
            spread_keys(0)
            for g in range(SG):
                if g + 1 < SG:
                    project(g + 1)
                exps(g)
                if g + 1 < SG:
                    values(g + 1)
                if g >= 1:
                    feed(g - 1)
                if g + 1 < SG:
                    spread_keys(g + 1)
                if g == 0:
                    routed(2)
                if g >= 1:
                    hidden(g - 1)
                if g == 1:
                    routed(3)
                second_rms(g)
            feed(SG - 1)
            hidden(SG - 1)

        @block.vector
        def _(v):
            done = [0]
            TT = v.tensor_tensor

            def link(ins):
                done[0] += 1
                ins.then_inc(s["dve"], 1)
                v.wait_ge(s["dve"], done[0])

            def moments(dst_s, dst_d, dst_q, x):
                TT(dst_s, x[:, :, 1], x[:, :, 4], ALU.add)
                TT(dst_q, x[:, :, 2], x[:, :, 5], ALU.add)
                link(TT(dst_d, x[:, :, 1], x[:, :, 4], ALU.subtract))
                link(v.scalar_tensor_tensor(dst_d, dst_d, D / 4.0, dst_d, ALU.mult, ALU.mult))
                return TT(dst_q, dst_q, dst_d, ALU.add)

            v.memset(eps_ln, LN_EPS)
            v.memset(eps_rms, RMS_EPS)
            v.wait_ge(s["s4in"], 32)
            v.wait_ge(s["act_s4"], 2)
            dt, ew, aw, bw = (s4v[:, i, :] for i in range(4))
            TT(aw, ew, dt, ALU.mult)
            link(TT(bw, s4in[:, 2, :], dt, ALU.mult))
            cb, sb_ = row1(c_c, HF), row1(c_s, HF)
            TT(er, col1(aw, FR), cb, ALU.mult)
            link(TT(t1, col1(bw, FR), cb, ALU.mult))
            link(TT(ei, sb_, t1, ALU.subtract))
            TT(iv, ei, ei, ALU.mult)
            link(TT(t1, er, er, ALU.mult))
            link(TT(iv, iv, t1, ALU.add))
            link(v.reciprocal(iv, iv))
            TT(er, er, iv, ALU.mult)
            TT(ei, ei, iv, ALU.mult).then_inc(s["x"], 1)
            v.wait_ge(s["pos"], 48)
            link(TT(posb[:, :, :], posb[:, :, :], row1(brow, 8), ALU.add))

            def kernel_spectrum():
                v.wait_ge(s["q"], 1)
                link(v.tensor_copy(late[0:FR, 0:2048], psum[0:FR, 4:8, :].rearrange("p b x -> p (b x)")))
                v.wait_ge(s["const"], 144)
                q = [qs[:, i] for i in range(8)]
                g = [gt[:, i] for i in range(8)]
                c = dft[:, 2 * S:2 * S + 1]
                TT(g[0], q[1], q[2], ALU.mult)
                TT(g[1], q[5], q[6], ALU.mult)
                TT(g[2], q[1], q[6], ALU.mult)
                link(TT(g[3], q[5], q[2], ALU.mult))
                TT(g[0], g[0], g[1], ALU.subtract)
                link(TT(g[2], g[2], g[3], ALU.add))
                v.tensor_scalar(g[0], g[0], c, None, ALU.mult)
                v.tensor_scalar(g[2], g[2], c, None, ALU.mult)
                v.tensor_scalar(g[4], q[3], c, 1.0, ALU.mult, ALU.add)
                link(v.tensor_scalar(g[5], q[7], c, None, ALU.mult))
                TT(g[6], g[4], g[4], ALU.mult)
                link(TT(g[7], g[5], g[5], ALU.mult))
                link(TT(g[6], g[6], g[7], ALU.add))
                link(v.reciprocal(g[6], g[6]))
                TT(g[1], g[0], g[4], ALU.mult)
                TT(g[3], g[2], g[5], ALU.mult)
                TT(g[7], g[2], g[4], ALU.mult)
                link(TT(g[0], g[0], g[5], ALU.mult))
                TT(g[1], g[1], g[3], ALU.add)
                link(TT(g[7], g[7], g[0], ALU.subtract))
                TT(g[1], g[1], g[6], ALU.mult)
                link(TT(g[7], g[7], g[6], ALU.mult))
                TT(g[0], q[0], g[1], ALU.subtract)
                link(TT(g[2], q[4], g[7], ALU.subtract))
                v.sem_inc(s["g"], 1)

            def kernel_parts():
                v.wait_ge(s["k"], 1)
                link(v.tensor_copy(ksb, psum[0:S, 2, 0:D]))
                link(v.tensor_scalar(kneg, ksb, -1.0, None, ALU.mult))
                link(TT(kneg, kneg, ksb, ALU.max))
                v.reduce_max(am64[0:S], kneg, AX).then_inc(s["am"], 1)
                v.wait_ge(s["amt"], 1)
                link(v.reduce_max(am1[0:1], psum[0:1, 3, 0:S], AX))
                v.tensor_scalar(am1[0:1], am1[0:1], 1e-30, None, ALU.max).then_inc(s["am"], 1)
                v.wait_ge(s["amt"], 2)
                link(v.tensor_copy(amax, psum[:, 3, 128:129]))
                v.tensor_scalar(yscale, amax, 1.0 / (T_PEAK * X_GAIN), None, ALU.mult).then_inc(s["amb"], 1)
                link(v.reciprocal(kscale, amax))
                link(v.tensor_scalar(kscale, kscale, T_PEAK, None, ALU.mult))
                link(v.tensor_scalar(ksb, ksb, kscale[0:S], None, ALU.mult))
                v.wait_ge(s["rhs"], 1)
                link(v.tensor_copy(kp[:, 0], ksb))
                link(TT(kp[:, 1], ksb, kp[:, 0], ALU.subtract))
                v.sem_inc(s["khl"], 1)

            def rope_angles():
                v.wait_ge(s["rope"], 32)
                v.wait_ge(s["embv"], CH // 2)
                for k in range(2):
                    ins = v.tensor_copy(rp[:, 0, k * 64:k * 64 + 64].rearrange("p (b d) -> p b d", b=NBB),
                                        col1(posi[:, k * NBB:(k + 1) * NBB], HD))
                link(ins)
                x = rp[:, 0].rearrange("p (x d) -> p x d", d=HD)
                link(TT(x, x, row1(invf, 8), ALU.mult))
                link(v.tensor_scalar(rp[:, 1], rp[:, 0], float(1 / (2 * np.pi)), 12582912.0, ALU.mult, ALU.add))
                link(v.tensor_scalar(rp[:, 1], rp[:, 1], -12582912.0, None, ALU.add))
                for part in TWO_PI:
                    link(v.scalar_tensor_tensor(rp[:, 0], rp[:, 1], -part, rp[:, 0], ALU.mult, ALU.add))
                link(v.tensor_scalar(rp[:, 2], rp[:, 0], float(np.pi / 2), None, ALU.add))
                link(v.tensor_scalar(rp[:, 1], rp[:, 2], float(np.pi), float(-2 * np.pi), ALU.is_gt, ALU.mult))
                link(TT(rp[:, 2], rp[:, 2], rp[:, 1], ALU.add))
                v.tensor_scalar(rp[:, 2], rp[:, 2], PI_LOW, -PI_LOW, ALU.min, ALU.max)
                link(v.tensor_scalar(rp[:, 3], rp[:, 0], PI_LOW, -PI_LOW, ALU.min, ALU.max))
                v.sem_inc(s["tabf"], 1)

            def normaliser(n):
                p = pos_of(ORDER[n])
                v.wait_ge(s["std"], n + 1)
                link(v.reciprocal(vec[:, V_R, p], vec[:, V_D, p]))
                link(v.tensor_scalar(vec[:, V_R, p], vec[:, V_R, p], X_GAIN, None, ALU.mult))
                v.scalar_tensor_tensor(vec[:, V_B, p], vec[:, V_S, p], -0.5, vec[:, V_R, p], ALU.mult, ALU.mult
                                       ).then_inc(s["nrm"], 1)

            def low_part(n):
                v.wait_ge(s["hi"], n + 1)
                v.wait_ge(s["t32"], n + 1)
                TT(hn[:, ORDER[n], 1], t32(n), hn[:, ORDER[n], 0], ALU.subtract).then_inc(s["lo"], 1)

            for n, c in enumerate(ORDER):
                if c == 0:
                    for i in range(CH // 2):
                        v.wait_ge(s["emb"], i + 1)
                        TT(h0[:, 2 * i:2 * i + 2, :].rearrange("p j d -> p (j d)"), psum[:, i if i < 2 else 2 + i, :],
                           posb[:, 2 * i:2 * i + 2, :].rearrange("p j d -> p (j d)"), ALU.add).then_inc(s["embv"], 1)
                    v.wait_ge(s["embv"], CH // 2)
                else:
                    v.wait_ge(s_txt[c], 32)
                for j in range(CH):
                    ins = v.bn_stats(st[:, c * CH + j, :], h0[:, c * CH + j, :])
                link(ins)
                p = pos_of(c)
                moments(vec[:, V_S, p], vec[:, V_D, p], vec[:, V_Q, p], st[:, p, :]).then_inc(s["var"], 1)
                if n >= 1:
                    normaliser(n - 1)
                if n >= 2:
                    low_part(n - 2)
                    for m in early_builds(n - 2, "tbv"):
                        keep_toep(v, v.tensor_copy, m)
                if n == 0:
                    kernel_spectrum()
                if n == 1:
                    kernel_parts()
                if n == 4:
                    rope_angles()
            normaliser(NCH - 1)
            for n in (NCH - 2, NCH - 1):
                low_part(n)
                for m in early_builds(n, "tbv"):
                    keep_toep(v, v.tensor_copy, m)
            for n in range(0, NGRP, 2):
                v.wait_ge(s["sil"], n + 1)
                add_group(v, n).then_inc(s["addv"], 1)
                for m in later_builds(n)[1:] + later_builds(n + 1)[1:]:
                    keep_toep(v, v.tensor_copy, m)
                if n >= NGRP // 2:
                    if n == NGRP // 2:
                        v.wait_ge(s["addv"], NGRP // 4)
                        v.wait_ge(s["addp"], NGRP // 4)
                    k = POS // (NGRP // 4)
                    for q in range((n - NGRP // 2) // 2 * k, (n - NGRP // 2) // 2 * k + k):
                        v.bn_stats(st_first[:, q, :], h0[:, q, 0:D // 2])
            v.wait_ge(s["addv"], NGRP // 2)
            v.wait_ge(s["addp"], NGRP // 2)
            for q in range(POS):
                ins = v.bn_stats(st[:, q, :], h0[:, q, D // 2:D])
            link(ins)
            A, B, S1, Q1 = vec[:, V_A, :], vec[:, V_B, :], vec[:, V_S, :], vec[:, V_Q, :]
            d, w = vec[:, V_D, :], vec[:, V_R, :]
            fa, fb = st_first, st
            TT(A, fa[:, :, 1], fa[:, :, 4], ALU.add)
            TT(B, fb[:, :, 1], fb[:, :, 4], ALU.add)
            TT(Q1, fa[:, :, 2], fa[:, :, 5], ALU.add)
            TT(w, fb[:, :, 2], fb[:, :, 5], ALU.add)
            TT(d, fa[:, :, 1], fa[:, :, 4], ALU.subtract)
            link(TT(S1, fb[:, :, 1], fb[:, :, 4], ALU.subtract))
            TT(Q1, Q1, w, ALU.add)
            TT(d, d, d, ALU.mult)
            link(TT(S1, S1, S1, ALU.mult))
            TT(w, A, B, ALU.subtract)
            link(TT(d, d, S1, ALU.add))
            link(v.scalar_tensor_tensor(Q1, d, D / 8.0, Q1, ALU.mult, ALU.add))
            link(TT(d, w, w, ALU.mult))
            link(TT(S1, A, B, ALU.add))
            v.scalar_tensor_tensor(Q1, d, D / 16.0, Q1, ALU.mult, ALU.add).then_inc(s["var3"], 1)
            link(v.tensor_scalar(S1, S1, 0.5, None, ALU.mult))
            v.wait_ge(s["conv"], NGRP)
            v.memset(ones_b, 1.0)
            for q in range(RW_ACT * CH, POS):
                v.tensor_tensor_reduce(hn32[:, q // CH, q % CH, :], h0[:, q, :], rwb[:, :], 1.0, 0.0, ALU.mult, ALU.add,
                                       vec[:, V_W, q:q + 1])
            link(v.reduce_sum(srw, rwb[:, :], AX))
            v.wait_ge(s["rwdot"], 1)
            v.wait_ge(s["std3"], 1)
            link(v.reciprocal(vec[:, V_R, :], vec[:, V_D, :]))
            link(v.scalar_tensor_tensor(vec[:, V_B, :], vec[:, V_S, :], -0.5, vec[:, V_R, :], ALU.mult, ALU.mult))
            TT(vec[:, V_W, :], vec[:, V_W, :], vec[:, V_R, :], ALU.mult)
            link(v.tensor_scalar(vec[:, V_A, :], vec[:, V_R, :], 1.0, None, ALU.add))
            link(v.scalar_tensor_tensor(vec[:, V_W, :], vec[:, V_B, :], srw, vec[:, V_W, :], ALU.mult, ALU.add))
            link(v.tensor_scalar(vec[:, V_W, :], vec[:, V_W, :], rbias, None, ALU.add))
            v.sem_inc(s["w72"], 1)
            W, W2, W3, gtm, eqm, pre, sel, key, _, m8 = (tk[:, i, 0:TOK] for i in range(10))
            v.wait_ge(s["wmov"], 1)
            for g in range(2):
                v.tensor_copy(W[:, 8 * g:8 * g + 8], psum[0:S, 0, g * POS:g * POS + 8])
                ins = v.tensor_copy(W[:, 16 + 64 * g:80 + 64 * g], psum[0:S, 0, g * POS + 8:(g + 1) * POS])
            link(ins)

            def top24(x, y, z):
                link(v.max(m8[:, 0:8], x))
                link(v.match_replace(y, m8[:, 0:8], x, NEG))
                link(v.max(m8[:, 8:16], y))
                link(v.match_replace(z, m8[:, 8:16], y, NEG))
                link(v.max(m8[:, 16:24], z))

            top24(W, W2, W3)
            last, thr = m8[:, KSEL - 1:KSEL], m8[:, KSEL:KSEL + 1]
            v.tensor_scalar(gtm, W, last, None, ALU.is_gt)
            v.tensor_scalar(key, W, thr, None, ALU.is_gt)
            link(v.memset(W2, 1.0))
            link(v.tensor_scalar(eqm, W, last, None, ALU.is_equal))
            v.reduce_sum(m8[:, 24:25], gtm, AX)
            link(v.tensor_tensor_scan(pre, W2, eqm, 0.0, ALU.mult, ALU.add))
            link(v.tensor_scalar(m8[:, 25:26], m8[:, 24:25], -1.0, float(KSEL), ALU.mult, ALU.add))
            link(v.scalar_tensor_tensor(eqm, pre, m8[:, 25:26], eqm, ALU.is_le, ALU.mult))
            TT(sel, gtm, eqm, ALU.add)
            v.wait_ge(s["tokload"], 16)
            link(TT(key, key, base, ALU.add))
            link(TT(key, key, sel, ALU.mult))
            top24(key, W2, W3)
            ki = tk[:, 13, 0:KSEL].bitcast(I32)
            kb = tk[:, 13, 32:32 + KSEL].bitcast(I32)
            bit, tok = tk[:, 14, 0:KSEL], tk[:, 14, 32:64]
            link(v.tensor_copy(ki, m8[:, 0:KSEL]))
            link(v.tensor_scalar(kb, ki, 1, None, ALU.bitwise_and))
            v.memset(tok, 0.0)
            v.memset(tk[:, 11, 0:SLOT], SKIP_ROW)
            v.memset(tk[:, 12, 0:SLOT], 0.0)
            link(v.tensor_copy(bit, kb))
            link(TT(tok[:, 0:KSEL], m8[:, 0:KSEL], bit, ALU.subtract))
            v.tensor_scalar(tk[:, 12, 0:KSEL], bit, -1.0, 1.0, ALU.mult, ALU.add)
            link(v.tensor_scalar(tok[:, 0:KSEL], tok[:, 0:KSEL], -0.5, 256.0, ALU.mult, ALU.add))
            v.tensor_scalar(tk[:, 11, 0:KSEL], tok[:, 0:KSEL], cst[0:S, 2:3], None, ALU.add)
            link(v.tensor_scalar(tk[:, 10, 0:SLOT], tok, cst[0:S, 2:3], None, ALU.add))
            v.sem_inc(s["idx"], 1)
            link(TT(dg, tok[:, 0:KSEL].rearrange("p (o i) -> p o i", o=1).to_broadcast([S, S, KSEL]),
                    col1(ident[0:S, 0:S], KSEL), ALU.mult))
            v.sem_inc(s["seldg"], 1)
            v.wait_ge(s["idxp"], 1)
            v.tensor_copy(idxg, psum[:, 1, 0:NQ])
            v.tensor_copy(idxs, psum[:, 1, NQ:2 * NQ])
            link(v.tensor_copy(notm, psum[:, 1, 2 * NQ:3 * NQ]))
            v.sem_inc(s["idxr"], 1)
            v.wait_ge(s["ind"], 1)
            sv = [su[:, x, :].rearrange("p (b n) -> p b n", b=4) for x in range(2)]
            v.tensor_scalar(sv[0], psum[:, 2:6, 0:NC], cst[:, 0:1], None, ALU.is_equal)
            link(v.tensor_scalar(sv[1], psum[:, 2:6, 0:NC], cst[:, 1:2], None, ALU.is_equal))
            v.sem_inc(s["oh"], 1)

            def begin(u):
                v.wait_ge(s["gemm"], use_of[u] + 1)
                return bank(u)

            v.memset(oT.rearrange("p q h b i -> p (q h b i)"), 0.0)
            link(v.memset(qT.rearrange("p h t i -> p (h t i)"), 0.0))

            def routed(g):
                q4 = slice(4 * g, 4 * g + 4)
                for q in range(4 * g, 4 * g + 4):
                    v.wait_ge(s_gath[q], 16)
                    ins = v.bn_stats(st2[:, q, :], h1s[:, q, :])
                link(ins)
                moments(sm[:, q4], sd[:, q4], sq_[:, q4], st2[:, q4, :]).then_inc(s["rvar"], 1)
                v.wait_ge(s["rstd"], g + 1)
                link(v.reciprocal(rr[:, q4], sd[:, q4]))
                v.scalar_tensor_tensor(nb[:, q4], sm[:, q4], -0.5, rr[:, q4], ALU.mult, ALU.mult).then_inc(s["rows"], 1)
                v.wait_ge(s["rows"], g + 1)
                TT(sd[:, q4], nb[:, q4], notm[:, q4], ALU.mult)
                link(TT(sm[:, q4], rr[:, q4], notm[:, q4], ALU.mult))
                v.tensor_scalar(sm[:, q4], sm[:, q4], 1.0, None, ALU.add).then_inc(s["ownf"], 1)
                for q in range(4 * g, 4 * g + 4):
                    v.wait_ge(s["g1"], q + 1)
                    link(v.tensor_tensor_reduce(junk_v, gs[:, q], rwb[:, :], 1.0, 0.0, ALU.mult, ALU.add, wsel[:, q:q + 1]))
                v.tensor_scalar(wsel[:, q4], wsel[:, q4], rbias, None, ALU.add)
                v.wait_ge(s["rms1"], g + 1)
                v.reciprocal(r1[:, q4], rms1[:, q4]).then_inc(s["rms1r"], 1)

            routed(0)

            def mask_rows():
                for g in range(SG):
                    for i in range(2):
                        o = begin(("u", g, i))
                        rows = P if i == 0 else TOK - P
                        v.tensor_copy(su[0:rows, 2 + i, g * NC:(g + 1) * NC], o[0:rows, 0:NC]).then_inc(s["evv"], 1)
                v.wait_ge(s["evv"], emptied[use_of[("mask", 0, 0)] - 4][1])
                v.memset(bank(("mask", 0, 0))[:, 0:NC], 0.0).then_inc(s["mbank"], 1)

            def mask():
                o = begin(("mask", 0, 0))
                v.tensor_copy(msk, o[:, 0:NC].rearrange("p (q k) -> p q k", q=NQ)).then_inc(s["evv"], 1)
                v.wait_ge(s["evv"], emptied[use_of[("mask", 0, 0)]][1])

            def project(g):
                c0 = slice(g * NC, (g + 1) * NC)
                if g >= 1:
                    v.wait_ge(s["sc"], g)
                for h in range(2):
                    for w in ("q", "k"):
                        o = begin((w, g, h))
                        if g == 0 and h == 0 and w == "q":
                            v.wait_ge(s["eva"], emptied[use_of[("cs", SG - 1, 1)]][1])
                        TT(tmp[:, 0], o[:, 0:NC], cs[:, 0, c0], ALU.mult)
                        v.stream_shuffle(tmp[:, 1], o[:, 0:NC], HALF_TURN).then_inc(s["evv"], 1)
                        v.wait_ge(s["evv"], emptied[use_of[(w, g, h)]][1])
                        link(TT(tmp[:, 1], tmp[:, 1], cs[:, 1, c0], ALU.mult))
                        t3 = [tmp[:, x].rearrange("p (t i) -> p t i", t=SQ) for x in range(2)]
                        if w == "q":
                            link(TT(qT[:, h, :, 0:KSEL], t3[0], t3[1], ALU.add))
                            v.sem_inc(s["qk"], 1)
                        else:
                            if g >= 1 and h == 1:
                                v.wait_ge(s["kx"], 2 * g)
                            link(TT(kT[:, h], t3[0], t3[1], ALU.add))
                            v.sem_inc(s["keys"], 1)

            def spread_keys(g):
                if g == 1:
                    v.wait_ge(s["outd"], 32 * NCH)
                spread(v, lambda o, x, f: v.tensor_scalar(o, x, f, None, ALU.mult), g, 0).then_inc(s["kx"], 1)

            def softmax(g):
                v.wait_ge(s["sc"], g + 1)
                if g >= 1:
                    v.wait_ge(s["pv"], g)
                p4 = pr.rearrange("p q c i -> p (q c) i")[:, :, 0:KSEL]
                link(TT(pr[:, :, :, 0:KSEL], psum[:, 0:4, 0:2 * HP * KSEL].rearrange("p q (c k) -> p q c k", k=KSEL),
                        msk[:, 4 * g:4 * g + 4, :].rearrange("p q (o k) -> p q o k", o=1).to_broadcast([P, 4, 2 * HP, KSEL]),
                        ALU.add))
                link(v.reduce_max(mx, p4, AX))
                TT(p4, p4, col1(mx, KSEL), ALU.subtract).then_inc(s["pin"], 1)

            def weights(g):
                p4 = pr.rearrange("p q c i -> p (q c) i")[:, :, 0:KSEL]
                v.wait_ge(s["pexp"], g + 1)
                link(v.reduce_sum(rinv, p4, AX))
                link(v.reciprocal(rinv, rinv))
                link(TT(p4, p4, col1(rinv, KSEL), ALU.mult))
                v.transpose(prT.rearrange("p q c i -> p (q c i)"), pr.rearrange("p q c i -> p (q c i)")
                            ).then_inc(s["pt"], 1)

            def heads_out(g):
                v.wait_ge(s["pv"], g + 1)
                if g >= 1:
                    v.wait_ge(s["gemm"], use_of[("o", g - 1, 3)] + 1)
                o8 = oT.rearrange("p q h b i -> p (q h) b i")
                pp = psum[:, 0:4, 0:8 * 34].rearrange("p b (x e i) -> p b x e i", x=8, e=2)
                for b in range(4):
                    ins = v.tensor_scalar(o8[:, :, b, 0:KSEL], pp[:, b, :, 0, :], cst[:, 3:4], None, ALU.mult)
                link(ins)
                for b in range(4):
                    ins = v.scalar_tensor_tensor(o8[:, :, b, 0:KSEL], pp[:, b, :, 1, :], cst[:, 4:5], o8[:, :, b, 0:KSEL],
                                                 ALU.mult, ALU.add)
                ins.then_inc(s["ot"], 1)

            def merge(g):
                for i in range(4):
                    o = begin(("o", g, i))
                    if g >= 2:
                        v.wait_ge(s_scat[g - 2], 64)
                    q = 4 * g + i
                    TT(x1[:, g % 2, i], o[:, 0:D], gs[:, q], ALU.add).then_inc(s["evv"], 1)
                    v.wait_ge(s["evv"], emptied[use_of[("o", g, i)]][1])
                    if i == 0:
                        v.wait_ge(s["own"], g + 1)
                    v.tensor_tensor_reduce(gs[:, q], x1[:, g % 2, i], x1[:, g % 2, i], 1.0, 0.0, ALU.mult, ALU.add,
                                           ssq2[:, q:q + 1]).then_inc(s["ssq2"], 1)

            def second_rms(g):
                v.wait_ge(s["rms2"], g + 1)
                v.reciprocal(rr2[:, 4 * g:4 * g + 4], rms2[:, 4 * g:4 * g + 4]).then_inc(s["rms2r"], 1)

            def mlp(g):
                if g == 0:
                    v.wait_ge(s["outd"], 32 * NCH)
                    link(v.memset(yT.rearrange("p h t i -> p (h t i)"), 0.0))
                for h in range(2):
                    o = begin(("y", g, h))
                    if g >= 1:
                        v.wait_ge(s["gemm"], use_of[("yt", g - 1, 3)] + 1)
                    v.tensor_copy(yT[:, h, :, 0:KSEL], o[:, 0:NC].rearrange("p (t i) -> p t i", t=SQ)).then_inc(s["evv"], 1)
                for i in range(4):
                    q = 4 * g + i
                    o = begin(("yt", g, i))
                    x = x1[:, g % 2, i]
                    TT(x, x, o[:, 0:D], ALU.add).then_inc(s["evv"], 1)
                    v.wait_ge(s["evv"], emptied[use_of[("yt", g, i)]][1])
                    v.scalar_tensor_tensor(x, x, wsel[:, q:q + 1], h1s[:, q], ALU.mult, ALU.add).then_inc(s["fin"], 1)

            project(0)
            mask_rows()
            routed(1)
            mask()
            spread_keys(0)
            for g in range(SG):
                softmax(g)
                if g >= 1:
                    second_rms(g - 1)
                if g + 1 < SG:
                    project(g + 1)
                weights(g)
                if g + 1 < SG:
                    spread_keys(g + 1)
                if g == 0:
                    routed(2)
                heads_out(g)
                if g == 1:
                    routed(3)
                if g >= 1:
                    mlp(g - 1)
                merge(g)
            second_rms(SG - 1)
            mlp(SG - 1)

        @block.gpsimd
        def _(pool):
            steps = [0]

            def link(ins):
                steps[0] += 1
                ins.then_inc(s["poolw"], 1)
                pool.wait_ge(s["poolw"], steps[0])

            TT = pool.tensor_tensor
            pool.wait_ge(s["s4in"], 32)
            pool.wait_ge(s["act_s4"], 1)
            dt = s4v[:, 0, :]
            Br, Bi, Pr, Pi, Cr, Ci = (s4in[:, 3 + i, :] for i in range(6))
            ta, tb = s4v[:, 12, :], s4v[:, 13, :]
            for ab, (xr, xi, yr, yi, sg) in enumerate([(Br, Bi, Cr, Ci, 1), (Br, Bi, Pr, Pi, -1),
                                                       (Pr, Pi, Cr, Ci, 1), (Pr, Pi, Pr, Pi, -1)]):
                re, im = s4v[:, 4 + ab, :], s4v[:, 8 + ab, :]
                TT(ta, xr, yr, ALU.mult)
                link(TT(tb, xi, yi, ALU.mult))
                link(TT(re, ta, tb, ALU.subtract if sg > 0 else ALU.add))
                TT(ta, xi, yr, ALU.mult)
                link(TT(tb, xr, yi, ALU.mult))
                link(TT(im, ta, tb, ALU.add if sg > 0 else ALU.subtract))
            link(TT(s4v[:, 4:12, :], s4v[:, 4:12, :], row1(dt, 8), ALU.mult))
            eb = row1(c_e, HF)
            for i in range(4):
                re, im = col1(s4v[:, 4 + i, :], HG), col1(s4v[:, 8 + i, :], HG)
                TT(rhsA[:, :, i, :], re, eb, ALU.mult)
                TT(rhsA[:, :, 4 + i, :], im, eb, ALU.mult)
                ins = TT(rhsB[:, :, i, :], im, eb, ALU.mult)
            link(ins)
            link(pool.tensor_scalar(s4v[:, 4:8, :], s4v[:, 4:8, :], -1.0, None, ALU.mult))
            for i in range(4):
                ins = TT(rhsB[:, :, 4 + i, :], col1(s4v[:, 4 + i, :], HG), eb, ALU.mult)
            ins.then_inc(s["rhs"], 1)
            pool.wait_ge(s["x"], 1)
            for n, c in enumerate(ORDER):
                pool.wait_ge(s["nrm"], n + 1)
                if n >= 2:
                    pool.wait_ge(s["lo"], n - 1)
                for j in range(CH):
                    q = c * CH + j
                    ins = pool.tensor_scalar(t32(n)[:, j, :], h0[:, q, :], vec[:, V_R, q:q + 1], vec[:, V_B, q:q + 1],
                                             ALU.mult, ALU.add)
                ins.then_inc(s["t32"], 1)
                if ORDER[n] == 0:
                    for g in range(2):
                        z = toep[64 * g:64 * g + 64, :, 64 - 64 * g:128 - 64 * g].rearrange("p r t l c -> p r (t l c)")
                        if g == 0:
                            pool.wait_ge(s["t32"], n + 1)
                        else:
                            pool.wait_ge(s["tz"], 1)
                        pool.memset(z, 0.0).then_inc(s["tz"], 1)
                    pool.wait_ge(s["tz"], 2)
            for n in range(1, NGRP, 2):
                pool.wait_ge(s["sil"], n + 1)
                add_group(pool, n).then_inc(s["addp"], 1)
            pool.wait_ge(s["addv"], NGRP // 2)
            pool.wait_ge(s["addp"], NGRP // 2)
            pool.wait_ge(s["conv"], NGRP)
            for c in range(RW_ACT):
                pool.tensor_tensor(hn32[:, c], h0[:, pos_of(c), :], row1(rwb[:, :], CH), ALU.mult).then_inc(s["rwprod"], 1)
            pool.wait_ge(s["tabs"], 1)
            pool.wait_ge(s["rwdot"], 1)
            for k in range(2):
                for f in range(2):
                    ins = pool.tensor_copy(tab[:, k, :, f, :].rearrange("p b (h d) -> p b h d", d=HD),
                                           rp[:, 2 + f, k * 64:k * 64 + 64].rearrange("p (b o d) -> p b o d", b=NBB, o=1)
                                           .to_broadcast([P, NBB, 8, HD]))
            ins.then_inc(s["tab"], 1)
            pool.wait_ge(s["wload"], 64)
            for c in range(2):
                pool.tensor_scalar(wsm[:, 0, c], wsm[:, 0, c], lnw[:, c:c + 1], HD ** -0.5, ALU.mult, ALU.mult)
                pool.tensor_scalar(wsm[:, 1, c], wsm[:, 1, c], lnw[:, c:c + 1], None, ALU.mult)
                ins = pool.tensor_scalar(wsm[:, 4, c], wsm[:, 4, c], lnw[:, c:c + 1], None, ALU.mult)
            link(ins)
            pool.sem_inc(s["wready"], 1)
            pool.wait_ge(s["h1out"], 128)
            pool.wait_ge(s["idxr"], 1)
            for q in range(NQ):
                pool.indirect_dma_start(h1s[:, q, :], None, h1_rows, bass.IndirectOffsetOnAxis(ap=idxg[:, q:q + 1], axis=0),
                                        bounds_check=S * TOK - 1, oob_is_err=False).then_inc(s_gath[q], 16)
            for c in range(NCH):
                for j in range(CH):
                    q = c * CH + j
                    ins = pool.tensor_scalar(h0[:, q, :], h0[:, q, :], vec[:, V_A, q:q + 1], vec[:, V_B, q:q + 1],
                                             ALU.mult, ALU.add)
                ins.then_inc(s["outc"], 1)
            pool.wait_ge(s["w1load"], 32)
            for c in range(2):
                ins = pool.tensor_scalar(w1[:, c], w1[:, c], lnw[:, 2 + c:3 + c], None, ALU.mult)
            link(ins)
            pool.sem_inc(s["wready"], 1)

            def own_part(g):
                pool.wait_ge(s["ownf"], g + 1)
                for q in range(4 * g, 4 * g + 4):
                    pool.wait_ge(s["g1"], q + 1)
                    ins = pool.tensor_scalar(h1s[:, q], h1s[:, q], sm[:, q:q + 1], sd[:, q:q + 1], ALU.mult, ALU.add)
                ins.then_inc(s["own"], 1)

            for g in range(SG):
                own_part(g)
            pool.wait_ge(s["outd"], 32 * NCH)
            for q in range(NQ):
                pool.wait_ge(s["fin"], q + 1)
                pool.indirect_dma_start(out.rearrange("s t d -> (s t) d"), bass.IndirectOffsetOnAxis(ap=idxs[:, q:q + 1], axis=0),
                                        x1[:, q // 4 % 2, q % 4, :], None, bounds_check=S * TOK - 1, oob_is_err=False
                                        ).then_inc(s_scat[q // 4], 16)
            for g in range(SG):
                pool.wait_ge(s_scat[g], 64)


def _constants():
    m = np.arange(FR)
    half = np.pi * m / S
    out = {}
    own = np.zeros((P, HG), np.float32)
    own[np.arange(P), np.arange(P) % HG] = 1
    wave = np.concatenate([np.cos(half), 2 * np.sin(half)]).astype(np.float32)
    wave[FR - 1] = 0.0
    out["s4c"] = np.concatenate([np.broadcast_to(wave, (P, 2 * FR)), own], axis=1)
    phase = 2 * np.pi * m[:, None] * (np.arange(S) + 0.5) / S
    wgt = (np.where((m == 0) | (m == FR - 1), 1, 2) / S)[:, None]
    out["dft"] = np.concatenate([wgt * np.cos(phase), -wgt * np.sin(phase), wave[:FR, None]], axis=1)
    out["ident"] = np.eye(P)
    cst = np.zeros((P, 5))
    cst[:, 0] = np.arange(P)
    cst[:, 1] = np.arange(P) + P
    cst[:S, 2] = TOK * np.arange(S)
    cst[:, 3] = np.arange(P) % 32 < HD
    cst[:, 4] = np.arange(P) % 32 >= HD
    out["cst"] = cst
    out["own_head"] = np.arange(P)[:, None] // HD == np.arange(HP)
    pick = np.zeros((S, 2 * S), np.float32)
    pick[S - 1 - np.arange(S), np.arange(S)] = 1
    out["base"] = np.broadcast_to(2.0 * (256 - np.arange(TOK)), (S, TOK))
    inv = 1.0 / np.float32(10000.0) ** (np.arange(0, HD, 2, dtype=np.float32) / np.float32(HD))
    out["invf"] = np.broadcast_to(np.concatenate([inv, inv]), (P, HD))
    return {"pick": pick.astype(np.float16)} | {k: np.ascontiguousarray(x, dtype=np.float32) for k, x in out.items()}


def _lay_out(i):
    i = {k: np.asarray(v) for k, v in i.items()}
    h = {}

    def states(x):
        return x.reshape(HF, HG, 16).transpose(2, 1, 0).reshape(P, HF)

    h["s4in"] = np.stack([states(np.broadcast_to(i["L0_attn_log_dt"], (D, 16))), states(i["L0_attn_inv_w_real"]),
                          states(i["L0_attn_w_imaginary"])]
                         + [states(i["L0_attn_" + n].reshape(D, 16, 2)[..., x]) for n in "BPC" for x in range(2)], axis=1)
    x = i["x"].reshape(S, 3, 4, 16, 4, 16).transpose(1, 3, 5, 2, 4, 0)
    h["img"] = x.reshape(KC, P, 2, CH, S).transpose(1, 0, 3, 2, 4).reshape(P, KC, CH, P)
    h["wT"] = i["L0_tok_W"].T.reshape(KC, P, D).transpose(1, 0, 2)
    lag0 = np.zeros((1, S), np.float32)
    lag0[0, 0] = 1
    h["drow"] = np.concatenate([i["L0_attn_D"].reshape(1, D), lag0, np.ones((1, P), np.float32)], axis=1)
    h["lnw"] = np.concatenate([i["L0_ffn_ln1"].reshape(2, P).T, i["L0_ffn_ln2"].reshape(2, P).T], axis=1)
    pos = np.zeros((2 * P, NBB), i["L0_ffn_position_ids"].dtype)
    pos[:TOK] = i["L0_ffn_position_ids"][:, :TOK].T
    h["posT"] = pos.reshape(2, P, NBB).transpose(1, 0, 2).reshape(P, 2 * NBB)
    h["mask"] = i["L0_ffn_attention_mask"][:, 0, :TOK, :TOK]
    for name, src in (("txt", "txt"), ("b", "L0_tok_b"), ("pos_emb", "L0_tok_pos_emb"), ("rw", "L0_ffn_router_w"),
                      ("rb", "L0_ffn_router_b"), ("wq", "L0_ffn_wq"), ("wk", "L0_ffn_wk"), ("wv", "L0_ffn_wv"),
                      ("wo", "L0_ffn_wo"), ("w1", "L0_ffn_w1"), ("w2", "L0_ffn_w2")):
        h[name] = i[src]
    return {k: np.ascontiguousarray(x) for k, x in h.items()}


def program(nc, arrays):
    args = {n: nc.dram_tensor("in_" + n, x.shape, mybir.dt.from_np(x.dtype), kind="ExternalInput").ap()
            for n, x in arrays.items()}
    out = nc.dram_tensor("out_rows", (S, TOK, D), F32, kind="ExternalOutput").ap()
    build(nc, args, out)


def kernel(**inputs):
    import concourse.bacc as bacc
    from concourse.bass_utils import run_bass_kernel_spmd as run

    arrays = {**_lay_out(inputs), **_constants()}
    nc = bacc.Bacc("TRN2", target_bir_lowering=False, num_devices=1)
    program(nc, arrays)
    r = run(nc, [{"in_" + n: x for n, x in arrays.items()}], core_ids=[0])
    return r.results[0]["out_rows"]
```

```python
from contextlib import ExitStack

import numpy as np

import concourse.bass as bass
from concourse import mybir

F32 = mybir.dt.float32
F16 = mybir.dt.float16
BF16 = mybir.dt.bfloat16
I32 = mybir.dt.int32
U32 = mybir.dt.uint32
ALU = mybir.AluOpType
ACT = mybir.ActivationFunctionType
AX = mybir.AxisListType.X

P = 128
S = 64
TOK = 144
D = 256
POS = TOK // 2
CH = 8
NCH = POS // CH
KC = 768 // P
FR = S // 2 + 1
HG = 8
HF = D // HG
TCH = 16
NT = D // TCH
TRING = 3
UCH = 64
NU = D // UCH
QT = 4
NB = S // QT
GRP = 8
NGRP = D // GRP
CSLOT = 2
SIL = 3
KSEL = int(0.125 * TOK) - 1
SLOT = 32
HD = 16
HALF_TURN = [16 * (j // 16) + (j + 8) % 16 for j in range(32)]
HP = P // HD
FF = 1024
FC = FF // P
SG = 4
SQ = S // SG
NC = SQ * KSEL
NQ = S // 4
NBB = 4
LN_EPS = 1e-5
RMS_EPS = 1e-6
T_PEAK = 1024.0
X_GAIN = 64.0
NEG = -3.0e38
IDLE_PRODUCTS = 16
TOKEN_BANK = (6, 7, 2, 3)
SKIP_ROW = 30000.0
ADD_LAST = 27
RW_TILE = 4
RW_ACT = 11
PI_LOW = 3.1415925
TWO_PI = (6.28125, 0.0019350051879882812, float(2 * np.pi - 6.28125 - 0.0019350051879882812))

ORDER = [1, 2, 3, 0, 4, 5, 6, 7, 8]


def gemm_plan():
    plan = [("cs", s, i) for s in range(SG) for i in range(2)]

    def project(s):
        return ([("xt", s, i) for i in range(4)] + [(w, s, h) for h in range(2) for w in ("q", "k")]
                + [("v", s, i) for i in range(4)])

    def hidden(s):
        return [("x2t", s, i) for i in range(4)] + [("h", s, i) for i in range(FC)]

    def outer(s):
        return [("y", s, i) for i in range(2)]

    def back(s):
        return [("yt", s, i) for i in range(4)]

    plan += project(0) + [("u", s, i) for s in range(SG) for i in range(2)] + [("mask", 0, 0)]
    for s in range(SG):
        if s + 1 < SG:
            plan += project(s + 1)
        if s >= 1:
            plan += hidden(s - 1) + outer(s - 1)
        plan += [("o", s, i) for i in range(4)]
        if s >= 1:
            plan += back(s - 1)
    return plan + hidden(SG - 1) + outer(SG - 1) + back(SG - 1)


BY_ACT = ("cs", "xt", "v", "x2t", "h")


def build(nc, a, out):
    with ExitStack() as ctx:
        def sb(name, shape, dt=F32):
            return ctx.enter_context(nc.sbuf_tensor(name, shape, dt))

        def sem(name):
            return ctx.enter_context(nc.semaphore(name))

        ctx.enter_context(nc.allow_non_contiguous_dma(reason="short rows of the kernel and of constants"))

        h1_rows = nc.dram_tensor("h1_rows", [S * TOK, D], F32, kind="Internal").ap()

        h0 = sb("h0", [P, POS, D])
        work = sb("work", [P, 24576])
        wbuf = sb("wbuf", [P, 20 * D])
        wsm = wbuf[:, 0:8 * D].rearrange("p (w c d) -> p w c d", w=4, c=2)
        w2 = wbuf[:, 12 * D:20 * D].rearrange("p (f d) -> p f d", f=FC)
        w1 = sb("w1", [P, 2, FF])
        ident = sb("ident", [P, P])
        st = sb("st", [P, POS, 6])
        vec = sb("vec", [P, 8, POS])
        small = sb("small", [P, 224])
        s4in = sb("s4in", [P, 9, HF])
        s4v = sb("s4v", [P, 14, HF])
        s4c = sb("s4c", [P, 2 * FR + HG])
        dft = sb("dft", [FR, 2 * S + 1])
        drow = sb("drow", [1, D + S + P])
        rwb = sb("rwb", [P, D])
        w1f = w1[:, :, :].rearrange("p a b -> p (a b)")
        V_S, V_D, V_Q, V_W, V_R, V_B, V_A, V_Z = range(8)

        wf = work[:, :]
        hn = wf[:, 0:18432].bitcast(F16).rearrange("p (c l j d) -> p c l j d", c=NCH, l=2, j=CH)
        hn32 = wf[:, 0:18432].rearrange("p (c j d) -> p c j d", c=NCH, j=CH)
        rw_products = wf[:, 0:18432].rearrange("p (q d) -> p q d", q=POS)
        toep = wf[:, 18432:24576].bitcast(F16).rearrange("p (r t l c) -> p r t l c", r=TRING, t=P, l=2)
        stage = wbuf[:, 0:16 * D].bitcast(F16).rearrange("p (b x c) -> p b x c", b=UCH // TCH, c=TCH)
        img = wf[:, 18432:24576].rearrange("p (k n q) -> p k n q", k=KC, n=CH)
        wT = wsm[:, 0:3].rearrange("p a b d -> p (a b d)").rearrange("p (k d) -> p k d", k=KC)
        brow = wsm[:, 3, 0]
        posb = w2
        t32_even = w1f.rearrange("p (j d) -> p j d", j=CH)

        def sil(n):
            return w1f[:, (n % SIL) * GRP * POS:(n % SIL + 1) * GRP * POS]

        late = h0[:, 5 * CH:POS].rearrange("p j d -> p (j d)")
        rhsA = late[:, 0:2048].rearrange("p (f c e) -> p f c e", f=HF, c=8)
        rhsB = late[:, 2048:4096].rearrange("p (f c e) -> p f c e", f=HF, c=8)
        NE = HF * FR
        er, ei, iv = (late[:, 4096 + i * NE:4096 + (i + 1) * NE].rearrange("p (f m) -> p f m", m=FR) for i in range(3))
        t1 = w1f[:, 0:NE].rearrange("p (f m) -> p f m", m=FR)
        qs = late[0:FR, 0:2048].rearrange("p (f c e) -> p c f e", f=HF, c=8)
        gt = late[0:FR, 2048:4096].rearrange("p (c f e) -> p c f e", c=8, f=HF)
        ksb = late[0:S, 4096:4352]
        kneg = late[0:S, 4352:4608]
        kp = s4in[0:S].rearrange("p a b -> p (a b)")[:, 0:D].bitcast(F16).rearrange("p (l c) -> p l c", l=2)
        pick = vec[0:S, V_Z, 0:S].bitcast(F16)

        h1s = wf[:, 0:4096].rearrange("p (q d) -> p q d", q=NQ)
        gs = wf[:, 4096:8192].rearrange("p (q d) -> p q d", q=NQ)
        xT = wf[:, 8192:9216].rearrange("p (c n) -> p c n", c=2)
        diag1 = wf[:, 11808:12320].rearrange("p (b d) -> p b d", b=4)
        diag2 = wf[:, 9728:10240].rearrange("p (b d) -> p b d", b=4)
        tab = wf[:, 8192:10240].rearrange("p (k b f n) -> p k b f n", k=2, b=NBB, f=2)
        qT = wf[:, 10240:11264].rearrange("p (h t i) -> p h t i", h=2, t=SQ)
        kT = wf[:, 11264:11808].rearrange("p (h t i) -> p h t i", h=2, t=SQ)
        tmp = wf[:, 12352:12896].rearrange("p (b n) -> p b n", b=2)
        cs = wf[:, 12896:15072].rearrange("p (f n) -> p f n", f=2)
        su = wf[:, 15072:19424].rearrange("p (x n) -> p x n", x=4)
        pr = wf[:, 15072:17120].rearrange("p (q c i) -> p q c i", q=4, c=2 * HP)
        prT = wf[:, 17120:19168].rearrange("p (q c i) -> p q c i", q=4, c=2 * HP)
        vv = wf[:, 19424:21472].rearrange("p (b q d) -> p b q d", b=2, q=4)
        oT = wf[:, 21472:22496].rearrange("p (q h b i) -> p q h b i", q=4, h=2, b=4)
        x1 = wf[:, 22496:24544].rearrange("p (b q d) -> p b q d", b=2, q=4)
        am = wf[:, 22496:23648].rearrange("p (k b n) -> p k b n", k=2, b=NBB)
        tk = wf[0:S, 4096:8192].rearrange("p (x n) -> p x n", n=256)
        rp = wbuf[:, 16 * D:18 * D].rearrange("p (x n) -> p x n", n=P)
        dg = wf[0:S, 19424:19968].bitcast(BF16).rearrange("p (t i) -> p t i", t=S)
        ones_b = wf[0:S, 19968:20032].bitcast(BF16)
        hT = h0[:, 0:9].rearrange("p j d -> p (j d)")[:, 0:FC * NC].rearrange("p (f n) -> p f n", f=FC)
        yT = h0[:, 12:16].rearrange("p j d -> p (j d)").rearrange("p (h t i) -> p h t i", h=2, t=SQ)
        x2T = h0[:, 16:20].rearrange("p j d -> p (j d)").rearrange("p (c n) -> p c n", c=2)
        def key_place(x):
            return x[:, 0:HP * NC].rearrange("p (t e i) -> p t e i", t=SQ, e=HP)

        kx_first = [key_place(wbuf[:, 8 * D:20 * D]),
                    key_place(h0[:, 0:9].rearrange("p j d -> p (j d)"))]
        kx_later = [key_place(h0[:, j:j + 9].rearrange("p j d -> p (j d)")) for j in (24, 33)]
        msk = s4in[:, :, :].rearrange("p a b -> p (a b)")[:, 0:NQ * KSEL].rearrange("p (q k) -> p q k", q=NQ)

        cols = {}

        def col(name, n=1):
            if name not in cols:
                cols[name] = sum(w for _, w in cols.values()), n
            o, w = cols[name]
            assert o + w <= 32
            return small[:, o:o + w]

        eps_ln, eps_rms, amax, kscale, yscale, am64, am1 = (
            col(x) for x in ("eps_ln", "eps_rms", "amax", "kscale", "yscale", "am64", "am1"))
        cst = col("cst", 5)
        own_head = col("own_head", HP)
        rbias = col("rbias")
        lnw = col("lnw", 4)
        srw = col("srw")
        idxg = small[:, 32:48].bitcast(U32)
        idxs = small[:, 48:64].bitcast(U32)
        notm = small[:, 64:80]
        wsel = small[:, 80:96]
        r1 = small[:, 96:112]
        sm, sd, sq_, rr, nb = (small[:, 112 + 16 * i:128 + 16 * i] for i in range(5))
        st_first = s4v[:, :, :].rearrange("p a b -> p (a b)")[:, 0:POS * 6].rearrange("p (q x) -> p q x", x=6)
        rinv = s4v[:, 0:2, :].rearrange("p a b -> p (a b)")
        mx = s4v[:, 2:4, :].rearrange("p a b -> p (a b)")
        st2 = s4v[:, 4:7, :].rearrange("p a b -> p (a b)").rearrange("p (q x) -> p q x", x=6)
        ssq = s4v[:, 7, 0:16]
        ssq2 = s4v[:, 7, 16:32]
        rms1 = s4v[:, 9, 0:16]
        rms2 = s4v[:, 8, 0:16]
        rr2 = s4v[:, 8, 16:32]
        posi = small[:, 192:200].bitcast(I32)
        invf = small[:, 200:216]
        base = s4in[0:S].rearrange("p a b -> p (a b)")[:, 0:TOK]
        c_c, c_s, c_e = s4c[:, 0:FR], s4c[:, FR:2 * FR], s4c[:, 2 * FR:]

        psum = ctx.enter_context(nc.psum_tensor("psum", [P, 8, 512], F32))

        names = """const s4in rope img pos khl act_s4 dve x rhs q g k am amt amb emb embv var std nrm t32 hi lo
            tz rwprod rwdot conv built tba tbv sil addv addp wload w1load w2load wready amz mload var3 std3 rows w72 wmov idx idxp idxr ind seldg
            oh
            tabf tabs tab tokload
            rvar rstd g1 ssq rms1 rms1r gemm evv eva qk keys kx ownf own sc pin pexp pt pv ot ssq2 rms2 rms2r
            hrow h2row fin outc outd outd01 mbank h1out poolw""".split()
        s = {n: sem("s_" + n) for n in names}
        s_txt = [sem(f"s_txt{c}") for c in range(NCH)]
        s_scat = [sem(f"s_scat{g}") for g in range(SG)]
        s_gath = [sem(f"s_gath{q}") for q in range(NQ)]

        plan = gemm_plan()
        use_of = {u: n for n, u in enumerate(plan)}
        emptied = []
        for n, (what, _, _) in enumerate(plan):
            by = what in BY_ACT
            emptied.append((by, 1 + sum(1 for b, _ in emptied if b == by)))

        s_toep = [sem(f"s_toep{r}") for r in range(TRING)]
        toep_emptied = []
        for m in range(NU * NB):
            by = "tbv" if (m % 3 == 2 if m < 2 * NB else m % 2) else "tba"
            toep_emptied.append((by, 1 + sum(1 for b, _ in toep_emptied if b == by)))

        def later_builds(n):
            m = 2 * NB + 2 * (n - 4)
            return (m, m + 1) if 2 * NB <= m < NU * NB else ()

        def early_builds(n, by):
            return [m for m in range(max(0, 6 * (n - 3)), min(6 * (n - 2), 2 * NB)) if toep_emptied[m][0] == by]

        def unit_kept(eng, u):
            for by in ("tba", "tbv"):
                count = max([c for b, c in toep_emptied[:(u + 1) * NB] if b == by] + [0])
                if count:
                    eng.wait_ge(s[by], count)

        def placed(eng, n):
            eng.wait_ge(s_toep[n % TRING], 32 * (n // TRING + 1))

        def keep_toep(eng, copy, m):
            u, k = divmod(m, NB)
            if u >= 2 and k < 2:
                for n in range(4 * (u - 2) + 1, 4 * (u - 2) + 4):
                    placed(eng, n)
            eng.wait_ge(s["built"], m + 1)
            h = slice(64 * (u % 2), 64 * (u % 2) + 64)
            copy(stage[h, :, k * 2 * QT:(k + 1) * 2 * QT, :].rearrange("p b x c -> p x b c"),
                 psum[h, 4 + m % 4, :].rearrange("p (x b c) -> p x b c", b=UCH // TCH, c=TCH)).then_inc(s[toep_emptied[m][0]], 1)

        def bank(u):
            return psum[:, 4 + use_of[u] % 4, :]

        def embedded(j):
            b = j // 2 if j < 4 else 2 + j // 2
            return psum[:, b, j % 2 * D:j % 2 * D + D]

        def pos_of(c):
            return slice(c * CH, c * CH + CH)

        def t32(n):
            return t32_even if n % 2 == 0 else hn32[:, ORDER[-1]]

        junk_v = st[:, :, :].rearrange("p a b -> p (a b)")[:, 0:D]

        def spread(eng, scaled, g, h):
            kx = kx_later if g else kx_first
            for e in range(HP):
                ins = scaled(kx[h][:, :, e, :], kT[:, h], own_head[:, e:e + 1])
            return ins

        adder = ["addp" if n % 2 and n < ADD_LAST else "addv" for n in range(NGRP)]

        def added(eng, n):
            for by in ("addv", "addp"):
                if by in adder[:n]:
                    eng.wait_ge(s[by], adder[:n].count(by))

        def rows_out(eng):
            eng.wait_ge(s["outd01"], 2 * 32)
            eng.wait_ge(s["outd"], (NCH - 2) * 32)

        def row1(x, n):
            return x.rearrange("p (o d) -> p o d", o=1).to_broadcast([x.shape[0], n, x.shape[1]])

        def col1(x, n):
            return x.rearrange("p (f o) -> p f o", o=1).to_broadcast([x.shape[0], x.shape[1], n])

        def add_group(eng, n):
            x = h0[:, :, n * GRP:(n + 1) * GRP]
            return eng.tensor_tensor(x, x, sil(n).rearrange("p (c j) -> p j c", c=GRP), ALU.add)

        block = ctx.enter_context(nc.Block())

        @block.sync
        def _(sp):
            sp.dma_start(s4in[:, :, :], a["s4in"]).then_inc(s["s4in"], 16)
            sp.dma_start(s4c[:, :], a["s4c"]).then_inc(s["s4in"], 16)
            for dst, name in ((dft[:, :], "dft"), (drow[:, :], "drow"), (ident[:, :], "ident"), (cst, "cst"),
                              (lnw, "lnw"), (own_head, "own_head"), (pick, "pick")):
                sp.dma_start(dst, a[name]).then_inc(s["const"], 16)
            sp.dma_start(rwb[:, :], a["rw"].rearrange("d o -> o d").to_broadcast([P, D])).then_inc(s["const"], 16)
            sp.dma_start(rbias, a["rb"].rearrange("(o d) -> o d", o=1).to_broadcast([P, 1])).then_inc(s["const"], 16)
            sp.dma_start(posi, a["posT"]).then_inc(s["rope"], 16)
            sp.dma_start(invf, a["invf"]).then_inc(s["rope"], 16)

            def text(c):
                for g in range(2):
                    lo = (c - 1) * CH + 64 * g
                    sp.dma_start(h0[64 * g:64 * g + 64, pos_of(c), :], a["txt"][:, lo:lo + CH, :]).then_inc(s_txt[c], 16)

            text(1)
            sp.dma_start(wT, a["wT"]).then_inc(s["img"], 16)
            sp.dma_start(img, a["img"]).then_inc(s["img"], 16)
            for g in range(2):
                sp.dma_start(posb[64 * g:64 * g + 64, :, :],
                             a["pos_emb"][g * 8:g * 8 + 8, :].rearrange("(o n) d -> o n d", o=1).to_broadcast([64, 8, D])
                             ).then_inc(s["pos"], 16)
            sp.dma_start(brow, a["b"].rearrange("(o d) -> o d", o=1).to_broadcast([P, D])).then_inc(s["pos"], 16)
            for c in range(2, 5):
                text(c)
            sp.wait_ge(s["khl"], 1)
            for c in range(5, 9):
                text(c)
            sp.wait_ge(s["tz"], 2)
            for n in range(NT):
                u, k = divmod(n, UCH // TCH)
                if k == 0:
                    unit_kept(sp, u)
                if n >= TRING:
                    sp.wait_ge(s["conv"], TCH // GRP * (n - TRING + 1))
                for g in range(2):
                    h = slice(64 * (u % 2), 64 * (u % 2) + 64)
                    sp.dma_start(toep[64 * g:64 * g + 64, n % TRING, 64 * g:64 * g + 64],
                                 stage[h, k].rearrange("p (t l) c -> p t l c", l=2)).then_inc(s_toep[n % TRING], 16)
            rows = h1_rows.rearrange("(s t) d -> s t d", t=TOK)
            for half in range(2):
                d = slice(half * D // 2, (half + 1) * D // 2)
                added(sp, NGRP // 2 * (half + 1))
                for g in range(2):
                    h = slice(64 * g, 64 * g + 64)
                    sp.dma_start(rows[:, 8 * g:8 * g + 8, d], h0[h, 0:8, d]).then_inc(s["h1out"], 16)
                    sp.dma_start(rows[:, 16 + 64 * g:80 + 64 * g, d], h0[h, 8:POS, d]).then_inc(s["h1out"], 16)
                if half == 0:
                    for n in range(NT - TRING, NT):
                        placed(sp, n)
                    for i, w in enumerate(("wq", "wk", "wv", "wo")):
                        sp.dma_start(wsm[:, i], a[w].rearrange("(c p) d -> p c d", p=P)).then_inc(s["wload"], 16)
                    sp.wait_ge(s["built"], NU * NB)
                    sp.dma_start(base, a["base"]).then_inc(s["tokload"], 16)
            sp.wait_ge(s["tab"], 1)
            sp.dma_start(w1[:, :, :], a["w1"].rearrange("(c p) f -> p c f", p=P)).then_inc(s["w1load"], 16)
            sp.wait_ge(s["amz"], 1)
            sp.dma_start(am[:, 0], a["mask"][:, 0:P, :].rearrange("b j n -> j b n")).then_inc(s["mload"], 16)
            sp.dma_start(am[0:TOK - P, 1], a["mask"][:, P:TOK, :].rearrange("b j n -> j b n")).then_inc(s["mload"], 16)
            for c in range(NCH):
                sp.wait_ge(s["outc"], c + 1)
                for g in range(2):
                    lo = 8 * g if c == 0 else 16 + 64 * g + (c - 1) * CH
                    sp.dma_start(out[:, lo:lo + CH, :], h0[64 * g:64 * g + 64, pos_of(c), :]
                                 ).then_inc(s["outd01" if c < 2 else "outd"], 16)
            sp.wait_ge(s["sc"], 1)
            sp.dma_start(w2, a["w2"].rearrange("(c p) d -> p c d", p=P)).then_inc(s["w2load"], 16)
            rows_out(sp)

        @block.tensor
        def _(pe):
            mm = pe.matmul
            pe.wait_ge(s["x"], 1)
            pe.wait_ge(s["rhs"], 1)
            for f in range(HF):
                o = psum[0:FR, 4 + f // 8, (f % 8) * 64:(f % 8) * 64 + 64]
                mm(o, er[:, f, :], rhsA[:, f].rearrange("p c e -> p (c e)"), start=True, stop=False)
                ins = mm(o, ei[:, f, :], rhsB[:, f].rearrange("p c e -> p (c e)"), start=False, stop=True)
            ins.then_inc(s["q"], 1)

            def embed(j):
                for k in range(KC):
                    ins = mm(embedded(j), img[:, k, j, :], wT[:, k, :], start=(k == 0), stop=(k == KC - 1))
                if j % 2:
                    ins.then_inc(s["emb"], 1)

            pe.wait_ge(s["img"], 32)
            for j in range(4):
                embed(j)
            pe.wait_ge(s["const"], 144)
            pe.wait_ge(s["g"], 1)
            mm(psum[0:S, 2, 0:D], dft[:, 0:S], gt[:, 0].rearrange("p f e -> p (f e)"), start=True, stop=False)
            mm(psum[0:S, 2, 0:D], dft[:, S:2 * S], gt[:, 2].rearrange("p f e -> p (f e)"), start=False, stop=False)
            mm(psum[0:S, 2, 0:D], drow[:, D:D + S], drow[:, 0:D], start=False, stop=True).then_inc(s["k"], 1)
            pe.wait_ge(s["am"], 1)
            pe.transpose(psum[0:1, 3, 0:S], am64[0:S], ident[0:S, 0:S]).then_inc(s["amt"], 1)
            pe.wait_ge(s["am"], 2)
            mm(psum[:, 3, 128:129], drow[:, D + S:], am1[0:1], start=True, stop=True).then_inc(s["amt"], 1)
            for j in range(4, CH):
                embed(j)
            pe.wait_ge(s["khl"], 1)

            def build(m):
                if m >= 4:
                    by, count = toep_emptied[m - 4]
                    pe.wait_ge(s[by], count)
                elif m == 0:
                    pe.wait_ge(s["embv"], CH // 2)
                u, k = divmod(m, NB)
                for i in range(QT):
                    t = k * QT + i
                    ins = mm(psum[64 * (u % 2):64 * (u % 2) + 64, 4 + m % 4, i * 2 * UCH:(i + 1) * 2 * UCH],
                             pick[:, S - 1 - t:2 * S - 1 - t], kp[:, :, u * UCH:(u + 1) * UCH], start=True, stop=True)
                ins.then_inc(s["built"], 1)

            for m in range(2 * NB):
                build(m)
            pe.wait_ge(s["hi"], NCH)
            pe.wait_ge(s["lo"], NCH)
            pe.wait_ge(s["amb"], 1)
            for n in range(NGRP):
                e, r = divmod(n, TCH // GRP)
                if r == 0:
                    placed(pe, e)
                if n >= CSLOT:
                    pe.wait_ge(s["sil"], n - CSLOT + 1)
                for i in range(GRP):
                    ch = n * GRP + i
                    o = psum[:, 2 * (n % CSLOT) + i // 4, (i % 4) * POS:(i % 4 + 1) * POS]
                    t_hi, t_lo = (toep[:, e % TRING, :, l, ch % TCH] for l in range(2))
                    x_hi, x_lo = (hn[:, :, l, :, ch] for l in range(2))
                    mm(o, t_hi, x_hi, start=True, stop=False)
                    mm(o, t_hi, x_lo, start=False, stop=False)
                    ins = mm(o, t_lo, x_hi, start=False, stop=True)
                ins.then_inc(s["conv"], 1)
                for m in later_builds(n):
                    build(m)

            pe.wait_ge(s["w72"], 1)
            pe.wait_ge(s["sil"], NGRP)
            for g in range(2):
                ins = mm(psum[0:S, 0, g * POS:(g + 1) * POS], ident[:, 64 * g:64 * g + 64], vec[:, V_W, :], start=True, stop=True)
            ins.then_inc(s["wmov"], 1)
            for _ in range(IDLE_PRODUCTS):
                mm(psum[:, 4, 0:D], ident[:, :], rwb[:, :], start=True, stop=True)
            pe.wait_ge(s["idx"], 1)
            for x in range(3):
                for b in range(4):
                    ins = mm(psum[32 * b:32 * b + 32, 1, x * NQ:(x + 1) * NQ], tk[:, 10 + x, 0:SLOT], ident[0:S, b:S:4],
                             start=True, stop=True)
            ins.then_inc(s["idxp"], 1)
            for b in range(SG):
                pe.wait_ge(s["seldg"], b + 1)
                mm(psum[:, TOKEN_BANK[b], 0:NC], ones_b, dg[:, SQ * b:SQ * b + SQ, :].rearrange("p t i -> p (t i)"),
                   start=True, stop=True).then_inc(s["ind"], 1)

            def begin(u):
                n = use_of[u]
                if n >= 4:
                    by, count = emptied[n - 4]
                    pe.wait_ge(s["eva"] if by else s["evv"], count)
                return bank(u)

            pe.wait_ge(s["tab"], 1)
            parts = [(bb * KSEL, (bb + 1) * KSEL, bb) for bb in range(NBB - 1)]
            for g in range(SG):
                pe.wait_ge(s["oh"], g + 1)
                for i in range(2):
                    o = begin(("cs", g, i))
                    for lo, hi, bb in (parts + [(3 * KSEL, NC, 3)] if g == 0 else [(0, NC, 3)]):
                        c = slice(g * NC + lo, g * NC + hi)
                        mm(o[:, lo:hi], tab[:, 0, bb, i, :], su[:, 0, c], start=True, stop=False)
                        ins = mm(o[:, lo:hi], tab[:, 1, bb, i, :], su[:, 1, c], start=False, stop=True)
                    ins.then_inc(s["gemm"], 1)

            def masks():
                pe.wait_ge(s["mload"], 32)
                for g in range(SG):
                    for i in range(2):
                        o = begin(("u", g, i))
                        rows = P if i == 0 else TOK - P
                        for lo, hi, bb in (parts + [(3 * KSEL, NC, 3)] if g == 0 else [(0, NC, 3)]):
                            c = slice(g * NC + lo, g * NC + hi)
                            mm(o[0:rows, lo:hi], am[:, 0, bb, P * i:P * i + rows], su[:, 0, c], start=True, stop=False)
                            ins = mm(o[0:rows, lo:hi], am[:, 1, bb, P * i:P * i + rows], su[:, 1, c], start=False, stop=True)
                        ins.then_inc(s["gemm"], 1)
                o = begin(("mask", 0, 0))
                pe.wait_ge(s["mbank"], 1)
                pe.wait_ge(s["evv"], emptied[use_of[("u", SG - 1, 1)]][1])
                for t in range(S):
                    c = slice(t * KSEL, (t + 1) * KSEL)
                    b, q = t % 4, t // 4
                    mm(o[32 * b:32 * b + KSEL, q * KSEL:(q + 1) * KSEL], su[:, 2, c], su[:, 0, c], start=True, stop=False)
                    ins = mm(o[32 * b:32 * b + KSEL, q * KSEL:(q + 1) * KSEL], su[0:16, 3, c], su[0:16, 1, c], start=False, stop=True)
                ins.then_inc(s["gemm"], 1)

            def project(g):
                for i in range(4):
                    o = begin(("xt", g, i))
                    pe.wait_ge(s["hrow"], 4 * g + i + 1)
                    for c in range(2):
                        ins = mm(o[:, c * P:(c + 1) * P], gs[:, 4 * g + i, c * P:(c + 1) * P], diag1[:, i], start=True, stop=True)
                    ins.then_inc(s["gemm"], 1)
                pe.wait_ge(s["eva"], emptied[use_of[("xt", g, 3)]][1])
                if g == 0:
                    pe.wait_ge(s["wready"], 1)
                for h in range(2):
                    for w, name in ((0, "q"), (1, "k")):
                        o = begin((name, g, h))
                        for c in range(2):
                            x = xT[:, c, :].rearrange("p (t i) -> p t i", i=SLOT)[:, :, 0:KSEL]
                            ins = mm(o[:, 0:NC], wsm[:, w, c, h * P:(h + 1) * P], x, start=(c == 0), stop=(c == 1))
                        ins.then_inc(s["gemm"], 1)

            def values(g):
                for i in range(4):
                    o = begin(("v", g, i))
                    for c in range(2):
                        ins = mm(o[:, 0:D], xT[:, c, i * P:(i + 1) * P], wsm[:, 2, c, :], start=(c == 0), stop=(c == 1))
                    ins.then_inc(s["gemm"], 1)

            def scores(g):
                pe.wait_ge(s["qk"], 2 * (g + 1))
                pe.wait_ge(s["kx"], 2 * (g + 1))
                kx = kx_later if g else kx_first
                if g >= 1:
                    pe.wait_ge(s["ot"], g)
                for q in range(4):
                    for h in range(2):
                        for b in range(4):
                            t = 4 * q + b
                            ins = mm(psum[32 * b:32 * b + 32, q, h * HP * KSEL:(h + 1) * HP * KSEL], qT[:, h, t, :],
                                     kx[h][:, t].rearrange("p e i -> p (e i)"), start=True, stop=True)
                ins.then_inc(s["sc"], 1)

            def attend(g):
                pe.wait_ge(s["eva"], emptied[use_of[("v", g, 3)]][1])
                for q in range(4):
                    if q % 2 == 0:
                        pe.wait_ge(s["pt"], 2 * g + 1 + q // 2)
                    for h in range(2):
                        for b in range(4):
                            for r in range(4):
                                ins = mm(psum[32 * r:32 * r + 32, b, (2 * q + h) * 34:(2 * q + h) * 34 + 34],
                                         vv[32 * b:32 * b + KSEL, g % 2, q, h * P + 32 * r:h * P + 32 * r + 32],
                                         prT[32 * b:32 * b + KSEL, q, HP * h + 2 * r:HP * h + 2 * r + 2, 0:KSEL],
                                         start=True, stop=True)
                    if q == 3:
                        ins.then_inc(s["pv"], 1)
                    elif g >= 1:
                        outer(g - 1, 0, 3 * q, min(3 * q + 3, FC))

            def merge(g):
                pe.wait_ge(s["ot"], g + 1)
                for i in range(4):
                    o = begin(("o", g, i))
                    for h in range(2):
                        ins = mm(o[:, 0:D], oT[:, i, h].rearrange("p b i -> p (b i)"), wsm[:, 3, h, :],
                                 start=(h == 0), stop=(h == 1))
                    ins.then_inc(s["gemm"], 1)

            def hidden(g):
                for i in range(4):
                    o = begin(("x2t", g, i))
                    pe.wait_ge(s["h2row"], 4 * g + i + 1)
                    for c in range(2):
                        ins = mm(o[:, c * P:(c + 1) * P], x1[:, g % 2, i, c * P:(c + 1) * P], diag2[:, i], start=True, stop=True)
                    ins.then_inc(s["gemm"], 1)
                pe.wait_ge(s["eva"], emptied[use_of[("x2t", g, 3)]][1])
                if g == 0:
                    pe.wait_ge(s["wready"], 2)
                for f in range(FC):
                    o = begin(("h", g, f))
                    for c in range(2):
                        x = x2T[:, c, :].rearrange("p (t i) -> p t i", i=SLOT)[:, :, 0:KSEL]
                        ins = mm(o[:, 0:NC], w1[:, c, f * P:(f + 1) * P], x, start=(c == 0), stop=(c == 1))
                    ins.then_inc(s["gemm"], 1)

            def outer(g, h, first, last):
                if g == 0 and h == 0 and first == 0:
                    pe.wait_ge(s["w2load"], 16)
                o = begin(("y", g, h)) if first == 0 else bank(("y", g, h))
                for f in range(first, last):
                    if h == 0:
                        pe.wait_ge(s["eva"], emptied[use_of[("h", g, f)]][1])
                    ins = mm(o[:, 0:NC], w2[:, f, h * P:(h + 1) * P], hT[:, f, :], start=(f == 0), stop=(f == FC - 1))
                if last == FC:
                    ins.then_inc(s["gemm"], 1)

            def back(g):
                pe.wait_ge(s["evv"], emptied[use_of[("y", g, 1)]][1])
                for i in range(4):
                    o = begin(("yt", g, i))
                    for h in range(2):
                        ins = pe.transpose(o[:, h * P:(h + 1) * P], yT[:, h, 4 * i:4 * i + 4, :].rearrange("p t i -> p (t i)"),
                                           ident[:, :])
                    ins.then_inc(s["gemm"], 1)

            project(0)
            values(0)
            masks()
            for g in range(SG):
                scores(g)
                if g + 1 < SG:
                    project(g + 1)
                    if g >= 1:
                        values(g + 1)
                if g >= 1:
                    hidden(g - 1)
                attend(g)
                if g == 0:
                    values(g + 1)
                if g >= 1:
                    outer(g - 1, 1, 0, FC)
                merge(g)
                if g >= 1:
                    back(g - 1)
            hidden(SG - 1)
            for h in range(2):
                outer(SG - 1, h, 0, FC)
            back(SG - 1)

        @block.scalar
        def _(act):
            fn = act.activation
            act.wait_ge(s["s4in"], 32)
            fn(s4v[:, 0, :], s4in[:, 0, :], ACT.Exp).then_inc(s["act_s4"], 1)
            fn(s4v[:, 1, :], s4in[:, 1, :], ACT.Exp).then_inc(s["act_s4"], 1)

            def deviations(n):
                p = pos_of(ORDER[n])
                act.wait_ge(s["var"], n + 1)
                fn(vec[:, V_D, p], vec[:, V_Q, p], ACT.Sqrt, bias=eps_ln, scale=1.0 / D).then_inc(s["std"], 1)

            deviations(0)
            for n, c in enumerate(ORDER):
                if n + 1 < NCH:
                    deviations(n + 1)
                act.wait_ge(s["nrm"], n + 1)
                if n == NCH - 1:
                    act.wait_ge(s["lo"], n)
                for j in range(CH):
                    q = c * CH + j
                    ins = fn(hn[:, c, 0, j, :], h0[:, q, :], ACT.Identity, bias=vec[:, V_B, q:q + 1], scale=vec[:, V_R, q:q + 1])
                ins.then_inc(s["hi"], 1)
                for m in early_builds(n, "tba"):
                    keep_toep(act, act.copy, m)
            act.wait_ge(s["tabf"], 1)
            fn(rp[:, 2], rp[:, 2], ACT.Sin)
            for k, sign in enumerate((-1.0, 1.0)):
                x = rp[:, 3].rearrange("p (x d) -> p x d", d=HD)[:, :, k * 8:k * 8 + 8]
                ins = fn(x, x, ACT.Sin, scale=sign)
            ins.then_inc(s["tabs"], 1)
            act.wait_ge(s["lo"], NCH)
            for n in range(NGRP):
                act.wait_ge(s["conv"], n + 1)
                if n >= SIL:
                    added(act, n - SIL + 1)
                k = 2 * (n % CSLOT)
                fn(sil(n).rearrange("p (b x) -> p b x", b=2), psum[:, k:k + 2, 0:4 * POS], ACT.Silu, scale=yscale
                   ).then_inc(s["sil"], 1)
                for m in later_builds(n)[0:1]:
                    keep_toep(act, act.copy, m)
            for x in range(RW_ACT):
                act.wait_ge(s["rwprod"], x + 1)
                for q in range(x * RW_TILE, (x + 1) * RW_TILE):
                    ins = fn(rw_products[:, q, :], rw_products[:, q, :], ACT.Identity, accum_out=vec[:, V_W, q:q + 1])
            ins.then_inc(s["rwdot"], 1)
            act.wait_ge(s["var3"], 1)
            fn(vec[:, V_D, :], vec[:, V_Q, :], ACT.Sqrt, bias=eps_ln, scale=1.0 / D).then_inc(s["std3"], 1)

            def routed_deviations(g):
                q4 = slice(4 * g, 4 * g + 4)
                act.wait_ge(s["rvar"], g + 1)
                fn(sd[:, q4], sq_[:, q4], ACT.Sqrt, bias=eps_ln, scale=1.0 / D).then_inc(s["rstd"], 1)

            def routed(g):
                q4 = slice(4 * g, 4 * g + 4)
                act.wait_ge(s["ssq"], g + 1)
                fn(rms1[:, q4], ssq[:, q4], ACT.Sqrt, bias=eps_rms, scale=1.0 / D).then_inc(s["rms1"], 1)
                act.wait_ge(s["rows"], g + 1)
                for q in range(4 * g, 4 * g + 4):
                    fn(gs[:, q], h1s[:, q], ACT.Identity, bias=nb[:, q:q + 1], scale=rr[:, q:q + 1]).then_inc(s["g1"], 1)

            def empty(u, dst, src, func=ACT.Copy):
                act.wait_ge(s["gemm"], use_of[u] + 1)
                fn(dst, src, func).then_inc(s["eva"], 1)

            def rope_columns(g):
                for i in range(2):
                    empty(("cs", g, i), cs[:, i, g * NC:(g + 1) * NC], bank(("cs", g, i))[:, 0:NC])

            def first_diagonals(g):
                act.wait_ge(s["rms1r"], g + 1)
                if g >= 1:
                    act.wait_ge(s["gemm"], use_of[("xt", g - 1, 3)] + 1)
                for i in range(4):
                    fn(diag1[:, i], ident[:, :], ACT.Copy, scale=r1[:, 4 * g + i:4 * g + i + 1]).then_inc(s["hrow"], 1)

            def project(g):
                if g == 0:
                    act.wait_ge(s["eva"], emptied[use_of[("cs", SG - 1, 1)]][1])
                else:
                    first_diagonals(g)
                for i in range(4):
                    turn(g, i)

            def values(g):
                for i in range(4):
                    if g >= 2:
                        act.wait_ge(s["pv"], g - 1)
                    empty(("v", g, i), vv[:, g % 2, i], bank(("v", g, i))[:, 0:D])

            def spread_keys(g):
                if g >= 1:
                    act.wait_ge(s["sc"], g)
                    if g == 1:
                        rows_out(act)
                else:
                    act.wait_ge(s["outd01"], 2 * 32)
                act.wait_ge(s["keys"], 2 * (g + 1))
                spread(act, lambda o, x, f: fn(o, x, ACT.Copy, scale=f), g, 1).then_inc(s["kx"], 1)

            def turn(g, i):
                if g >= 1:
                    act.wait_ge(s["gemm"], use_of[("v", g - 1, 3)] + 1)
                empty(("xt", g, i), xT[:, :, i * P:(i + 1) * P], bank(("xt", g, i))[:, 0:2 * P].rearrange("p (c n) -> p c n", c=2))

            def second_rms(g):
                q4 = slice(4 * g, 4 * g + 4)
                act.wait_ge(s["ssq2"], 4 * g + 4)
                fn(rms2[:, q4], ssq2[:, q4], ACT.Sqrt, bias=eps_rms, scale=1.0 / D).then_inc(s["rms2"], 1)

            def second_diagonals(g):
                act.wait_ge(s["rms2r"], g + 1)
                if g >= 1:
                    act.wait_ge(s["gemm"], use_of[("x2t", g - 1, 3)] + 1)
                for i in range(4):
                    fn(diag2[:, i], ident[:, :], ACT.Copy, scale=rr2[:, 4 * g + i:4 * g + i + 1]).then_inc(s["h2row"], 1)

            def feed(g):
                for i in range(4):
                    if g >= 1:
                        act.wait_ge(s["gemm"], use_of[("h", g - 1, FC - 1)] + 1)
                    else:
                        rows_out(act)
                    empty(("x2t", g, i), x2T[:, :, i * P:(i + 1) * P],
                          bank(("x2t", g, i))[:, 0:2 * P].rearrange("p (c n) -> p c n", c=2))

            def hidden(g):
                for f in range(FC):
                    if g >= 1:
                        act.wait_ge(s["gemm"], use_of[("y", g - 1, 1)] + 1)
                    empty(("h", g, f), hT[:, f, :], bank(("h", g, f))[:, 0:NC], ACT.Gelu_apprx_tanh)

            def exps(g):
                act.wait_ge(s["pin"], g + 1)
                p3 = pr.rearrange("p q c i -> p (q c) i")[:, :, 0:KSEL]
                fn(p3, p3, ACT.Exp).then_inc(s["pexp"], 1)

            rope_columns(0)
            routed_deviations(0)
            routed(0)
            rope_columns(1)
            first_diagonals(0)
            rope_columns(2)
            rope_columns(3)
            routed_deviations(1)
            project(0)
            routed_deviations(2)
            routed_deviations(3)
            routed(1)
            values(0)
            spread_keys(0)
            routed(2)
            routed(3)
            for g in range(SG):
                if g >= 1:
                    second_diagonals(g - 1)
                if g + 1 < SG:
                    project(g + 1)
                    exps(g)
                    values(g + 1)
                    if g >= 1:
                        feed(g - 1)
                else:
                    feed(g - 1)
                    exps(g)
                if g + 1 < SG:
                    spread_keys(g + 1)
                if g >= 1:
                    hidden(g - 1)
                second_rms(g)
            second_diagonals(SG - 1)
            feed(SG - 1)
            hidden(SG - 1)

        @block.vector
        def _(v):
            done = [0]
            TT = v.tensor_tensor

            def link(ins):
                done[0] += 1
                ins.then_inc(s["dve"], 1)
                v.wait_ge(s["dve"], done[0])

            def moments(dst_s, dst_d, dst_q, x):
                TT(dst_s, x[:, :, 1], x[:, :, 4], ALU.add)
                TT(dst_q, x[:, :, 2], x[:, :, 5], ALU.add)
                link(TT(dst_d, x[:, :, 1], x[:, :, 4], ALU.subtract))
                link(v.scalar_tensor_tensor(dst_d, dst_d, D / 4.0, dst_d, ALU.mult, ALU.mult))
                return TT(dst_q, dst_q, dst_d, ALU.add)

            v.memset(eps_ln, LN_EPS)
            v.memset(eps_rms, RMS_EPS)
            v.wait_ge(s["s4in"], 32)
            v.wait_ge(s["act_s4"], 2)
            dt, ew, aw, bw = (s4v[:, i, :] for i in range(4))
            TT(aw, ew, dt, ALU.mult)
            link(TT(bw, s4in[:, 2, :], dt, ALU.mult))
            cb, sb_ = row1(c_c, HF), row1(c_s, HF)
            TT(er, col1(aw, FR), cb, ALU.mult)
            link(TT(t1, col1(bw, FR), cb, ALU.mult))
            link(TT(ei, sb_, t1, ALU.subtract))
            TT(iv, ei, ei, ALU.mult)
            link(TT(t1, er, er, ALU.mult))
            link(TT(iv, iv, t1, ALU.add))
            link(v.reciprocal(iv, iv))
            TT(er, er, iv, ALU.mult)
            TT(ei, ei, iv, ALU.mult).then_inc(s["x"], 1)
            v.wait_ge(s["pos"], 48)
            link(TT(posb[:, :, :], posb[:, :, :], row1(brow, 8), ALU.add))

            def kernel_spectrum():
                v.wait_ge(s["q"], 1)
                link(v.tensor_copy(late[0:FR, 0:2048], psum[0:FR, 4:8, :].rearrange("p b x -> p (b x)")))
                v.wait_ge(s["const"], 144)
                q = [qs[:, i] for i in range(8)]
                g = [gt[:, i] for i in range(8)]
                c = dft[:, 2 * S:2 * S + 1]
                TT(g[0], q[1], q[2], ALU.mult)
                TT(g[1], q[5], q[6], ALU.mult)
                TT(g[2], q[1], q[6], ALU.mult)
                link(TT(g[3], q[5], q[2], ALU.mult))
                TT(g[0], g[0], g[1], ALU.subtract)
                link(TT(g[2], g[2], g[3], ALU.add))
                v.tensor_scalar(g[0], g[0], c, None, ALU.mult)
                v.tensor_scalar(g[2], g[2], c, None, ALU.mult)
                v.tensor_scalar(g[4], q[3], c, 1.0, ALU.mult, ALU.add)
                link(v.tensor_scalar(g[5], q[7], c, None, ALU.mult))
                TT(g[6], g[4], g[4], ALU.mult)
                link(TT(g[7], g[5], g[5], ALU.mult))
                link(TT(g[6], g[6], g[7], ALU.add))
                link(v.reciprocal(g[6], g[6]))
                TT(g[1], g[0], g[4], ALU.mult)
                TT(g[3], g[2], g[5], ALU.mult)
                TT(g[7], g[2], g[4], ALU.mult)
                link(TT(g[0], g[0], g[5], ALU.mult))
                TT(g[1], g[1], g[3], ALU.add)
                link(TT(g[7], g[7], g[0], ALU.subtract))
                TT(g[1], g[1], g[6], ALU.mult)
                link(TT(g[7], g[7], g[6], ALU.mult))
                TT(g[0], q[0], g[1], ALU.subtract)
                link(TT(g[2], q[4], g[7], ALU.subtract))
                v.sem_inc(s["g"], 1)

            def kernel_parts():
                v.wait_ge(s["k"], 1)
                link(v.tensor_copy(ksb, psum[0:S, 2, 0:D]))
                link(v.tensor_scalar(kneg, ksb, -1.0, None, ALU.mult))
                link(TT(kneg, kneg, ksb, ALU.max))
                v.reduce_max(am64[0:S], kneg, AX).then_inc(s["am"], 1)
                v.wait_ge(s["amt"], 1)
                link(v.reduce_max(am1[0:1], psum[0:1, 3, 0:S], AX))
                v.tensor_scalar(am1[0:1], am1[0:1], 1e-30, None, ALU.max).then_inc(s["am"], 1)
                v.wait_ge(s["amt"], 2)
                link(v.tensor_copy(amax, psum[:, 3, 128:129]))
                v.tensor_scalar(yscale, amax, 1.0 / (T_PEAK * X_GAIN), None, ALU.mult).then_inc(s["amb"], 1)
                link(v.reciprocal(kscale, amax))
                link(v.tensor_scalar(kscale, kscale, T_PEAK, None, ALU.mult))
                link(v.tensor_scalar(ksb, ksb, kscale[0:S], None, ALU.mult))
                v.wait_ge(s["rhs"], 1)
                link(v.tensor_copy(kp[:, 0], ksb))
                link(TT(kp[:, 1], ksb, kp[:, 0], ALU.subtract))
                v.sem_inc(s["khl"], 1)

            def rope_angles():
                v.wait_ge(s["rope"], 32)
                v.wait_ge(s["embv"], CH // 2)
                for k in range(2):
                    ins = v.tensor_copy(rp[:, 0, k * 64:k * 64 + 64].rearrange("p (b d) -> p b d", b=NBB),
                                        col1(posi[:, k * NBB:(k + 1) * NBB], HD))
                link(ins)
                x = rp[:, 0].rearrange("p (x d) -> p x d", d=HD)
                link(TT(x, x, row1(invf, 8), ALU.mult))
                link(v.tensor_scalar(rp[:, 1], rp[:, 0], float(1 / (2 * np.pi)), 12582912.0, ALU.mult, ALU.add))
                link(v.tensor_scalar(rp[:, 1], rp[:, 1], -12582912.0, None, ALU.add))
                for part in TWO_PI:
                    link(v.scalar_tensor_tensor(rp[:, 0], rp[:, 1], -part, rp[:, 0], ALU.mult, ALU.add))
                link(v.tensor_scalar(rp[:, 2], rp[:, 0], float(np.pi / 2), None, ALU.add))
                link(v.tensor_scalar(rp[:, 1], rp[:, 2], float(np.pi), float(-2 * np.pi), ALU.is_gt, ALU.mult))
                link(TT(rp[:, 2], rp[:, 2], rp[:, 1], ALU.add))
                v.tensor_scalar(rp[:, 2], rp[:, 2], PI_LOW, -PI_LOW, ALU.min, ALU.max)
                link(v.tensor_scalar(rp[:, 3], rp[:, 0], PI_LOW, -PI_LOW, ALU.min, ALU.max))
                v.sem_inc(s["tabf"], 1)

            def normaliser(n):
                p = pos_of(ORDER[n])
                v.wait_ge(s["std"], n + 1)
                link(v.reciprocal(vec[:, V_R, p], vec[:, V_D, p]))
                link(v.tensor_scalar(vec[:, V_R, p], vec[:, V_R, p], X_GAIN, None, ALU.mult))
                v.scalar_tensor_tensor(vec[:, V_B, p], vec[:, V_S, p], -0.5, vec[:, V_R, p], ALU.mult, ALU.mult
                                       ).then_inc(s["nrm"], 1)

            def low_part(n):
                v.wait_ge(s["hi"], n + 1)
                v.wait_ge(s["t32"], n + 1)
                TT(hn[:, ORDER[n], 1], t32(n), hn[:, ORDER[n], 0], ALU.subtract).then_inc(s["lo"], 1)

            for n, c in enumerate(ORDER):
                if c == 0:
                    for i in range(CH // 2):
                        v.wait_ge(s["emb"], i + 1)
                        TT(h0[:, 2 * i:2 * i + 2, :].rearrange("p j d -> p (j d)"), psum[:, i if i < 2 else 2 + i, :],
                           posb[:, 2 * i:2 * i + 2, :].rearrange("p j d -> p (j d)"), ALU.add).then_inc(s["embv"], 1)
                    v.wait_ge(s["embv"], CH // 2)
                else:
                    v.wait_ge(s_txt[c], 32)
                for j in range(CH):
                    ins = v.bn_stats(st[:, c * CH + j, :], h0[:, c * CH + j, :])
                link(ins)
                p = pos_of(c)
                moments(vec[:, V_S, p], vec[:, V_D, p], vec[:, V_Q, p], st[:, p, :]).then_inc(s["var"], 1)
                if n >= 1:
                    normaliser(n - 1)
                if n >= 2:
                    low_part(n - 2)
                    for m in early_builds(n - 2, "tbv"):
                        keep_toep(v, v.tensor_copy, m)
                if n == 0:
                    kernel_spectrum()
                if n == 1:
                    kernel_parts()
                if n == 4:
                    rope_angles()
                    v.reduce_sum(srw, rwb[:, :], AX)
            normaliser(NCH - 1)
            for n in (NCH - 2, NCH - 1):
                low_part(n)
                for m in early_builds(n, "tbv"):
                    keep_toep(v, v.tensor_copy, m)
            for n in range(NGRP):
                if adder[n] == "addv":
                    v.wait_ge(s["sil"], n + 1)
                    add_group(v, n).then_inc(s["addv"], 1)
                for m in later_builds(n)[1:]:
                    keep_toep(v, v.tensor_copy, m)
                if n >= NGRP // 2:
                    if n == NGRP // 2:
                        added(v, NGRP // 2)
                    k = n - NGRP // 2
                    for q in range(k * POS // (NGRP // 2), (k + 1) * POS // (NGRP // 2)):
                        v.bn_stats(st_first[:, q, :], h0[:, q, 0:D // 2])
            added(v, NGRP)
            for q in range(POS):
                ins = v.bn_stats(st[:, q, :], h0[:, q, D // 2:D])
            link(ins)
            A, B, S1, Q1 = vec[:, V_A, :], vec[:, V_B, :], vec[:, V_S, :], vec[:, V_Q, :]
            d, w = vec[:, V_D, :], vec[:, V_R, :]
            fa, fb = st_first, st
            TT(A, fa[:, :, 1], fa[:, :, 4], ALU.add)
            TT(B, fb[:, :, 1], fb[:, :, 4], ALU.add)
            TT(Q1, fa[:, :, 2], fa[:, :, 5], ALU.add)
            TT(w, fb[:, :, 2], fb[:, :, 5], ALU.add)
            TT(d, fa[:, :, 1], fa[:, :, 4], ALU.subtract)
            link(TT(S1, fb[:, :, 1], fb[:, :, 4], ALU.subtract))
            TT(Q1, Q1, w, ALU.add)
            TT(d, d, d, ALU.mult)
            link(TT(S1, S1, S1, ALU.mult))
            TT(w, A, B, ALU.subtract)
            link(TT(d, d, S1, ALU.add))
            link(v.scalar_tensor_tensor(Q1, d, D / 8.0, Q1, ALU.mult, ALU.add))
            link(TT(d, w, w, ALU.mult))
            link(TT(S1, A, B, ALU.add))
            v.scalar_tensor_tensor(Q1, d, D / 16.0, Q1, ALU.mult, ALU.add).then_inc(s["var3"], 1)
            link(v.tensor_scalar(S1, S1, 0.5, None, ALU.mult))
            v.wait_ge(s["conv"], NGRP)
            v.memset(ones_b, 1.0)
            v.memset(am[:, 1].rearrange("p b n -> p (b n)"), 0.0).then_inc(s["amz"], 1)
            for q in range(RW_ACT * RW_TILE, POS):
                v.tensor_tensor_reduce(rw_products[:, q, :], h0[:, q, :], rwb[:, :], 1.0, 0.0, ALU.mult, ALU.add,
                                       vec[:, V_W, q:q + 1])
            v.wait_ge(s["rwdot"], 1)
            v.wait_ge(s["std3"], 1)
            link(v.reciprocal(vec[:, V_R, :], vec[:, V_D, :]))
            v.scalar_tensor_tensor(vec[:, V_B, :], vec[:, V_S, :], -0.5, vec[:, V_R, :], ALU.mult, ALU.mult)
            link(TT(vec[:, V_W, :], vec[:, V_W, :], vec[:, V_R, :], ALU.mult))
            link(v.scalar_tensor_tensor(vec[:, V_W, :], vec[:, V_B, :], srw, vec[:, V_W, :], ALU.mult, ALU.add))
            v.tensor_scalar(vec[:, V_W, :], vec[:, V_W, :], rbias, None, ALU.add).then_inc(s["w72"], 1)
            v.tensor_scalar(vec[:, V_A, :], vec[:, V_R, :], 1.0, None, ALU.add)
            W, W2, W3, gtm, eqm, pre, sel, key = (tk[:, i, 0:TOK] for i in range(8))
            m8 = tk[:, 9, 0:TOK]
            v.wait_ge(s["wmov"], 1)
            for g in range(2):
                v.tensor_copy(W[:, 8 * g:8 * g + 8], psum[0:S, 0, g * POS:g * POS + 8])
                ins = v.tensor_copy(W[:, 16 + 64 * g:80 + 64 * g], psum[0:S, 0, g * POS + 8:(g + 1) * POS])
            link(ins)

            def top24(x, y, z):
                link(v.max(m8[:, 0:8], x))
                link(v.match_replace(y, m8[:, 0:8], x, NEG))
                link(v.max(m8[:, 8:16], y))
                link(v.match_replace(z, m8[:, 8:16], y, NEG))
                link(v.max(m8[:, 16:24], z))

            top24(W, W2, W3)
            last, thr = m8[:, KSEL - 1:KSEL], m8[:, KSEL:KSEL + 1]
            v.tensor_scalar(gtm, W, last, None, ALU.is_gt)
            v.tensor_scalar(key, W, thr, None, ALU.is_gt)
            link(v.memset(W2, 1.0))
            link(v.tensor_scalar(eqm, W, last, None, ALU.is_equal))
            v.reduce_sum(m8[:, 24:25], gtm, AX)
            link(v.tensor_tensor_scan(pre, W2, eqm, 0.0, ALU.mult, ALU.add))
            link(v.tensor_scalar(m8[:, 25:26], m8[:, 24:25], -1.0, float(KSEL), ALU.mult, ALU.add))
            link(v.scalar_tensor_tensor(eqm, pre, m8[:, 25:26], eqm, ALU.is_le, ALU.mult))
            TT(sel, gtm, eqm, ALU.add)
            v.wait_ge(s["tokload"], 16)
            link(TT(key, key, base, ALU.add))
            link(TT(key, key, sel, ALU.mult))
            top24(key, W2, W3)
            ki = tk[:, 13, 0:KSEL].bitcast(I32)
            kb = tk[:, 13, 32:32 + KSEL].bitcast(I32)
            bit, tok = tk[:, 14, 0:KSEL], tk[:, 14, 32:64]
            link(v.tensor_copy(ki, m8[:, 0:KSEL]))
            link(v.tensor_scalar(kb, ki, 1, None, ALU.bitwise_and))
            v.memset(tok, 0.0)
            v.memset(tk[:, 11, 0:SLOT], SKIP_ROW)
            v.memset(tk[:, 12, 0:SLOT], 0.0)
            link(v.tensor_copy(bit, kb))
            link(TT(tok[:, 0:KSEL], m8[:, 0:KSEL], bit, ALU.subtract))
            v.tensor_scalar(tk[:, 12, 0:KSEL], bit, -1.0, 1.0, ALU.mult, ALU.add)
            link(v.tensor_scalar(tok[:, 0:KSEL], tok[:, 0:KSEL], -0.5, 256.0, ALU.mult, ALU.add))
            v.tensor_scalar(tk[:, 11, 0:KSEL], tok[:, 0:KSEL], cst[0:S, 2:3], None, ALU.add)
            link(v.tensor_scalar(tk[:, 10, 0:SLOT], tok, cst[0:S, 2:3], None, ALU.add))
            v.sem_inc(s["idx"], 1)
            for b in range(SG):
                own = slice(SQ * b, SQ * b + SQ)
                TT(dg[:, own, :], row1(tok[:, 0:KSEL], SQ), col1(ident[0:S, own], KSEL), ALU.mult).then_inc(s["seldg"], 1)
            v.wait_ge(s["idxp"], 1)
            v.tensor_copy(idxg, psum[:, 1, 0:NQ])
            v.tensor_copy(idxs, psum[:, 1, NQ:2 * NQ])
            link(v.tensor_copy(notm, psum[:, 1, 2 * NQ:3 * NQ]))
            v.sem_inc(s["idxr"], 1)
            for g in range(SG):
                v.wait_ge(s["ind"], g + 1)
                for x in range(2):
                    ins = v.tensor_scalar(su[:, x, g * NC:(g + 1) * NC], psum[:, TOKEN_BANK[g], 0:NC], cst[:, x:x + 1], None,
                                          ALU.is_equal)
                ins.then_inc(s["oh"], 1)

            def begin(u):
                v.wait_ge(s["gemm"], use_of[u] + 1)
                return bank(u)


            def routed_statistics(g):
                q4 = slice(4 * g, 4 * g + 4)
                for q in range(4 * g, 4 * g + 4):
                    v.wait_ge(s_gath[q], 16)
                    ins = v.bn_stats(st2[:, q, :], h1s[:, q, :])
                link(ins)
                moments(sm[:, q4], sd[:, q4], sq_[:, q4], st2[:, q4, :]).then_inc(s["rvar"], 1)

            def routed_factors(g):
                q4 = slice(4 * g, 4 * g + 4)
                v.wait_ge(s["rstd"], g + 1)
                link(v.reciprocal(rr[:, q4], sd[:, q4]))
                v.scalar_tensor_tensor(nb[:, q4], sm[:, q4], -0.5, rr[:, q4], ALU.mult, ALU.mult).then_inc(s["rows"], 1)
                link(TT(ssq[:, q4], sq_[:, q4], rr[:, q4], ALU.mult))
                TT(ssq[:, q4], ssq[:, q4], rr[:, q4], ALU.mult).then_inc(s["ssq"], 1)
                v.wait_ge(s["rows"], g + 1)
                TT(sd[:, q4], nb[:, q4], notm[:, q4], ALU.mult)
                link(TT(sm[:, q4], rr[:, q4], notm[:, q4], ALU.mult))
                v.tensor_scalar(sm[:, q4], sm[:, q4], 1.0, None, ALU.add).then_inc(s["ownf"], 1)

            def routed(g):
                q4 = slice(4 * g, 4 * g + 4)
                v.wait_ge(s["rms1"], g + 1)
                v.reciprocal(r1[:, q4], rms1[:, q4]).then_inc(s["rms1r"], 1)
                for q in range(4 * g, 4 * g + 4):
                    v.wait_ge(s["g1"], q + 1)
                    link(v.tensor_tensor_reduce(junk_v, gs[:, q], rwb[:, :], 1.0, 0.0, ALU.mult, ALU.add, wsel[:, q:q + 1]))
                v.tensor_scalar(wsel[:, q4], wsel[:, q4], rbias, None, ALU.add)

            routed_statistics(0)
            routed_factors(0)
            routed(0)
            link(v.memset(qT.rearrange("p h t i -> p (h t i)"), 0.0))
            routed_statistics(1)
            routed_factors(1)
            routed_statistics(2)
            routed_statistics(3)

            def mask_rows():
                for g in range(SG):
                    for i in range(2):
                        o = begin(("u", g, i))
                        rows = P if i == 0 else TOK - P
                        v.tensor_copy(su[0:rows, 2 + i, g * NC:(g + 1) * NC], o[0:rows, 0:NC]).then_inc(s["evv"], 1)
                v.wait_ge(s["evv"], emptied[use_of[("mask", 0, 0)] - 4][1])
                v.memset(bank(("mask", 0, 0))[:, 0:NC], 0.0).then_inc(s["mbank"], 1)

            def mask():
                o = begin(("mask", 0, 0))
                v.tensor_copy(msk, o[:, 0:NC].rearrange("p (q k) -> p q k", q=NQ)).then_inc(s["evv"], 1)
                v.wait_ge(s["evv"], emptied[use_of[("mask", 0, 0)]][1])

            def project(g):
                c0 = slice(g * NC, (g + 1) * NC)
                if g >= 1:
                    v.wait_ge(s["sc"], g)
                for h in range(2):
                    for w in ("q", "k"):
                        o = begin((w, g, h))
                        if g == 0 and h == 0 and w == "q":
                            v.wait_ge(s["eva"], emptied[use_of[("cs", SG - 1, 1)]][1])
                        TT(tmp[:, 0], o[:, 0:NC], cs[:, 0, c0], ALU.mult)
                        v.stream_shuffle(tmp[:, 1], o[:, 0:NC], HALF_TURN).then_inc(s["evv"], 1)
                        v.wait_ge(s["evv"], emptied[use_of[(w, g, h)]][1])
                        link(TT(tmp[:, 1], tmp[:, 1], cs[:, 1, c0], ALU.mult))
                        t3 = [tmp[:, x].rearrange("p (t i) -> p t i", t=SQ) for x in range(2)]
                        if w == "q":
                            link(TT(qT[:, h, :, 0:KSEL], t3[0], t3[1], ALU.add))
                            v.sem_inc(s["qk"], 1)
                        else:
                            if g >= 1 and h == 1:
                                v.wait_ge(s["kx"], 2 * g)
                            link(TT(kT[:, h], t3[0], t3[1], ALU.add))
                            v.sem_inc(s["keys"], 1)

            def spread_keys(g):
                if g == 1:
                    rows_out(v)
                spread(v, lambda o, x, f: v.tensor_scalar(o, x, f, None, ALU.mult), g, 0).then_inc(s["kx"], 1)

            def softmax(g):
                v.wait_ge(s["sc"], g + 1)
                if g >= 1:
                    v.wait_ge(s["pv"], g)
                p4 = pr.rearrange("p q c i -> p (q c) i")[:, :, 0:KSEL]
                link(TT(pr[:, :, :, 0:KSEL], psum[:, 0:4, 0:2 * HP * KSEL].rearrange("p q (c k) -> p q c k", k=KSEL),
                        msk[:, 4 * g:4 * g + 4, :].rearrange("p q (o k) -> p q o k", o=1).to_broadcast([P, 4, 2 * HP, KSEL]),
                        ALU.add))
                link(v.reduce_max(mx, p4, AX))
                TT(p4, p4, col1(mx, KSEL), ALU.subtract).then_inc(s["pin"], 1)

            def weights(g):
                p4 = pr.rearrange("p q c i -> p (q c) i")[:, :, 0:KSEL]
                v.wait_ge(s["pexp"], g + 1)
                link(v.reduce_sum(rinv, p4, AX))
                link(v.reciprocal(rinv, rinv))
                link(TT(p4, p4, col1(rinv, KSEL), ALU.mult))
                for half in (slice(0, 2), slice(2, 4)):
                    v.transpose(prT[:, half].rearrange("p q c i -> p (q c i)"), pr[:, half].rearrange("p q c i -> p (q c i)")
                                ).then_inc(s["pt"], 1)

            def heads_out(g):
                v.wait_ge(s["pv"], g + 1)
                if g >= 1:
                    v.wait_ge(s["gemm"], use_of[("o", g - 1, 3)] + 1)
                o8 = oT.rearrange("p q h b i -> p (q h) b i")
                pp = psum[:, 0:4, 0:8 * 34].rearrange("p b (x e i) -> p b x e i", x=8, e=2)
                for b in range(4):
                    ins = v.tensor_scalar(o8[:, :, b, 0:KSEL], pp[:, b, :, 0, :], cst[:, 3:4], None, ALU.mult)
                link(ins)
                for b in range(4):
                    ins = v.scalar_tensor_tensor(o8[:, :, b, 0:KSEL], pp[:, b, :, 1, :], cst[:, 4:5], o8[:, :, b, 0:KSEL],
                                                 ALU.mult, ALU.add)
                ins.then_inc(s["ot"], 1)

            def merge(g):
                for i in range(4):
                    o = begin(("o", g, i))
                    if g >= 2:
                        v.wait_ge(s_scat[g - 2], 64)
                    q = 4 * g + i
                    TT(x1[:, g % 2, i], o[:, 0:D], gs[:, q], ALU.add).then_inc(s["evv"], 1)
                    v.wait_ge(s["evv"], emptied[use_of[("o", g, i)]][1])
                    if i == 0:
                        v.wait_ge(s["own"], g + 1)
                    v.tensor_tensor_reduce(gs[:, q], x1[:, g % 2, i], x1[:, g % 2, i], 1.0, 0.0, ALU.mult, ALU.add,
                                           ssq2[:, q:q + 1]).then_inc(s["ssq2"], 1)

            def second_rms(g):
                v.wait_ge(s["rms2"], g + 1)
                v.reciprocal(rr2[:, 4 * g:4 * g + 4], rms2[:, 4 * g:4 * g + 4]).then_inc(s["rms2r"], 1)

            def outer(g):
                if g == 0:
                    rows_out(v)
                    link(v.memset(yT.rearrange("p h t i -> p (h t i)"), 0.0))
                for h in range(2):
                    o = begin(("y", g, h))
                    if g >= 1:
                        v.wait_ge(s["gemm"], use_of[("yt", g - 1, 3)] + 1)
                    v.tensor_copy(yT[:, h, :, 0:KSEL], o[:, 0:NC].rearrange("p (t i) -> p t i", t=SQ)).then_inc(s["evv"], 1)

            def back(g):
                for i in range(4):
                    q = 4 * g + i
                    o = begin(("yt", g, i))
                    x = x1[:, g % 2, i]
                    TT(x, x, o[:, 0:D], ALU.add).then_inc(s["evv"], 1)
                    v.wait_ge(s["evv"], emptied[use_of[("yt", g, i)]][1])
                    v.scalar_tensor_tensor(x, x, wsel[:, q:q + 1], h1s[:, q], ALU.mult, ALU.add).then_inc(s["fin"], 1)

            project(0)
            link(v.memset(oT.rearrange("p q h b i -> p (q h b i)"), 0.0))
            routed_factors(2)
            routed_factors(3)
            mask_rows()
            spread_keys(0)
            routed(1)
            mask()
            for g in range(SG):
                softmax(g)
                if g == 0:
                    routed(2)
                    weights(g)
                if g + 1 < SG:
                    project(g + 1)
                if g >= 1:
                    weights(g)
                else:
                    routed(3)
                if g + 1 < SG:
                    spread_keys(g + 1)
                heads_out(g)
                if g >= 1:
                    outer(g - 1)
                merge(g)
                second_rms(g)
                if g >= 1:
                    back(g - 1)
            outer(SG - 1)
            back(SG - 1)

        @block.gpsimd
        def _(pool):
            steps = [0]

            def link(ins):
                steps[0] += 1
                ins.then_inc(s["poolw"], 1)
                pool.wait_ge(s["poolw"], steps[0])

            TT = pool.tensor_tensor
            pool.wait_ge(s["s4in"], 32)
            pool.wait_ge(s["act_s4"], 1)
            dt = s4v[:, 0, :]
            Br, Bi, Pr, Pi, Cr, Ci = (s4in[:, 3 + i, :] for i in range(6))
            ta, tb = s4v[:, 12, :], s4v[:, 13, :]
            for ab, (xr, xi, yr, yi, sg) in enumerate([(Br, Bi, Cr, Ci, 1), (Br, Bi, Pr, Pi, -1),
                                                       (Pr, Pi, Cr, Ci, 1), (Pr, Pi, Pr, Pi, -1)]):
                re, im = s4v[:, 4 + ab, :], s4v[:, 8 + ab, :]
                TT(ta, xr, yr, ALU.mult)
                link(TT(tb, xi, yi, ALU.mult))
                link(TT(re, ta, tb, ALU.subtract if sg > 0 else ALU.add))
                TT(ta, xi, yr, ALU.mult)
                link(TT(tb, xr, yi, ALU.mult))
                link(TT(im, ta, tb, ALU.add if sg > 0 else ALU.subtract))
            link(TT(s4v[:, 4:12, :], s4v[:, 4:12, :], row1(dt, 8), ALU.mult))
            eb = row1(c_e, HF)
            for i in range(4):
                re, im = col1(s4v[:, 4 + i, :], HG), col1(s4v[:, 8 + i, :], HG)
                TT(rhsA[:, :, i, :], re, eb, ALU.mult)
                TT(rhsA[:, :, 4 + i, :], im, eb, ALU.mult)
                ins = TT(rhsB[:, :, i, :], im, eb, ALU.mult)
            link(ins)
            link(pool.tensor_scalar(s4v[:, 4:8, :], s4v[:, 4:8, :], -1.0, None, ALU.mult))
            for i in range(4):
                ins = TT(rhsB[:, :, 4 + i, :], col1(s4v[:, 4 + i, :], HG), eb, ALU.mult)
            ins.then_inc(s["rhs"], 1)
            pool.wait_ge(s["x"], 1)
            for n, c in enumerate(ORDER):
                pool.wait_ge(s["nrm"], n + 1)
                if n >= 2:
                    pool.wait_ge(s["lo"], n - 1)
                for j in range(CH):
                    q = c * CH + j
                    ins = pool.tensor_scalar(t32(n)[:, j, :], h0[:, q, :], vec[:, V_R, q:q + 1], vec[:, V_B, q:q + 1],
                                             ALU.mult, ALU.add)
                ins.then_inc(s["t32"], 1)
                if ORDER[n] == 0:
                    for g in range(2):
                        z = toep[64 * g:64 * g + 64, :, 64 - 64 * g:128 - 64 * g].rearrange("p r t l c -> p r (t l c)")
                        if g == 0:
                            pool.wait_ge(s["t32"], n + 1)
                        else:
                            pool.wait_ge(s["tz"], 1)
                        pool.memset(z, 0.0).then_inc(s["tz"], 1)
                    pool.wait_ge(s["tz"], 2)
            for n in range(NGRP):
                if adder[n] == "addp":
                    pool.wait_ge(s["sil"], n + 1)
                    add_group(pool, n).then_inc(s["addp"], 1)
            added(pool, NGRP)
            pool.wait_ge(s["conv"], NGRP)
            for x in range(RW_ACT):
                p = slice(x * RW_TILE, (x + 1) * RW_TILE)
                pool.tensor_tensor(rw_products[:, p, :], h0[:, p, :], row1(rwb[:, :], RW_TILE), ALU.mult).then_inc(s["rwprod"], 1)
            pool.wait_ge(s["tabs"], 1)
            pool.wait_ge(s["rwdot"], 1)
            for k in range(2):
                for f in range(2):
                    ins = pool.tensor_copy(tab[:, k, :, f, :].rearrange("p b (h d) -> p b h d", d=HD),
                                           rp[:, 2 + f, k * 64:k * 64 + 64].rearrange("p (b o d) -> p b o d", b=NBB, o=1)
                                           .to_broadcast([P, NBB, 8, HD]))
            ins.then_inc(s["tab"], 1)
            pool.wait_ge(s["wload"], 64)
            for c in range(2):
                pool.tensor_scalar(wsm[:, 0, c], wsm[:, 0, c], lnw[:, c:c + 1], HD ** -0.5, ALU.mult, ALU.mult)
                pool.tensor_scalar(wsm[:, 1, c], wsm[:, 1, c], lnw[:, c:c + 1], None, ALU.mult)
                ins = pool.tensor_scalar(wsm[:, 2, c], wsm[:, 2, c], lnw[:, c:c + 1], None, ALU.mult)
            link(ins)
            pool.sem_inc(s["wready"], 1)
            pool.wait_ge(s["h1out"], 128)
            pool.wait_ge(s["idxr"], 1)
            for q in range(NQ):
                pool.indirect_dma_start(h1s[:, q, :], None, h1_rows, bass.IndirectOffsetOnAxis(ap=idxg[:, q:q + 1], axis=0),
                                        bounds_check=S * TOK - 1, oob_is_err=False).then_inc(s_gath[q], 16)
            for c in range(NCH):
                for j in range(CH):
                    q = c * CH + j
                    ins = pool.tensor_scalar(h0[:, q, :], h0[:, q, :], vec[:, V_A, q:q + 1], vec[:, V_B, q:q + 1],
                                             ALU.mult, ALU.add)
                ins.then_inc(s["outc"], 1)
            pool.wait_ge(s["w1load"], 16)
            for c in range(2):
                ins = pool.tensor_scalar(w1[:, c], w1[:, c], lnw[:, 2 + c:3 + c], None, ALU.mult)
            link(ins)
            pool.sem_inc(s["wready"], 1)

            def own_part(g):
                pool.wait_ge(s["ownf"], g + 1)
                for q in range(4 * g, 4 * g + 4):
                    pool.wait_ge(s["g1"], q + 1)
                    ins = pool.tensor_scalar(h1s[:, q], h1s[:, q], sm[:, q:q + 1], sd[:, q:q + 1], ALU.mult, ALU.add)
                ins.then_inc(s["own"], 1)

            for g in range(SG):
                own_part(g)
            rows_out(pool)
            for q in range(NQ):
                pool.wait_ge(s["fin"], q + 1)
                pool.indirect_dma_start(out.rearrange("s t d -> (s t) d"), bass.IndirectOffsetOnAxis(ap=idxs[:, q:q + 1], axis=0),
                                        x1[:, q // 4 % 2, q % 4, :], None, bounds_check=S * TOK - 1, oob_is_err=False
                                        ).then_inc(s_scat[q // 4], 16)
            for g in range(SG):
                pool.wait_ge(s_scat[g], 64)


def _constants():
    m = np.arange(FR)
    half = np.pi * m / S
    out = {}
    own = np.zeros((P, HG), np.float32)
    own[np.arange(P), np.arange(P) % HG] = 1
    wave = np.concatenate([np.cos(half), 2 * np.sin(half)]).astype(np.float32)
    wave[FR - 1] = 0.0
    out["s4c"] = np.concatenate([np.broadcast_to(wave, (P, 2 * FR)), own], axis=1)
    phase = 2 * np.pi * m[:, None] * (np.arange(S) + 0.5) / S
    wgt = (np.where((m == 0) | (m == FR - 1), 1, 2) / S)[:, None]
    out["dft"] = np.concatenate([wgt * np.cos(phase), -wgt * np.sin(phase), wave[:FR, None]], axis=1)
    out["ident"] = np.eye(P)
    cst = np.zeros((P, 5))
    cst[:, 0] = np.arange(P)
    cst[:, 1] = np.arange(P) + P
    cst[:S, 2] = TOK * np.arange(S)
    cst[:, 3] = np.arange(P) % 32 < HD
    cst[:, 4] = np.arange(P) % 32 >= HD
    out["cst"] = cst
    out["own_head"] = np.arange(P)[:, None] // HD == np.arange(HP)
    pick = np.zeros((S, 2 * S), np.float32)
    pick[S - 1 - np.arange(S), np.arange(S)] = 1
    out["base"] = np.broadcast_to(2.0 * (256 - np.arange(TOK)), (S, TOK))
    inv = 1.0 / np.float32(10000.0) ** (np.arange(0, HD, 2, dtype=np.float32) / np.float32(HD))
    out["invf"] = np.broadcast_to(np.concatenate([inv, inv]), (P, HD))
    return {"pick": pick.astype(np.float16)} | {k: np.ascontiguousarray(x, dtype=np.float32) for k, x in out.items()}


def _lay_out(i):
    i = {k: np.asarray(v) for k, v in i.items()}
    h = {}

    def states(x):
        return x.reshape(HF, HG, 16).transpose(2, 1, 0).reshape(P, HF)

    h["s4in"] = np.stack([states(np.broadcast_to(i["L0_attn_log_dt"], (D, 16))), states(i["L0_attn_inv_w_real"]),
                          states(i["L0_attn_w_imaginary"])]
                         + [states(i["L0_attn_" + n].reshape(D, 16, 2)[..., x]) for n in "BPC" for x in range(2)], axis=1)
    x = i["x"].reshape(S, 3, 4, 16, 4, 16).transpose(1, 3, 5, 2, 4, 0)
    h["img"] = x.reshape(KC, P, 2, CH, S).transpose(1, 0, 3, 2, 4).reshape(P, KC, CH, P)
    h["wT"] = i["L0_tok_W"].T.reshape(KC, P, D).transpose(1, 0, 2)
    lag0 = np.zeros((1, S), np.float32)
    lag0[0, 0] = 1
    h["drow"] = np.concatenate([i["L0_attn_D"].reshape(1, D), lag0, np.ones((1, P), np.float32)], axis=1)
    h["lnw"] = np.concatenate([i["L0_ffn_ln1"].reshape(2, P).T, i["L0_ffn_ln2"].reshape(2, P).T], axis=1)
    pos = np.zeros((2 * P, NBB), i["L0_ffn_position_ids"].dtype)
    pos[:TOK] = i["L0_ffn_position_ids"][:, :TOK].T
    h["posT"] = pos.reshape(2, P, NBB).transpose(1, 0, 2).reshape(P, 2 * NBB)
    h["mask"] = i["L0_ffn_attention_mask"][:, 0, :TOK, :TOK]
    for name, src in (("txt", "txt"), ("b", "L0_tok_b"), ("pos_emb", "L0_tok_pos_emb"), ("rw", "L0_ffn_router_w"),
                      ("rb", "L0_ffn_router_b"), ("wq", "L0_ffn_wq"), ("wk", "L0_ffn_wk"), ("wv", "L0_ffn_wv"),
                      ("wo", "L0_ffn_wo"), ("w1", "L0_ffn_w1"), ("w2", "L0_ffn_w2")):
        h[name] = i[src]
    return {k: np.ascontiguousarray(x) for k, x in h.items()}


def program(nc, arrays):
    args = {n: nc.dram_tensor("in_" + n, x.shape, mybir.dt.from_np(x.dtype), kind="ExternalInput").ap()
            for n, x in arrays.items()}
    out = nc.dram_tensor("out_rows", (S, TOK, D), F32, kind="ExternalOutput").ap()
    build(nc, args, out)


def kernel(**inputs):
    import concourse.bacc as bacc
    from concourse.bass_utils import run_bass_kernel_spmd as run

    arrays = {**_lay_out(inputs), **_constants()}
    nc = bacc.Bacc("TRN2", target_bir_lowering=False, num_devices=1)
    program(nc, arrays)
    r = run(nc, [{"in_" + n: x for n, x in arrays.items()}], core_ids=[0])
    return r.results[0]["out_rows"]
```
